# Optimizing a Trainium2 kernel written in Bass

```python
import numpy as np
import jax
import jax.numpy as jnp

def _softmax(x, axis=-1):
    return jax.nn.softmax(x, axis=axis)

def _gelu(x):
    return jax.nn.gelu(x, approximate=True)

def _silu(x):
    return jax.nn.silu(x)

def _sigmoid(x):
    return jax.nn.sigmoid(x)

def _layernorm(x, axis=-1, eps=1e-05):
    m = jnp.mean(x, axis=axis, keepdims=True)
    v = jnp.var(x, axis=axis, keepdims=True)
    return (x - m) / jnp.sqrt(v + eps)

def _scatter_add(tgt, idx, src, axis=0):
    return tgt.at[idx].add(src)

def _segment_sum(src, seg, n):
    return jax.ops.segment_sum(src, seg, n)
kernel_name = 'mk_gnn_preln_d4_gnn_r8_c51b7b'

def setup_inputs(seed: int=0):
    np.random.seed(seed)
    _w = jnp.asarray

    def _rec_inputs():
        import jax
        import jax.numpy as jnp
        _gk = jax.random.key(seed)
        x = -0.0005121 + 1.001 * jax.random.normal(jax.random.fold_in(_gk, 1), (12500, 64), jnp.float32)
        src = jax.random.randint(jax.random.fold_in(_gk, 2), (400000,), 0, 12500, jnp.int32)
        dst = jnp.minimum((12500 * jax.random.uniform(jax.random.fold_in(_gk, 3), (400000,)) ** 2.0).astype(jnp.int32), 99999)
        _o = jnp.argsort(dst, stable=True)
        src = src[_o]
        dst = dst[_o]
        edge_attr_16 = 0.000254156 + 0.999948 * jax.random.normal(jax.random.fold_in(_gk, 11), (400000, 16), jnp.float32)
        edge_attr_64 = -2.25437e-05 + 0.999858 * jax.random.normal(jax.random.fold_in(_gk, 12), (400000, 64), jnp.float32)
        return (x, src, dst, edge_attr_16, edge_attr_64)
    x, src, dst, edge_attr_16, edge_attr_64 = _rec_inputs()

    def _L0_gnn_setup():
        import jax, jax.numpy as jnp
        import numpy as np
        N, E = (6250, 100000)
        NODE_DIM, EDGE_DIM, HEADS = (64, 16, 4)
        C = NODE_DIM // HEADS
        NEG_SLOPE = 0.2
        BN_EPS = 1e-05
        key = jax.random.key(seed)
        ks = jax.random.split(key, 12)
        glorot = lambda k, shape: jax.random.normal(k, shape, jnp.float32) * np.sqrt(2.0 / (shape[0] + shape[-1]))
        return {'x': jax.random.normal(ks[0], (N, NODE_DIM), jnp.float32), 'edge_index': jax.random.randint(ks[1], (2, E), 0, N, jnp.int32), 'edge_attr': jax.random.normal(ks[2], (E, EDGE_DIM), jnp.float32), 'W_l': glorot(ks[3], (NODE_DIM, HEADS * C)), 'b_l': jnp.zeros((HEADS * C,), jnp.float32), 'W_r': glorot(ks[4], (NODE_DIM, HEADS * C)), 'b_r': jnp.zeros((HEADS * C,), jnp.float32), 'W_e': glorot(ks[5], (EDGE_DIM, HEADS * C)), 'att': glorot(ks[6], (HEADS, C)), 'bias': jnp.zeros((HEADS * C,), jnp.float32), 'gamma': jnp.ones((NODE_DIM,), jnp.float32), 'beta': jnp.zeros((NODE_DIM,), jnp.float32)}
    _L0_gnn_all = _L0_gnn_setup()
    _L0_gnn_in = {k: v for k, v in _L0_gnn_all.items() if k in ('W_l', 'b_l', 'W_r', 'b_r', 'W_e', 'att', 'bias', 'gamma', 'beta')}
    del _L0_gnn_all

    def _L1_gnn_setup():
        import jax, jax.numpy as jnp
        import numpy as np
        N_NODES = 12500
        N_EDGES = 200000
        IN_CH = 64
        OUT_CH = 64
        key = jax.random.key(seed)
        ks = jax.random.split(key, 6)
        x = jax.random.normal(ks[0], (N_NODES, IN_CH), dtype=jnp.float32)
        edge_index = jax.random.randint(ks[1], (2, N_EDGES), 0, N_NODES, dtype=jnp.int64)
        W1 = jax.random.normal(ks[2], (2 * IN_CH, OUT_CH), dtype=jnp.float32) * (1.0 / np.sqrt(2 * IN_CH))
        b1 = jnp.zeros((OUT_CH,), dtype=jnp.float32)
        W2 = jax.random.normal(ks[3], (OUT_CH, OUT_CH), dtype=jnp.float32) * (1.0 / np.sqrt(OUT_CH))
        b2 = jnp.zeros((OUT_CH,), dtype=jnp.float32)
        return {'x': x, 'edge_index': edge_index, 'W1': W1, 'b1': b1, 'W2': W2, 'b2': b2}
    _L1_gnn_all = _L1_gnn_setup()
    _L1_gnn_in = {k: v for k, v in _L1_gnn_all.items() if k in ('W1', 'b1', 'W2', 'b2')}
    del _L1_gnn_all

    def _L2_gnn_setup():
        import jax, jax.numpy as jnp
        import numpy as np
        N, E, D, ED = (6250, 100000, 64, 16)
        H1 = 2 * D + ED

        def _forward(x, edge_weights, W_att1, b_att1, W_att2, b_att2, W_lin, b_lin, W_ih, b_ih, W_hh, b_hh, edge_idx):
            num_nodes = x.shape[0]
            src = edge_idx[0]
            dst = edge_idx[1]
            lin_x = x @ W_lin.T + b_lin
            feat = jnp.concatenate([x[src], edge_weights, x[dst]], axis=1)
            h = jax.nn.relu(feat @ W_att1.T + b_att1)
            scores = (h @ W_att2.T + b_att2)[:, 0]
            m = jax.ops.segment_max(scores, src, num_segments=num_nodes)
            e = jnp.exp(scores - m[src])
            denom = jax.ops.segment_sum(e, src, num_segments=num_nodes)
            alpha = e / denom[src]
            msg = jax.ops.segment_sum(alpha[:, None] * lin_x[dst], src, num_segments=num_nodes)
            gi = x @ W_ih.T + b_ih
            gh = msg @ W_hh.T + b_hh
            i_r, i_z, i_n = jnp.split(gi, 3, axis=1)
            h_r, h_z, h_n = jnp.split(gh, 3, axis=1)
            r = jax.nn.sigmoid(i_r + h_r)
            z = jax.nn.sigmoid(i_z + h_z)
            n = jnp.tanh(i_n + r * h_n)
            new_h = (1.0 - z) * n + z * msg
            deg = jax.ops.segment_sum(jnp.ones_like(scores), src, num_segments=num_nodes)
            return jnp.where(deg[:, None] > 0, new_h, x)
        key = jax.random.key(seed)
        ks = jax.random.split(key, 16)
        s = 0.05
        inp = {'x': jax.random.normal(ks[0], (N, D), jnp.float32), 'edge_idx': jax.random.randint(ks[1], (2, E), 0, N, jnp.int64), 'edge_weights': jax.random.normal(ks[2], (E, ED), jnp.float32), 'W_att1': jax.random.normal(ks[3], (H1, H1), jnp.float32) * s, 'b_att1': jnp.zeros((H1,), jnp.float32), 'W_att2': jax.random.normal(ks[4], (1, H1), jnp.float32) * s, 'b_att2': jnp.zeros((1,), jnp.float32), 'W_lin': jax.random.normal(ks[5], (D, D), jnp.float32) * s, 'b_lin': jnp.zeros((D,), jnp.float32), 'W_ih': jax.random.normal(ks[6], (3 * D, D), jnp.float32) * s, 'b_ih': jnp.zeros((3 * D,), jnp.float32), 'W_hh': jax.random.normal(ks[7], (3 * D, D), jnp.float32) * s, 'b_hh': jnp.zeros((3 * D,), jnp.float32)}
        return inp
    _L2_gnn_all = _L2_gnn_setup()
    _L2_gnn_in = {k: v for k, v in _L2_gnn_all.items() if k in ('W_att1', 'b_att1', 'W_att2', 'b_att2', 'W_lin', 'b_lin', 'W_ih', 'b_ih', 'W_hh', 'b_hh')}
    del _L2_gnn_all

    def _L3_gnn_setup():
        import jax, jax.numpy as jnp
        import numpy as np
        LN_EPS = 1e-05
        key = jax.random.key(seed)
        ks = jax.random.split(key, 8)
        N, E, D = (12500, 125000, 64)
        node_feats = jax.random.normal(ks[0], (N, D), dtype=jnp.float32)
        edge_feats = jax.random.normal(ks[1], (E, D), dtype=jnp.float32)
        edge_index = jax.random.randint(ks[2], (2, E), 0, N, dtype=jnp.int64)
        W1 = jax.random.normal(ks[3], (D, 2 * D), dtype=jnp.float32) / np.sqrt(D)
        b1 = jnp.zeros((2 * D,), dtype=jnp.float32)
        ln_g = jnp.ones((2 * D,), dtype=jnp.float32)
        ln_b = jnp.zeros((2 * D,), dtype=jnp.float32)
        W2 = jax.random.normal(ks[4], (2 * D, D), dtype=jnp.float32) / np.sqrt(2 * D)
        b2 = jnp.zeros((D,), dtype=jnp.float32)
        eps = jnp.zeros((1,), dtype=jnp.float32)
        return {'node_feats': node_feats, 'edge_feats': edge_feats, 'W1': W1, 'b1': b1, 'ln_g': ln_g, 'ln_b': ln_b, 'W2': W2, 'b2': b2, 'eps': eps, 'edge_index': edge_index, 'num_nodes': 12500}
    _L3_gnn_all = _L3_gnn_setup()
    _L3_gnn_in = {k: v for k, v in _L3_gnn_all.items() if k in ('W1', 'b1', 'ln_g', 'ln_b', 'W2', 'b2', 'eps')}
    del _L3_gnn_all
    return {'x': x, 'src': src, 'dst': dst, 'edge_attr_16': edge_attr_16, 'edge_attr_64': edge_attr_64, 'L0_gnn_W_l': _L0_gnn_in['W_l'], 'L0_gnn_b_l': _L0_gnn_in['b_l'], 'L0_gnn_W_r': _L0_gnn_in['W_r'], 'L0_gnn_b_r': _L0_gnn_in['b_r'], 'L0_gnn_W_e': _L0_gnn_in['W_e'], 'L0_gnn_att': _L0_gnn_in['att'], 'L0_gnn_bias': _L0_gnn_in['bias'], 'L0_gnn_gamma': _L0_gnn_in['gamma'], 'L0_gnn_beta': _L0_gnn_in['beta'], 'L1_gnn_W1': _L1_gnn_in['W1'], 'L1_gnn_b1': _L1_gnn_in['b1'], 'L1_gnn_W2': _L1_gnn_in['W2'], 'L1_gnn_b2': _L1_gnn_in['b2'], 'L2_gnn_W_att1': _L2_gnn_in['W_att1'], 'L2_gnn_b_att1': _L2_gnn_in['b_att1'], 'L2_gnn_W_att2': _L2_gnn_in['W_att2'], 'L2_gnn_b_att2': _L2_gnn_in['b_att2'], 'L2_gnn_W_lin': _L2_gnn_in['W_lin'], 'L2_gnn_b_lin': _L2_gnn_in['b_lin'], 'L2_gnn_W_ih': _L2_gnn_in['W_ih'], 'L2_gnn_b_ih': _L2_gnn_in['b_ih'], 'L2_gnn_W_hh': _L2_gnn_in['W_hh'], 'L2_gnn_b_hh': _L2_gnn_in['b_hh'], 'L3_gnn_W1': _L3_gnn_in['W1'], 'L3_gnn_b1': _L3_gnn_in['b1'], 'L3_gnn_ln_g': _L3_gnn_in['ln_g'], 'L3_gnn_ln_b': _L3_gnn_in['ln_b'], 'L3_gnn_W2': _L3_gnn_in['W2'], 'L3_gnn_b2': _L3_gnn_in['b2'], 'L3_gnn_eps': _L3_gnn_in['eps']}

def reference(x, src, dst, edge_attr_16, edge_attr_64, L0_gnn_W_l, L0_gnn_b_l, L0_gnn_W_r, L0_gnn_b_r, L0_gnn_W_e, L0_gnn_att, L0_gnn_bias, L0_gnn_gamma, L0_gnn_beta, L1_gnn_W1, L1_gnn_b1, L1_gnn_W2, L1_gnn_b2, L2_gnn_W_att1, L2_gnn_b_att1, L2_gnn_W_att2, L2_gnn_b_att2, L2_gnn_W_lin, L2_gnn_b_lin, L2_gnn_W_ih, L2_gnn_b_ih, L2_gnn_W_hh, L2_gnn_b_hh, L3_gnn_W1, L3_gnn_b1, L3_gnn_ln_g, L3_gnn_ln_b, L3_gnn_W2, L3_gnn_b2, L3_gnn_eps):
    import jax
    import jax.numpy as jnp

    def _L0_gnn_ref(x, edge_index, edge_attr, W_l, b_l, W_r, b_r, W_e, att, bias, gamma, beta):
        import jax, jax.numpy as jnp
        import numpy as np
        N, E = (6250, 100000)
        NODE_DIM, EDGE_DIM, HEADS = (64, 16, 4)
        C = NODE_DIM // HEADS
        NEG_SLOPE = 0.2
        BN_EPS = 1e-05
        src, dst = (edge_index[0], edge_index[1])
        n = x.shape[0]
        xl = (x @ W_l + b_l).reshape(n, HEADS, C)
        xr = (x @ W_r + b_r).reshape(n, HEADS, C)
        e = (edge_attr @ W_e).reshape(-1, HEADS, C)
        g = jax.nn.leaky_relu(xl[src] + xr[dst] + e, NEG_SLOPE)
        logits = jnp.einsum('ehc,hc->eh', g, att)
        amax = jax.ops.segment_max(logits, dst, num_segments=n)
        ex = jnp.exp(logits - amax[dst])
        denom = jax.ops.segment_sum(ex, dst, num_segments=n)
        alpha = ex / (denom[dst] + 1e-16)
        msg = xl[src] * alpha[..., None]
        out = jax.ops.segment_sum(msg, dst, num_segments=n).reshape(n, HEADS * C) + bias
        mean = out.mean(axis=0)
        var = out.var(axis=0)
        out = (out - mean) * jax.lax.rsqrt(var + BN_EPS) * gamma + beta
        return jax.nn.gelu(out + x, approximate=False)

    def _L1_gnn_ref(x, edge_index, W1, b1, W2, b2):
        import jax, jax.numpy as jnp
        import numpy as np
        N_NODES = 12500
        N_EDGES = 200000
        IN_CH = 64
        OUT_CH = 64
        src = edge_index[0]
        dst = edge_index[1]
        x_i = x[dst]
        x_j = x[src]
        edge_features = jnp.concatenate([x_i, x_j - x_i], axis=-1)
        h = jax.nn.relu(edge_features @ W1 + b1)
        edge_messages = h @ W2 + b2
        out = jax.ops.segment_max(edge_messages, dst, num_segments=x.shape[0])
        return jnp.where(jnp.isfinite(out), out, jnp.zeros_like(out))

    def _L2_gnn_ref(x, edge_idx, edge_weights, W_att1, b_att1, W_att2, b_att2, W_lin, b_lin, W_ih, b_ih, W_hh, b_hh):
        import jax, jax.numpy as jnp
        import numpy as np
        N, E, D, ED = (6250, 100000, 64, 16)
        H1 = 2 * D + ED

        def _forward(x, edge_weights, W_att1, b_att1, W_att2, b_att2, W_lin, b_lin, W_ih, b_ih, W_hh, b_hh, edge_idx):
            num_nodes = x.shape[0]
            src = edge_idx[0]
            dst = edge_idx[1]
            lin_x = x @ W_lin.T + b_lin
            feat = jnp.concatenate([x[src], edge_weights, x[dst]], axis=1)
            h = jax.nn.relu(feat @ W_att1.T + b_att1)
            scores = (h @ W_att2.T + b_att2)[:, 0]
            m = jax.ops.segment_max(scores, src, num_segments=num_nodes)
            e = jnp.exp(scores - m[src])
            denom = jax.ops.segment_sum(e, src, num_segments=num_nodes)
            alpha = e / denom[src]
            msg = jax.ops.segment_sum(alpha[:, None] * lin_x[dst], src, num_segments=num_nodes)
            gi = x @ W_ih.T + b_ih
            gh = msg @ W_hh.T + b_hh
            i_r, i_z, i_n = jnp.split(gi, 3, axis=1)
            h_r, h_z, h_n = jnp.split(gh, 3, axis=1)
            r = jax.nn.sigmoid(i_r + h_r)
            z = jax.nn.sigmoid(i_z + h_z)
            n = jnp.tanh(i_n + r * h_n)
            new_h = (1.0 - z) * n + z * msg
            deg = jax.ops.segment_sum(jnp.ones_like(scores), src, num_segments=num_nodes)
            return jnp.where(deg[:, None] > 0, new_h, x)
        return _forward(x, edge_weights, W_att1, b_att1, W_att2, b_att2, W_lin, b_lin, W_ih, b_ih, W_hh, b_hh, edge_idx)

    def _L3_gnn_ref(node_feats, edge_feats, W1, b1, ln_g, ln_b, W2, b2, eps, edge_index, num_nodes):
        import jax, jax.numpy as jnp
        import numpy as np
        LN_EPS = 1e-05
        message = jax.nn.relu(node_feats[edge_index[1]] + edge_feats)
        message_reduce = jax.ops.segment_sum(message, edge_index[0], num_segments=num_nodes)
        h = (1.0 + eps) * node_feats + message_reduce
        x = h @ W1 + b1
        mu = jnp.mean(x, axis=-1, keepdims=True)
        var = jnp.mean(jnp.square(x - mu), axis=-1, keepdims=True)
        x = (x - mu) * jax.lax.rsqrt(var + LN_EPS) * ln_g + ln_b
        x = jax.nn.relu(x)
        return x @ W2 + b2
    edge_index = jnp.stack([src, dst])
    h = jnp.maximum(_layernorm(x, axis=-1), 0.0)
    x = x + _L0_gnn_ref(h, edge_index, edge_attr_16, L0_gnn_W_l, L0_gnn_b_l, L0_gnn_W_r, L0_gnn_b_r, L0_gnn_W_e, L0_gnn_att, L0_gnn_bias, L0_gnn_gamma, L0_gnn_beta)
    h = jnp.maximum(_layernorm(x, axis=-1), 0.0)
    x = x + _L1_gnn_ref(h, edge_index, L1_gnn_W1, L1_gnn_b1, L1_gnn_W2, L1_gnn_b2)
    h = jnp.maximum(_layernorm(x, axis=-1), 0.0)
    x = x + _L2_gnn_ref(h, edge_index, edge_attr_16, L2_gnn_W_att1, L2_gnn_b_att1, L2_gnn_W_att2, L2_gnn_b_att2, L2_gnn_W_lin, L2_gnn_b_lin, L2_gnn_W_ih, L2_gnn_b_ih, L2_gnn_W_hh, L2_gnn_b_hh)
    h = jnp.maximum(_layernorm(x, axis=-1), 0.0)
    x = x + _L3_gnn_ref(h, edge_attr_64, L3_gnn_W1, L3_gnn_b1, L3_gnn_ln_g, L3_gnn_ln_b, L3_gnn_W2, L3_gnn_b2, L3_gnn_eps, edge_index, 12500)
    return x

_drawn_inputs = setup_inputs


def setup_inputs(seed=0):
    import zlib

    import numpy as np

    out = dict(_drawn_inputs(seed))
    spreads = {'L0_gnn_b_l': (0.0, 0.546),
     'L0_gnn_b_r': (0.0, 0.533),
     'L0_gnn_bias': (0.0, 2.0),
     'L0_gnn_gamma': (1.0, 0.2),
     'L0_gnn_beta': (0.0, 0.1),
     'L1_gnn_b1': (0.0, 0.284),
     'L1_gnn_b2': (0.0, 0.1),
     'L2_gnn_b_att1': (0.0, 2.0),
     'L2_gnn_b_lin': (0.0, 0.394),
     'L2_gnn_b_ih': (0.0, 0.345),
     'L2_gnn_b_hh': (0.0, 0.765),
     'L3_gnn_b1': (0.0, 2.0),
     'L3_gnn_ln_g': (1.0, 0.2),
     'L3_gnn_ln_b': (0.0, 0.1),
     'L3_gnn_b2': (0.0, 0.1)}
    factors = {'L2_gnn_W_att1': 8.0, 'L2_gnn_W_att2': 8.0, 'L2_gnn_W_hh': 5.486}
    for name, (base, spread) in spreads.items():
        noise = np.random.default_rng([zlib.crc32(name.encode()), seed]).standard_normal(out[name].shape)
        drawn = base * np.exp(spread * noise) if base else spread * noise
        out[name] = jnp.asarray(drawn.astype(out[name].dtype))
    for name, factor in factors.items():
        out[name] = (out[name] * factor).astype(out[name].dtype)
    return out
```

```python
from contextlib import ExitStack, contextmanager

import numpy as np
import concourse.bass as bass
from concourse import mybir

F32 = mybir.dt.float32
BF16 = mybir.dt.bfloat16
I32 = mybir.dt.int32
ALU = mybir.AluOpType
ACT = mybir.ActivationFunctionType
AX = mybir.AxisListType

STOP = 0
P = 128
D = 64
DE = 16
T = 4
GE = T * P
SLOTS = 4
ATT = 2 * D + DE
REC = 82
EA16, EA64 = 2, 2 + DE
BIG = 1.0e30
PAD = 2 * GE
FAR = 1 << 20
SORT_T = 5
HEADS = 4


def at_least(eng, sem, value):
    if not isinstance(value, int) or value > 0:
        eng.wait_ge(sem, value)


def steps(eng, n, body, unroll=SLOTS):
    assert n % unroll == 0 and n > unroll
    for k in range(unroll):
        body(k, k, 0)
    with eng.Fori(1, n // unroll) as r:
        for k in range(unroll):
            body(r * unroll + k, k, r)


def settle(eng):
    eng.nop(nofuse=True)


def bcast(ap, axis, n):
    a = ap.unsqueeze(axis)
    shape = list(a.shape)
    shape[axis] = n
    return a.broadcast_to(shape)


ROWS = {}
for _name, _n in (("att", D), ("bias", D), ("gamma", D), ("beta", D), ("b2_l1", D), ("w_att2", ATT), ("b_att2", 1),
                  ("ln_g", 2 * D), ("ln_b", 2 * D), ("b2_l3", D), ("eps", 1)):
    ROWS[_name] = slice(ROWS["_end"] if ROWS else 0, (ROWS["_end"] if ROWS else 0) + _n)
    ROWS["_end"] = ROWS[_name].stop


def program(nc, x, src, dst, ea16, ea64, rowvec, wtab0, w_e, wtab1, w2, wtab2, watt_e, wgru, bgru, w1, w3, out):
    N, E = x.shape[0], src.shape[0]
    NBLK = -(-N // P)
    NB = NBLK + NBLK % 2
    assert E % (P * SORT_T) == 0 and NB < P and D == x.shape[1]
    NG = (E + NBLK * (GE - 1)) // GE
    NG = -(-NG // SLOTS) * SLOTS
    EPP = E // P
    last_rows = N - P * (NBLK - 1)

    with ExitStack() as top:
        def dram(name, shape, dt=F32):
            return nc.dram_tensor(name, shape, dt).ap()

        def sb_in(ctx, name, shape, dt=F32):
            return ctx.enter_context(nc.sbuf_tensor(name, shape, dt))

        def ps_in(ctx, name, shape, dt=F32):
            return ctx.enter_context(nc.psum_tensor(name, shape, dt))

        held = []

        def sem_in(ctx, name):
            held.append(nc.alloc_semaphore(name))
            return held[-1]

        @contextmanager
        def phase():
            with ExitStack() as ctx:
                yield ctx
            nc.clear_and_free_semaphores(held)
            held.clear()
            nc.all_engine_barrier()

        def sb(name, shape, dt=F32):
            return sb_in(top, name, shape, dt)

        keyp = dram("keyp", (1 + E + PAD,), I32)
        srcp = dram("srcp", (E + PAD,), I32)
        eap = dram("eap", (E + PAD, DE))
        rec = dram("rec", (NG * GE, REC), I32)
        tab0 = dram("tab0", (NB * P, D))
        tab1 = dram("tab1", (NB * P, D))
        tab2 = dram("tab2", (NB * P, ATT + D))
        tab3 = dram("tab3", (NB * P, D))

        ident = sb("ident", [P, P])
        iota_n = sb("iota_n", [P, P])
        ones = sb("ones", [P, P])
        X = sb("X", [P, NB, D])
        H = sb("H", [P, NB, D])
        blk = sb("blk", [P, 2, NG], I32)
        base_node = sb("base_node", [P, 2, NG])
        goff = sb("goff", [P, NG], I32)
        rows = sb("rows", [P, ROWS["_end"]])

        with phase() as ctx:
            ii = sb_in(ctx, "ii", [P, P], I32)
            z16 = sb_in(ctx, "z16", [P, PAD * DE // P])
            fk = sb_in(ctx, "fk", [P, 16], I32)
            rinit = sb_in(ctx, "rinit", [P, 80, REC], I32)
            s_id, s_x, s_fill, s_dma, s_ones, s_cast = (sem_in(ctx, n) for n in (
                "ident_zero", "x_zero", "pads_filled", "setup_dma", "ones_set", "iota_done"))
            block = ctx.enter_context(nc.Block())

            @block.gpsimd
            def _(pool):
                pool.memset(ident[:], 0.0).then_inc(s_id, 1)
                pool.wait_ge(s_id, 1)
                pool.affine_select(out=ident[:], in_=ident[:], compare_op=ALU.not_equal, fill=1.0, base=0,
                                   pattern=[[-1, P]], channel_multiplier=1).then_inc(s_id, 1)
                pool.iota(ii[:], [[1, P]], base=0, channel_multiplier=0).then_inc(s_id, 1)

            @block.vector
            def _(dve):
                dve.memset(X[:], 0.0).then_inc(s_x, 1)
                dve.memset(z16[:], 0.0).then_inc(s_fill, 1)
                dve.memset(fk[:, 0:8], FAR).then_inc(s_fill, 1)
                dve.memset(fk[:, 8:16], 0).then_inc(s_fill, 1)
                dve.memset(rinit[:], 0).then_inc(s_fill, 1)
                dve.wait_ge(s_fill, 4)
                dve.memset(rinit[:, :, 0:1], -1).then_inc(s_fill, 1)
                dve.memset(ones[:], 1.0).then_inc(s_ones, 1)
                dve.wait_ge(s_id, 3)
                dve.tensor_copy(iota_n[:], ii[:]).then_inc(s_cast, 1)

            @block.sync
            def _(sp):
                sp.dma_start(rows[:], rowvec.partition_broadcast(P)).then_inc(s_dma, 16)
                sp.wait_ge(s_x, 1)
                sp.dma_start(X[:, 0:NBLK - 1, :], x[0:P * (NBLK - 1), :].rearrange("(b p) d -> p b d", p=P)).then_inc(s_dma, 16)
                sp.dma_start(X[0:last_rows, NBLK - 1, :], x[P * (NBLK - 1):N, :]).then_inc(s_dma, 16)
                sp.dma_start(keyp[1:1 + E].rearrange("(a b) -> a b", a=16), dst.rearrange("(a b) -> a b", a=16)).then_inc(s_dma, 16)
                sp.dma_start(srcp[0:E].rearrange("(a b) -> a b", a=16), src.rearrange("(a b) -> a b", a=16)).then_inc(s_dma, 16)
                sp.dma_start(eap[0:E, :].rearrange("(a b) d -> a (b d)", a=64), ea16.rearrange("(a b) d -> a (b d)", a=64)).then_inc(s_dma, 16)
                sp.wait_ge(s_fill, 5)
                sp.dma_start(keyp[1 + E:1 + E + PAD].rearrange("(p c) -> p c", p=P), fk[:, 0:8]).then_inc(s_dma, 16)
                sp.dma_start(keyp[0:1].rearrange("(p c) -> p c", p=1), rinit[0:1, 0, 0:1]).then_inc(s_dma, 16)
                sp.dma_start(srcp[E:E + PAD].rearrange("(p c) -> p c", p=P), fk[:, 8:16]).then_inc(s_dma, 16)
                sp.dma_start(eap[E:E + PAD, :].rearrange("(p c) d -> p (c d)", p=P), z16[:]).then_inc(s_dma, 16)
                places = NG * T
                rv = rec.rearrange("(p r) c -> p r c", p=P)
                n = 10
                for r in range(0, places, 80):
                    m = min(80, places - r)
                    sp.dma_start(rv[:, r:r + m, :], rinit[:, 0:m, :]).then_inc(s_dma, 16)
                    n += 1
                sp.wait_ge(s_dma, 16 * n)

        with phase() as ctx:
            keys = [sb_in(ctx, f"keys{o}", [P, EPP], I32) for o in range(2)]
            ki = sb_in(ctx, "ki", [P, EPP], I32)
            hi = [sb_in(ctx, f"hi{o}", [P, EPP]) for o in range(2)]
            junk = sb_in(ctx, "junk", [P, EPP], BF16)
            cnt = sb_in(ctx, "cnt", [P, 2, P])
            small = [sb_in(ctx, f"small{o}", [P, 6, P]) for o in range(2)]
            gi = sb_in(ctx, "gi", [P, 2, P], I32)
            cols = sb_in(ctx, "cols", [P, 2, 2])
            jd = sb_in(ctx, "jd", [P, P])
            giota_i = sb_in(ctx, "giota_i", [P, NG], I32)
            giota = sb_in(ctx, "giota", [P, NG])
            past = sb_in(ctx, "past", [P, 2, NG])
            fo = sb_in(ctx, "fo", [P, NG])
            base = sb_in(ctx, "base", [P, P])
            ps_c = ps_in(ctx, "ps_c", [P, 2, P])
            ps_g = ps_in(ctx, "ps_g", [P, 2, 512])
            s_k, s_gi, s_hi, s_cnt, s_ct, s_sm, s_past, s_psg, s_tab = (sem_in(ctx, n) for n in (
                "keys_landed", "group_iota", "hi_steps", "counted", "counts_summed", "table_steps", "past_ready",
                "group_sums", "group_sums_read"))
            NSL = -(-NG // 512)
            with nc.Block() as block:
                @block.sync
                def _(sp):
                    sp.dma_start(keys[0][:], dst.rearrange("(p c) -> p c", p=P)).then_inc(s_k, 16)
                    sp.dma_start(keys[1][:], src.rearrange("(p c) -> p c", p=P)).then_inc(s_k, 16)

                @block.gpsimd
                def _(pool):
                    pool.iota(giota_i[:], [[1, NG]], base=0, channel_multiplier=0).then_inc(s_gi, 1)

                @block.vector
                def _(dve):
                    nh = 0
                    dve.wait_ge(s_gi, 1)
                    dve.tensor_copy(giota[:], giota_i[:]).then_inc(s_hi, 1)
                    dve.memset(cnt[:], 0.0).then_inc(s_hi, 1)
                    dve.wait_ge(s_k, 32)
                    nh = 2
                    for o in range(2):
                        dve.wait_ge(s_hi, nh)
                        dve.tensor_scalar(ki[:], keys[o][:], 7, None, ALU.arith_shift_right).then_inc(s_hi, 1)
                        dve.wait_ge(s_hi, nh + 1)
                        dve.tensor_copy(hi[o][:], ki[:]).then_inc(s_hi, 1)
                        nh += 2
                    dve.wait_ge(s_hi, nh)
                    for o in range(2):
                        def count(b):
                            dve.tensor_scalar(junk[:], hi[o][:], iota_n[:, bass.ds(b, 1)], None, ALU.is_equal, ALU.add,
                                              accum_out=cnt[:, o, bass.ds(b, 1)]).then_inc(s_cnt, 1)

                        at_least(dve, s_cnt, o * NBLK)
                        count(0)
                        with dve.Fori(1, NBLK) as b:
                            dve.wait_ge(s_cnt, b + o * NBLK)
                            count(b)
                    ns = 0
                    dve.wait_ge(s_ct, 1)

                    def do(ins):
                        nonlocal ns
                        ns += 1
                        ins.then_inc(s_sm, 1)
                        dve.wait_ge(s_sm, ns)

                    for o in range(2):
                        c, gf, gend, pad, padsum, at = (small[o][:, k, :] for k in range(6))
                        do(dve.tensor_copy(c, ps_c[:, o, :]))
                        do(dve.tensor_scalar(gf, c, float(GE - 1), None, ALU.add))
                        do(dve.tensor_copy(gi[:, o, :], gf))
                        do(dve.tensor_scalar(gi[:, o, :], gi[:, o, :], 9, None, ALU.arith_shift_right))
                        do(dve.tensor_copy(gf, gi[:, o, :]))
                        do(dve.tensor_tensor_scan(gend, gf, gf, 0.0, ALU.add, ALU.bypass))
                        do(dve.scalar_tensor_tensor(pad, gf, float(GE), c, ALU.mult, ALU.subtract))
                        do(dve.tensor_tensor(at, gend, gf, ALU.subtract))
                        do(dve.tensor_scalar(at, at, float(GE), None, ALU.mult))
                        do(dve.tensor_tensor_reduce(jd[:], gend, ident[:], 1.0, 0.0, ALU.mult, ALU.add, cols[:, o, 0:1]))
                        do(dve.tensor_tensor_reduce(jd[:], pad, ident[:], 1.0, 0.0, ALU.mult, ALU.add, cols[:, o, 1:2]))
                        do(dve.tensor_scalar(past[:, o, :], giota[:], cols[:, o, 0:1], None, ALU.is_ge))
                    do(dve.tensor_copy(base[:], small[1][:, 5, :]))
                    dve.memset(jd[:], 1.0).then_inc(s_past, 1)
                    nt = 0
                    for o in range(2):
                        for c in range(NSL):
                            a, b = 512 * c, min(NG, 512 * c + 512)
                            nt += 1
                            dve.wait_ge(s_psg, nt)
                            do(dve.tensor_scalar(base_node[:, o, a:b], ps_g[:, nt % 2, 0:b - a], float(NB), None, ALU.min))
                            do(dve.tensor_copy(blk[:, o, a:b], base_node[:, o, a:b]))
                            dve.tensor_scalar(base_node[:, o, a:b], base_node[:, o, a:b], float(P), None, ALU.mult).then_inc(s_tab, 1)
                    for c in range(NSL):
                        a, b = 512 * c, min(NG, 512 * c + 512)
                        nt += 1
                        dve.wait_ge(s_psg, nt)
                        do(dve.scalar_tensor_tensor(fo[:, a:b], giota[:, a:b], float(GE), ps_g[:, nt % 2, 0:b - a], ALU.mult, ALU.subtract))
                        do(dve.tensor_scalar(fo[:, a:b], fo[:, a:b], float(E), None, ALU.min))
                        dve.tensor_copy(goff[:, a:b], fo[:, a:b]).then_inc(s_tab, 1)

                @block.tensor
                def _(pe):
                    pe.wait_ge(s_cnt, 2 * NBLK)
                    pe.matmul(ps_c[:].rearrange("p o b -> p (o b)"), ones[:], cnt[:].rearrange("p o b -> p (o b)"), start=True, stop=True).then_inc(s_ct, 1)
                    pe.wait_ge(s_past, 1)
                    nt = 0
                    for o, w in ((0, None), (1, None), (0, 1)):
                        for c in range(NSL):
                            a, b = 512 * c, min(NG, 512 * c + 512)
                            nt += 1
                            at_least(pe, s_tab, nt - 2)
                            lhs = ones[:] if w is None else cols[:, 0, 1:2].broadcast_to([P, P])
                            pe.matmul(ps_g[:, nt % 2, 0:b - a], lhs, past[:, o, a:b], start=True, stop=True).then_inc(s_psg, 1)

            tri = sb_in(ctx, "tri", [P, P], BF16)
            oneb = sb_in(ctx, "oneb", [P, P], BF16)
            oh = sb_in(ctx, "s_oh", [P, 2, SORT_T, NB], BF16)
            tmp = sb_in(ctx, "s_tmp", [P, SORT_T, NB])
            posf = sb_in(ctx, "posf", [P, SORT_T])
            SS = 5
            posi = sb_in(ctx, "posi", [P, SS, SORT_T], I32)
            rb = sb_in(ctx, "rb", [P, SS, SORT_T, REC])
            ps_r = ps_in(ctx, "ps_r", [P, 2, 512])
            ps_s = ps_in(ctx, "ps_s", [P, 2, 512])
            NSTEP = EPP // SORT_T
            s_tri = sem_in(ctx, "tri_ready")
            s_ld = [sem_in(ctx, f"features_landed{k}") for k in range(SS)]
            s_sc = [sem_in(ctx, f"scattered{k}") for k in range(SS)]
            s_oh, s_r, s_add, s_mul, s_red, s_pos, s_base, s_key = (sem_in(ctx, n) for n in (
                "sort_onehot", "sort_ranks", "sort_added", "sort_masked", "sort_reduced", "places_ready", "base_moved", "keys_in_record"))
            ea16v = ea16.rearrange("(p c) d -> p c d", p=P)
            ea64v = ea64.rearrange("(p c) d -> p c d", p=P)
            rbi = rb[:].bitcast(I32)
            with nc.Block() as block:
                @block.sync
                def _(sp):
                    def body(g, k, r):
                        at_least(sp, s_sc[k], r * (16 * SORT_T))
                        settle(sp)
                        sp.dma_start(rb[:, k, :, EA16:EA16 + DE], ea16v[:, bass.ds(g * SORT_T, SORT_T), :]).then_inc(s_ld[k], 16)
                        sp.dma_start(rb[:, k, :, EA64:EA64 + D], ea64v[:, bass.ds(g * SORT_T, SORT_T), :]).then_inc(s_ld[k], 16)
                    steps(sp, NSTEP, body, SS)

                @block.gpsimd
                def _(pool):
                    pool.memset(oneb[:], 1.0).then_inc(s_tri, 1)
                    pool.wait_ge(s_tri, 1)
                    pool.affine_select(out=tri[:], in_=oneb[:], compare_op=ALU.is_gt, fill=0.0, base=0,
                                       pattern=[[1, P]], channel_multiplier=-1).then_inc(s_tri, 1)

                    def body(g, k, r):
                        pool.wait_ge(s_ld[k], r * 32 + 32)
                        pool.wait_ge(s_pos, g + 1)
                        settle(pool)
                        for t in range(SORT_T):
                            pool.indirect_dma_start(rec, bass.IndirectOffsetOnAxis(ap=posi[:, k, t:t + 1], axis=0),
                                                    rbi[:, k, t, :], None).then_inc(s_sc[k], 16)
                    steps(pool, NSTEP, body, SS)
                    for k in range(SS):
                        pool.wait_ge(s_sc[k], 16 * SORT_T * (NSTEP // SS))

                @block.vector
                def _(dve):
                    def body(g, k, r):
                        q = k % 2 if isinstance(g, int) else k % 2
                        cols_g = bass.ds(g * SORT_T, SORT_T)
                        at_least(dve, s_sc[k], r * (16 * SORT_T))
                        dve.tensor_copy(rbi[:, k, :, 0:1], bcast(keys[1][:, cols_g], 2, 1)).then_inc(s_key, 1)
                        dve.tensor_copy(rbi[:, k, :, 1:2], bcast(keys[0][:, cols_g], 2, 1)).then_inc(s_key, 1)
                        at_least(dve, s_r, g)
                        dve.tensor_tensor(oh[:, 0], bcast(iota_n[:, 0:NB], 1, SORT_T), bcast(hi[1][:, cols_g], 2, NB),
                                          ALU.is_equal).then_inc(s_oh, 1)
                        dve.wait_ge(s_r, g + 1)
                        at_least(dve, s_base, g)
                        dve.tensor_tensor(tmp[:], ps_r[:, 0, 0:SORT_T * NB].rearrange("p (t b) -> p t b", t=SORT_T),
                                          bcast(base[:, 0:NB], 1, SORT_T), ALU.add).then_inc(s_add, 1)
                        dve.wait_ge(s_add, g + 1)
                        dve.tensor_tensor(base[:, 0:NB], base[:, 0:NB], ps_s[:, 0, 0:NB], ALU.add).then_inc(s_base, 1)
                        dve.tensor_tensor(tmp[:], tmp[:], oh[:, 0], ALU.mult).then_inc(s_mul, 1)
                        dve.wait_ge(s_mul, g + 1)
                        dve.tensor_reduce(posf[:], tmp[:], AX.X, ALU.add).then_inc(s_red, 1)
                        dve.wait_ge(s_red, g + 1)
                        dve.wait_ge(s_key, g * 2 + 2)
                        dve.tensor_copy(posi[:, k, :], posf[:]).then_inc(s_pos, 1)
                    steps(dve, NSTEP, body, SS)

                @block.tensor
                def _(pe):
                    pe.wait_ge(s_tri, 2)

                    def body(g, k, r):
                        pe.wait_ge(s_oh, g + 1)
                        at_least(pe, s_base, g)
                        for t in range(SORT_T):
                            pe.matmul(ps_r[:, 0, t * NB:t * NB + NB], tri[:], oh[:, 0, t], start=True, stop=(t == 0))
                            for u in range(t):
                                pe.matmul(ps_r[:, 0, t * NB:t * NB + NB], oneb[:], oh[:, 0, u], start=False, stop=(u == t - 1))
                        for t in range(SORT_T):
                            mm = pe.matmul(ps_s[:, 0, 0:NB], oneb[:], oh[:, 0, t], start=(t == 0), stop=(t == SORT_T - 1))
                        mm.then_inc(s_r, 1)
                    steps(pe, NSTEP, body, SS)


        ACC = sb("ACC", [P, NB + 1, HEADS * (D // HEADS + 1)])
        PT = sb("PT", [P, NB + 1, ATT])

        def chain(eng, sem):
            n = 0

            def do(ins):
                nonlocal n
                n += 1
                ins.then_inc(sem, 1)
                eng.wait_ge(sem, n)
            return do

        def layer_input(layer):
            with phase() as ctx:
                st = sb_in(ctx, f"ln_stat{layer}", [P, 4, NB])
                epsc = sb_in(ctx, f"ln_eps{layer}", [P, 1])
                s_v, s_var, s_std = (sem_in(ctx, f"{n}{layer}") for n in ("ln_steps", "ln_var_ready", "ln_std_ready"))
                sq = PT[:, 0:NB, 0:D]
                with nc.Block() as block:
                    @block.vector
                    def _(dve):
                        do = chain(dve, s_v)
                        do(dve.memset(epsc[:], 1e-5))
                        do(dve.tensor_reduce(st[:, 0, :], X[:], AX.X, ALU.add))
                        do(dve.tensor_scalar(st[:, 0, :], st[:, 0, :], 1.0 / D, None, ALU.mult))
                        do(dve.tensor_tensor(H[:], X[:], bcast(st[:, 0, :], 2, D), ALU.subtract))
                        do(dve.tensor_tensor(sq, H[:], H[:], ALU.mult))
                        dve.tensor_reduce(st[:, 1, :], sq, AX.X, ALU.add).then_inc(s_var, 1)
                        do(dve.memset(ACC[:], 0.0))
                        dve.wait_ge(s_std, 1)
                        do(dve.reciprocal(st[:, 3, :], st[:, 2, :]))
                        do(dve.tensor_tensor(H[:], H[:], bcast(st[:, 3, :], 2, D), ALU.mult))
                        do(dve.tensor_scalar(H[:], H[:], 0.0, None, ALU.max))
                        do(dve.memset(PT[:], 0.0))

                    @block.scalar
                    def _(act):
                        act.wait_ge(s_var, 1)
                        act.activation(st[:, 2, :], st[:, 1, :], ACT.Sqrt, bias=epsc[:], scale=1.0 / D).then_inc(s_std, 1)

        def node_tables(layer, weights, width, n_gather, table, fold=False):
            n_pt = width - n_gather
            with phase() as ctx:
                w = sb_in(ctx, f"w_tab{layer}", [D + 1, width])
                hb = sb_in(ctx, f"hb{layer}", [P, 2, D])
                hT = sb_in(ctx, f"hT{layer}", [D + 1, 2, P])
                stage = sb_in(ctx, f"stage{layer}", [P, 2, n_gather])
                ps_t = ps_in(ctx, f"ps_t{layer}", [P, 2, 512])
                ps_w = ps_in(ctx, f"ps_w{layer}", [P, 2, 512])
                s_w, s_one, s_fold, s_hb, s_t, s_hT, s_mm, s_st, s_pt = (sem_in(ctx, f"{n}{layer}") for n in (
                    "weights_landed", "ones_row", "weights_folded", "block_copied", "block_turned", "turned_copied", "rows_ready", "rows_staged", "rows_kept"))
                s_out = [sem_in(ctx, f"rows_stored{layer}_{k}") for k in range(2)]
                with nc.Block() as block:
                    @block.sync
                    def _(sp):
                        sp.dma_start(w[:], weights).then_inc(s_w, 16)

                        def body(b, k, r):
                            sp.wait_ge(s_st, b + 1)
                            settle(sp)
                            sp.dma_start(table[bass.ds(b * P, P), :], stage[:, k, :]).then_inc(s_out[k], 16)
                        steps(sp, NB, body, 2)
                        for k in range(2):
                            sp.wait_ge(s_out[k], 16 * (NB // 2))

                    @block.vector
                    def _(dve):
                        dve.memset(hT[D:D + 1, :, :], 1.0).then_inc(s_one, 1)
                        if fold:
                            dve.wait_ge(s_w, 16)
                            dve.tensor_tensor(w[0:D, D:2 * D], w[0:D, D:2 * D], w[0:D, 0:D], ALU.subtract).then_inc(s_fold, 1)

                        def body(b, k, r):
                            at_least(dve, s_t, b - 1)
                            dve.tensor_copy(hb[:, k, :], H[:, bass.ds(b, 1), :].rearrange("p a d -> p (a d)")).then_inc(s_hb, 1)
                            dve.wait_ge(s_st, b + 1)
                            settle(dve)
                            dve.tensor_copy(PT[:, bass.ds(b, 1), 0:n_pt].rearrange("p a d -> p (a d)"),
                                            ps_w[:, k, n_gather:width]).then_inc(s_pt, 1)
                        steps(dve, NB, body, 2)

                    @block.tensor
                    def _(pe):
                        pe.wait_ge(s_one, 1)
                        pe.wait_ge(s_w, 16)
                        at_least(pe, s_fold, int(fold))

                        def body(b, k, r):
                            pe.wait_ge(s_hb, b + 1)
                            at_least(pe, s_hT, b - 1)
                            settle(pe)
                            pe.transpose(ps_t[0:D, k, 0:P], hb[:, k, :], ident[:]).then_inc(s_t, 1)
                            pe.wait_ge(s_hT, b + 1)
                            at_least(pe, s_st, b - 1)
                            at_least(pe, s_pt, b - 1)
                            pe.matmul(ps_w[:, k, 0:width], hT[:, k, :], w[:], start=True, stop=True).then_inc(s_mm, 1)
                        steps(pe, NB, body, 2)

                    @block.scalar
                    def _(act):
                        def body(b, k, r):
                            act.wait_ge(s_t, b + 1)
                            at_least(act, s_mm, b - 1)
                            act.copy(hT[0:D, k, :], ps_t[0:D, k, 0:P]).then_inc(s_hT, 1)
                            act.wait_ge(s_mm, b + 1)
                            at_least(act, s_out[k], r * 16)
                            act.copy(stage[:, k, :], ps_w[:, k, 0:n_gather]).then_inc(s_st, 1)
                        steps(act, NB, body, 2)

        def attention(layer, order, table, heads, width, we, n_val):
            R = table.shape[1]
            VC = n_val // heads + 1
            v0 = R - n_val
            banks = 1 if T * width <= 512 else 2
            tpb = T // banks
            att = rows[:, ROWS["att"]] if layer == 0 else rows[:, ROWS["w_att2"]]
            with phase() as ctx:
                def sbl(name, shape, dt=F32):
                    return sb_in(ctx, f"{name}{layer}", shape, dt)

                def seml(name):
                    return sem_in(ctx, f"{name}{layer}")

                w = sbl("w_ea", [DE, width])
                if layer == 0:
                    key = sbl("key", [P, SLOTS, T, 1], I32)
                    idx = sbl("idx", [P, SLOTS, T, 1], I32)
                    ea = sbl("ea", [P, SLOTS, T, DE])
                    n_loads = 3
                else:
                    rs = sbl("rs", [P, SLOTS, T, REC], I32)
                    key, idx = rs[:, :, :, 0:1], rs[:, :, :, 1:2]
                    ea = rs[:].bitcast(F32)[:, :, :, EA16:EA16 + DE]
                    n_loads = 1
                G = sbl("G", [P, SLOTS, T, R])
                lo = sbl("lo", [P, T])
                oh = sbl("oh", [P, 2, T, P])
                ohN = sbl("ohN", [P, 2, T, P])
                pen = sbl("pen", [P, 2, T, P])
                eaT = sbl("eaT", [DE, T, P])
                z = sbl("z", [P, T, width])
                lg = sbl("lg", [P, 2, T, heads])
                junk = sbl("junk", [P, T, P], BF16)
                gm = sbl("gm", [P, heads])
                mn = sbl("mn", [P, heads])
                df = sbl("df", [P, heads])
                corr = sbl("corr", [P, heads])
                dd = sbl("dd", [P, T, heads])
                ss = sbl("ss", [P, T, heads])
                V = sbl("V", [P, T, heads, VC])
                M = sbl("M", [P, NB + 1, heads])
                ps_oh = ps_in(ctx, f"ps_oh{layer}", [P, T, P])
                ps_ea = ps_in(ctx, f"ps_ea{layer}", [P, T, P])
                ps_z = ps_in(ctx, f"ps_z{layer}", [P, banks, 512])
                n_lb = min(heads, 2)
                ps_lb = ps_in(ctx, f"ps_lb{layer}", [P, n_lb, T, P])
                ps_m = ps_in(ctx, f"ps_m{layer}", [P, 512])
                ps_a = ps_in(ctx, f"ps_a{layer}", [P, 512])
                zv = [ps_z[:, b, 0:tpb * width].rearrange("p (t c) -> p t c", t=tpb) for b in range(banks)]

                s_w, s_mi = seml("ea_weights"), seml("maxima_set")
                s_ld = [seml(f"edges_landed{k}_") for k in range(SLOTS)]
                s_g = [seml(f"gathered{k}_") for k in range(SLOTS)]
                (s_lo, s_oh, s_ohT, s_ohN, s_pen, s_eaP, s_eaT, s_z, s_add, s_act, s_mul, s_lg0, s_lg, s_mn, s_df, s_mb, s_corr,
                 s_me, s_d0, s_d, s_p, s_V, s_acc, s_sc, s_done) = (seml(n) for n in (
                    "local_key", "onehot", "onehot_turned", "onehot_nodes", "penalty", "ea_turned", "ea_ready", "key_rows",
                    "rows_added", "activated", "weighted", "score_sum", "score", "new_max", "max_step", "max_stored", "rescale",
                    "edge_max", "score_less_max", "exponent", "weight", "values", "group_sums", "acc_rescaled", "group_done"))
                s_lb = [seml(f"scores_spread{h}_") for h in range(heads)]
                s_gm = [seml(f"group_max{h}_") for h in range(heads)]

                with nc.Block() as block:
                    @block.sync
                    def _(sp):
                        sp.dma_start(w[:], we).then_inc(s_w, 16)

                        def body(g, k, r):
                            at_least(sp, s_lo, g - SLOTS + 1)
                            settle(sp)
                            at_least(sp, s_g[k], r * (16 * T))
                            at_least(sp, s_eaP, g - SLOTS + 1)
                            settle(sp)
                            if layer == 0:
                                e = sp.value_load(goff[0:1, bass.ds(g, 1)], min_val=0, max_val=E)
                                sp.dma_start(key[:, k, :, 0], keyp[bass.ds(e + 1, GE)].rearrange("(p t) -> p t", p=P)).then_inc(s_ld[k], 16)
                                sp.dma_start(idx[:, k, :, 0], srcp[bass.ds(e, GE)].rearrange("(p t) -> p t", p=P)).then_inc(s_ld[k], 16)
                                sp.dma_start(ea[:, k], eap[bass.ds(e, GE), :].rearrange("(p t) c -> p t c", p=P)).then_inc(s_ld[k], 16)
                            else:
                                sp.dma_start(rs[:, k], rec[bass.ds(g * GE, GE), :].rearrange("(p t) c -> p t c", p=P)).then_inc(s_ld[k], 16)
                        steps(sp, NG, body)

                    @block.gpsimd
                    def _(pool):
                        def body(g, k, r):
                            at_least(pool, s_V, g - SLOTS + 1)
                            pool.wait_ge(s_ld[k], (r + 1) * (16 * n_loads))
                            settle(pool)
                            for t in range(T):
                                pool.indirect_dma_start(G[:, k, t, :], None, table,
                                                        bass.IndirectOffsetOnAxis(ap=idx[:, k, t, :], axis=0)).then_inc(s_g[k], 16)
                        steps(pool, NG, body)

                    @block.vector
                    def _(dve):
                        dve.memset(M[:], -BIG).then_inc(s_mi, 1)
                        dve.wait_ge(s_mi, 1)

                        def onehot(g, k, r):
                            q = k % 2
                            dve.wait_ge(s_ld[k], (r + 1) * (16 * n_loads))
                            dve.tensor_scalar(lo[:], key[:, k, :, 0], base_node[:, order, bass.ds(g, 1)], None, ALU.subtract).then_inc(s_lo, 1)
                            dve.wait_ge(s_lo, g + 1)
                            at_least(dve, s_acc, g - 1)
                            dve.tensor_tensor(oh[:, q], bcast(iota_n[:], 1, T), bcast(lo[:], 2, P), ALU.is_equal).then_inc(s_oh, 1)

                        def scores(g, k, r):
                            q = k % 2
                            dve.wait_ge(s_g[k], (r + 1) * (16 * T))
                            dve.wait_ge(s_z, g + 1)
                            for b in range(banks):
                                ts = slice(b * tpb, (b + 1) * tpb)
                                dve.tensor_tensor(z[:, ts, :], zv[b], G[:, k, ts, 0:width], ALU.add).then_inc(s_add, 1)
                            dve.wait_ge(s_add, g * banks + banks)
                            if layer == 0:
                                dve.scalar_tensor_tensor(z[:], z[:], 0.2, z[:], ALU.mult, ALU.max).then_inc(s_act, 1)
                                dve.wait_ge(s_act, g + 1)
                                dve.tensor_tensor(z[:], z[:], bcast(att, 1, T), ALU.mult).then_inc(s_mul, 1)
                            else:
                                dve.scalar_tensor_tensor(z[:], z[:], 0.0, bcast(att, 1, T), ALU.max, ALU.mult).then_inc(s_mul, 1)
                            dve.wait_ge(s_mul, g + 1)
                            zr = z[:].rearrange("p t (h c) -> p t h c", h=heads)
                            if layer == 0:
                                dve.tensor_reduce(lg[:, q], zr, AX.X, ALU.add).then_inc(s_lg, 1)
                            else:
                                at_least(dve, s_lg, g)
                                dve.tensor_reduce(ss[:], zr, AX.X, ALU.add).then_inc(s_lg0, 1)
                                dve.wait_ge(s_lg0, g + 1)
                                dve.tensor_scalar(lg[:, q], ss[:], rows[:, ROWS["b_att2"]], None, ALU.add).then_inc(s_lg, 1)

                        def maxima(g, k, r):
                            q = k % 2
                            blk_g = dve.value_load(blk[0:1, order, bass.ds(g, 1)], min_val=0, max_val=NB)
                            m_old = M[:, bass.ds(blk_g, 1), :].rearrange("p a h -> p (a h)")
                            for h in range(heads):
                                dve.wait_ge(s_lb[h], g + 1)
                                if h == 0:
                                    dve.wait_ge(s_pen, g + 1)
                                else:
                                    dve.wait_ge(s_gm[h - 1], g + 1)
                                settle(dve)
                                dve.tensor_tensor_reduce(junk[:].rearrange("p t e -> p (t e)"), ps_lb[:, h % n_lb].rearrange("p t e -> p (t e)"),
                                                         pen[:, q].rearrange("p t e -> p (t e)"), 1.0, -BIG, ALU.add, ALU.max,
                                                         gm[:, h:h + 1]).then_inc(s_gm[h], 1)
                            dve.wait_ge(s_gm[heads - 1], g + 1)
                            dve.tensor_tensor(mn[:], m_old, gm[:], ALU.max).then_inc(s_mn, 1)
                            dve.wait_ge(s_mn, g + 1)
                            at_least(dve, s_corr, g)
                            dve.tensor_tensor(df[:], m_old, mn[:], ALU.subtract).then_inc(s_df, 1)
                            dve.wait_ge(s_df, g + 1)
                            settle(dve)
                            dve.tensor_copy(m_old, mn[:]).then_inc(s_mb, 1)

                        def sums(g, k, r):
                            q = k % 2
                            blk_g = dve.value_load(blk[0:1, order, bass.ds(g, 1)], min_val=0, max_val=NB)
                            acc = ACC[:, bass.ds(blk_g, 1), 0:heads * VC].rearrange("p a (h c) -> p (a h) c", h=heads)
                            dve.wait_ge(s_me, g + 1)
                            dve.tensor_tensor(dd[:].rearrange("p t h -> p (t h)"), lg[:, q].rearrange("p t h -> p (t h)"),
                                              ps_m[:, 0:T * heads], ALU.subtract).then_inc(s_d0, 1)
                            dve.wait_ge(s_d0, g + 1)
                            dve.tensor_scalar(dd[:], dd[:], 0.0, None, ALU.min).then_inc(s_d, 1)
                            dve.wait_ge(s_corr, g + 1)
                            dve.tensor_tensor(acc, acc, bcast(corr[:], 2, VC), ALU.mult).then_inc(s_sc, 1)
                            dve.wait_ge(s_p, g + 1)
                            dve.tensor_tensor(V[:, :, :, 0:VC - 1], G[:, k, :, v0:R].rearrange("p t (h c) -> p t h c", h=heads),
                                              V[:, :, :, VC - 1:VC].broadcast_to([P, T, heads, VC - 1]), ALU.mult).then_inc(s_V, 1)
                            dve.wait_ge(s_sc, g + 1)
                            dve.wait_ge(s_acc, g + 1)
                            dve.tensor_tensor(acc, acc, ps_a[:, 0:heads * VC].rearrange("p (h c) -> p h c", h=heads), ALU.add).then_inc(s_done, 1)

                        def body(g, k, r):
                            onehot(g, k, r)
                            prev = (g - 1, (k - 1) % SLOTS, r if k else r - 1)
                            if not (isinstance(g, int) and g == 0):
                                at_least(dve, s_done, prev[0])
                                at_least(dve, s_mb, prev[0])
                                maxima(*prev)
                            scores(g, k, r)
                            if not (isinstance(g, int) and g == 0):
                                sums(*prev)
                        steps(dve, NG, body)
                        last = (NG - 1, SLOTS - 1, NG // SLOTS - 1)
                        dve.wait_ge(s_done, NG - 1)
                        dve.wait_ge(s_mb, NG - 1)
                        maxima(*last)
                        sums(*last)
                        dve.wait_ge(s_done, NG)

                    @block.tensor
                    def _(pe):
                        pe.wait_ge(s_w, 16)

                        def spread(g, k, hs):
                            q = k % 2
                            for h in hs:
                                if h == 0:
                                    pe.wait_ge(s_lg, g + 1)
                                if h >= n_lb:
                                    pe.wait_ge(s_gm[h - n_lb], g + 1)
                                else:
                                    at_least(pe, s_gm[heads - n_lb + h], g)
                                for t in range(T):
                                    mm = pe.matmul(ps_lb[:, h % n_lb, t, :], lg[:, q, t, h:h + 1].broadcast_to([P, P]), ident[:], start=True, stop=True)
                                mm.then_inc(s_lb[h], 1)

                        def turn(g, k, r):
                            q = k % 2
                            pe.wait_ge(s_oh, g + 1)
                            at_least(pe, s_ohN, g)
                            at_least(pe, s_pen, g)
                            for t in range(T):
                                mm = pe.transpose(ps_oh[:, t, :], oh[:, q, t, :], ident[:])
                            mm.then_inc(s_ohT, 1)
                            pe.wait_ge(s_ld[k], (r + 1) * (16 * n_loads))
                            at_least(pe, s_eaT, g)
                            for t in range(T):
                                mm = pe.transpose(ps_ea[0:DE, t, :], ea[:, k, t, :], ident[:])
                            mm.then_inc(s_eaP, 1)

                        def key_rows(g, k, r):
                            q = k % 2
                            blk_g = pe.value_load(blk[0:1, order, bass.ds(g, 1)], min_val=0, max_val=NB)
                            pe.wait_ge(s_ohN, g + 1)
                            pe.wait_ge(s_eaT, g + 1)
                            at_least(pe, s_add, g * banks)
                            for t in range(T):
                                pe.matmul(zv[t // tpb][:, t % tpb, :], ohN[:, q, t, :], PT[:, bass.ds(blk_g, 1), 0:width].rearrange("p a c -> p (a c)"),
                                          start=True, stop=False)
                                mm = pe.matmul(zv[t // tpb][:, t % tpb, :], eaT[:, t, :], w[:], start=False, stop=True)
                            mm.then_inc(s_z, 1)

                        def edge_sums(g, k, r):
                            q = k % 2
                            pe.wait_ge(s_mn, g + 1)
                            at_least(pe, s_d0, g)
                            for t in range(T):
                                mm = pe.matmul(ps_m[:, t * heads:(t + 1) * heads], ohN[:, q, t, :], mn[:], start=True, stop=True)
                            mm.then_inc(s_me, 1)
                            pe.wait_ge(s_V, g + 1)
                            at_least(pe, s_done, g)
                            for t in range(T):
                                mm = pe.matmul(ps_a[:, 0:heads * VC], oh[:, q, t, :], V[:, t].rearrange("p h c -> p (h c)"),
                                               start=(t == 0), stop=(t == T - 1))
                            mm.then_inc(s_acc, 1)

                        def body(g, k, r):
                            prev = (g - 1, (k - 1) % SLOTS, r if k else r - 1)
                            first = isinstance(g, int) and g == 0
                            turn(g, k, r)
                            if not first:
                                spread(prev[0], prev[1], range(heads))
                            key_rows(g, k, r)
                            if not first:
                                edge_sums(*prev)
                        steps(pe, NG, body)
                        last = (NG - 1, SLOTS - 1, NG // SLOTS - 1)
                        spread(last[0], last[1], range(heads))
                        edge_sums(*last)

                    @block.scalar
                    def _(act):
                        def copies(g, k, r):
                            q = k % 2
                            act.wait_ge(s_ohT, g + 1)
                            at_least(act, s_me, g - 1)
                            act.copy(ohN[:, q], ps_oh[:]).then_inc(s_ohN, 1)
                            at_least(act, s_gm[heads - 1], g - 1)
                            act.activation(pen[:, q], ps_oh[:], ACT.Copy, bias=-BIG, scale=BIG).then_inc(s_pen, 1)
                            act.wait_ge(s_eaP, g + 1)
                            at_least(act, s_z, g)
                            act.copy(eaT[:], ps_ea[0:DE]).then_inc(s_eaT, 1)

                        def weights(g, k, r):
                            act.wait_ge(s_df, g + 1)
                            at_least(act, s_sc, g)
                            act.activation(corr[:], df[:], ACT.Exp).then_inc(s_corr, 1)
                            act.wait_ge(s_d, g + 1)
                            at_least(act, s_acc, g)
                            act.activation(V[:, :, :, VC - 1], dd[:], ACT.Exp).then_inc(s_p, 1)

                        def body(g, k, r):
                            copies(g, k, r)
                            if not (isinstance(g, int) and g == 0):
                                weights(g - 1, (k - 1) % SLOTS, r if k else r - 1)
                        steps(act, NG, body)
                        weights(NG - 1, SLOTS - 1, NG // SLOTS - 1)

        def segment_max():
            with phase() as ctx:
                w = sb_in(ctx, "w2_sb", [D, D])
                key = sb_in(ctx, "m_key", [P, SLOTS, T], I32)
                nxt = sb_in(ctx, "m_next", [P, SLOTS, T], I32)
                idx = sb_in(ctx, "m_idx", [P, SLOTS, T, 1], I32)
                row = sb_in(ctx, "m_row", [D, SLOTS, 1 + GE], I32)
                G = sb_in(ctx, "m_G", [P, SLOTS, T, D])
                lo = sb_in(ctx, "m_lo", [P, 3, T])
                oh = sb_in(ctx, "m_oh", [P, T, P])
                ohL = sb_in(ctx, "m_ohL", [P, 2, T, P])
                ohN = sb_in(ctx, "m_ohN", [P, T, P])
                fl = sb_in(ctx, "m_fl", [D, GE])
                flp = sb_in(ctx, "m_flp", [D, 2, GE])
                z = sb_in(ctx, "m_z", [P, T, D])
                zr = sb_in(ctx, "m_zr", [P, T, D])
                zT = sb_in(ctx, "m_zT", [D, GE])
                S = sb_in(ctx, "m_S", [D, 2, GE])
                Sx = sb_in(ctx, "m_Sx", [P, T, D + 1])
                ps_oh = ps_in(ctx, "m_ps_oh", [P, T, P])
                ps_z = ps_in(ctx, "m_ps_z", [P, T, P])
                ps_t = ps_in(ctx, "m_ps_t", [P, GE])
                ps_m = ps_in(ctx, "m_ps_m", [P, GE])
                ps_s = ps_in(ctx, "m_ps_s", [P, T, P])
                ps_a = ps_in(ctx, "m_ps_a", [P, 512])
                (s_w, s_one, s_lo, s_eq, s_lol, s_oh, s_ohL, s_fl, s_flp, s_ohT, s_ohN, s_kr, s_z, s_zr, s_tp, s_zT, s_msg, s_scan, s_st, s_Sx,
                 s_acc, s_done) = (sem_in(ctx, "m_" + n) for n in (
                    "weights", "ones_column", "local_key", "same_as_next", "last_key", "onehot", "onehot_last", "changes", "resets",
                    "onehot_turned", "onehot_nodes", "key_rows", "rows_added", "hidden", "hidden_turned", "hidden_copied", "messages",
                    "scanned", "scan_turned", "scan_copied", "group_values", "group_done"))
                s_ld = [sem_in(ctx, f"m_edges_landed{k}") for k in range(SLOTS)]
                s_g = [sem_in(ctx, f"m_gathered{k}") for k in range(SLOTS)]
                N_LOADS = 4
                with nc.Block() as block:
                    @block.sync
                    def _(sp):
                        sp.dma_start(w[:], w2).then_inc(s_w, 16)

                        def body(g, k, r):
                            at_least(sp, s_lol, g - SLOTS + 1)
                            at_least(sp, s_fl, g - SLOTS + 1)
                            settle(sp)
                            at_least(sp, s_g[k], r * (16 * T))
                            settle(sp)
                            e = sp.value_load(goff[0:1, bass.ds(g, 1)], min_val=0, max_val=E)
                            sp.dma_start(key[:, k, :], keyp[bass.ds(e + 1, GE)].rearrange("(p t) -> p t", p=P)).then_inc(s_ld[k], 16)
                            sp.dma_start(nxt[:, k, :], keyp[bass.ds(e + 2, GE)].rearrange("(p t) -> p t", p=P)).then_inc(s_ld[k], 16)
                            sp.dma_start(idx[:, k, :, 0], srcp[bass.ds(e, GE)].rearrange("(p t) -> p t", p=P)).then_inc(s_ld[k], 16)
                            sp.dma_start(row[:, k, :], keyp[bass.ds(e, GE + 1)].partition_broadcast(D)).then_inc(s_ld[k], 16)
                        steps(sp, NG, body)

                    @block.gpsimd
                    def _(pool):
                        def body(g, k, r):
                            at_least(pool, s_z, g - SLOTS + 1)
                            pool.wait_ge(s_ld[k], (r + 1) * (16 * N_LOADS))
                            settle(pool)
                            for t in range(T):
                                pool.indirect_dma_start(G[:, k, t, :], None, tab1,
                                                        bass.IndirectOffsetOnAxis(ap=idx[:, k, t, :], axis=0)).then_inc(s_g[k], 16)
                        steps(pool, NG, body)

                    @block.vector
                    def _(dve):
                        dve.memset(Sx[:], 1.0).then_inc(s_one, 1)

                        def onehots(g, k, r):
                            q = k % 2
                            dve.wait_ge(s_ld[k], (r + 1) * (16 * N_LOADS))
                            dve.tensor_scalar(lo[:, 0], key[:, k], base_node[:, 0, bass.ds(g, 1)], None, ALU.subtract).then_inc(s_lo, 1)
                            dve.tensor_tensor(lo[:, 1], key[:, k], nxt[:, k], ALU.is_equal).then_inc(s_eq, 1)
                            dve.wait_ge(s_lo, g + 1)
                            dve.wait_ge(s_eq, g + 1)
                            dve.scalar_tensor_tensor(lo[:, 2], lo[:, 1], float(FAR), lo[:, 0], ALU.mult, ALU.add).then_inc(s_lol, 1)
                            at_least(dve, s_ohT, g)
                            dve.tensor_tensor(oh[:], bcast(iota_n[:], 1, T), bcast(lo[:, 0], 2, P), ALU.is_equal).then_inc(s_oh, 1)
                            dve.wait_ge(s_lol, g + 1)
                            at_least(dve, s_acc, g - 1)
                            dve.tensor_tensor(ohL[:, q], bcast(iota_n[:], 1, T), bcast(lo[:, 2], 2, P), ALU.is_equal).then_inc(s_ohL, 1)
                            at_least(dve, s_flp, g)
                            dve.tensor_tensor(fl[:], row[:, k, 1:1 + GE], row[:, k, 0:GE], ALU.not_equal).then_inc(s_fl, 1)

                        def scan(g, k, r):
                            q = k % 2
                            first = isinstance(g, int) and g == 0
                            dve.wait_ge(s_msg, g + 1)
                            dve.wait_ge(s_flp, g + 1)
                            at_least(dve, s_st, g - 1)
                            at_least(dve, s_scan, g)
                            dve.tensor_tensor_scan(S[:, q], flp[:, q], ps_m[0:D, :], 0.0 if first else S[:, 1 - q, GE - 1:GE],
                                                   ALU.add, ALU.max).then_inc(s_scan, 1)

                        def add(g, k, r):
                            dve.wait_ge(s_g[k], (r + 1) * (16 * T))
                            dve.wait_ge(s_kr, g + 1)
                            at_least(dve, s_zr, g)
                            dve.tensor_tensor(z[:], ps_z[:, :, 0:D], G[:, k], ALU.add).then_inc(s_z, 1)

                        def keep(g, k, r):
                            blk_g = dve.value_load(blk[0:1, 0, bass.ds(g, 1)], min_val=0, max_val=NB)
                            acc = ACC[:, bass.ds(blk_g, 1), 0:D + 1].rearrange("p a c -> p (a c)")
                            dve.wait_ge(s_acc, g + 1)
                            at_least(dve, s_done, g)
                            dve.tensor_tensor(acc, acc, ps_a[:, 0:D + 1], ALU.add).then_inc(s_done, 1)

                        def body(g, k, r):
                            prev = (g - 1, (k - 1) % SLOTS, r if k else r - 1)
                            first = isinstance(g, int) and g == 0
                            onehots(g, k, r)
                            if not first:
                                scan(*prev)
                            add(g, k, r)
                            if not first:
                                keep(*prev)
                        steps(dve, NG, body)
                        last = (NG - 1, SLOTS - 1, NG // SLOTS - 1)
                        scan(*last)
                        keep(*last)

                    @block.tensor
                    def _(pe):
                        pe.wait_ge(s_w, 16)

                        def turn(g, k, r):
                            pe.wait_ge(s_oh, g + 1)
                            at_least(pe, s_ohN, g)
                            for t in range(T):
                                mm = pe.transpose(ps_oh[:, t, :], oh[:, t, :], ident[:])
                            mm.then_inc(s_ohT, 1)

                        def messages(g, k, r):
                            pe.wait_ge(s_zr, g + 1)
                            at_least(pe, s_zT, g)
                            settle(pe)
                            for t in range(T):
                                mm = pe.transpose(ps_t[0:D, :].rearrange("d (p t) -> d t p", t=T)[:, t, :], zr[:, t, :], ident[:])
                            mm.then_inc(s_tp, 1)
                            pe.wait_ge(s_zT, g + 1)
                            at_least(pe, s_scan, g)
                            settle(pe)
                            pe.matmul(ps_m[0:D, :], w[:], zT[:], start=True, stop=True).then_inc(s_msg, 1)

                        def key_rows(g, k, r):
                            blk_g = pe.value_load(blk[0:1, 0, bass.ds(g, 1)], min_val=0, max_val=NB)
                            pe.wait_ge(s_ohN, g + 1)
                            at_least(pe, s_z, g)
                            for t in range(T):
                                mm = pe.matmul(ps_z[:, t, 0:D], ohN[:, t, :], PT[:, bass.ds(blk_g, 1), 0:D].rearrange("p a c -> p (a c)"),
                                               start=True, stop=True)
                            mm.then_inc(s_kr, 1)

                        def values(g, k, r):
                            q = k % 2
                            pe.wait_ge(s_scan, g + 1)
                            at_least(pe, s_Sx, g)
                            settle(pe)
                            for t in range(T):
                                mm = pe.transpose(ps_s[:, t, 0:D], S[:, q, :].rearrange("d (p t) -> d t p", t=T)[:, t, :], ident[0:D, 0:D])
                            mm.then_inc(s_st, 1)
                            pe.wait_ge(s_Sx, g + 1)
                            pe.wait_ge(s_ohL, g + 1)
                            at_least(pe, s_done, g)
                            for t in range(T):
                                mm = pe.matmul(ps_a[:, 0:D + 1], ohL[:, q, t, :], Sx[:, t, :], start=(t == 0), stop=(t == T - 1))
                            mm.then_inc(s_acc, 1)

                        def body(g, k, r):
                            prev = (g - 1, (k - 1) % SLOTS, r if k else r - 1)
                            first = isinstance(g, int) and g == 0
                            turn(g, k, r)
                            if not first:
                                messages(*prev)
                            key_rows(g, k, r)
                            if not first:
                                values(*prev)
                        steps(pe, NG, body)
                        last = (NG - 1, SLOTS - 1, NG // SLOTS - 1)
                        messages(*last)
                        values(*last)

                    @block.scalar
                    def _(act):
                        act.wait_ge(s_one, 1)

                        def copies(g, k, r):
                            act.wait_ge(s_ohT, g + 1)
                            at_least(act, s_kr, g)
                            act.copy(ohN[:], ps_oh[:]).then_inc(s_ohN, 1)
                            act.wait_ge(s_fl, g + 1)
                            at_least(act, s_scan, g - 1)
                            act.activation(flp[:, k % 2], fl[:], ACT.Copy, scale=-3.0e38).then_inc(s_flp, 1)

                        def hidden_turned(g, k, r):
                            act.wait_ge(s_tp, g + 1)
                            at_least(act, s_msg, g)
                            act.copy(zT[:], ps_t[0:D, :]).then_inc(s_zT, 1)

                        def scanned(g, k, r):
                            act.wait_ge(s_st, g + 1)
                            at_least(act, s_acc, g)
                            act.copy(Sx[:, :, 0:D], ps_s[:, :, 0:D]).then_inc(s_Sx, 1)

                        def relu(g, k, r):
                            act.wait_ge(s_z, g + 1)
                            at_least(act, s_tp, g)
                            act.activation(zr[:], z[:], ACT.Relu).then_inc(s_zr, 1)

                        def body(g, k, r):
                            prev = (g - 1, (k - 1) % SLOTS, r if k else r - 1)
                            first = isinstance(g, int) and g == 0
                            copies(g, k, r)
                            if not first:
                                hidden_turned(*prev)
                            relu(g, k, r)
                            if not first:
                                scanned(*prev)
                        steps(act, NG, body)
                        last = (NG - 1, SLOTS - 1, NG // SLOTS - 1)
                        hidden_turned(*last)
                        scanned(*last)

        def segment_sum():
            with phase() as ctx:
                rs = sb_in(ctx, "g_rs", [P, SLOTS, T, REC], I32)
                ea = rs[:].bitcast(F32)[:, :, :, EA64:EA64 + D]
                G = sb_in(ctx, "g_G", [P, SLOTS, T, D])
                lo = sb_in(ctx, "g_lo", [P, T])
                oh = sb_in(ctx, "g_oh", [P, 2, T, P])
                z = sb_in(ctx, "g_z", [P, 2, T, D])
                zr = sb_in(ctx, "g_zr", [P, 2, T, D])
                ps_a = ps_in(ctx, "g_ps_a", [P, 2, 512])
                s_lo, s_oh, s_z, s_zr, s_acc, s_done = (sem_in(ctx, "g_" + n) for n in (
                    "local_key", "onehot", "rows_added", "messages", "group_sums", "group_done"))
                s_ld = [sem_in(ctx, f"g_edges_landed{k}") for k in range(SLOTS)]
                s_g = [sem_in(ctx, f"g_gathered{k}") for k in range(SLOTS)]
                with nc.Block() as block:
                    @block.sync
                    def _(sp):
                        def body(g, k, r):
                            at_least(sp, s_z, g - SLOTS + 1)
                            settle(sp)
                            at_least(sp, s_g[k], r * (16 * T))
                            settle(sp)
                            sp.dma_start(rs[:, k], rec[bass.ds(g * GE, GE), :].rearrange("(p t) c -> p t c", p=P)).then_inc(s_ld[k], 16)
                        steps(sp, NG, body)

                    @block.gpsimd
                    def _(pool):
                        def body(g, k, r):
                            at_least(pool, s_z, g - SLOTS + 1)
                            pool.wait_ge(s_ld[k], (r + 1) * 16)
                            settle(pool)
                            for t in range(T):
                                pool.indirect_dma_start(G[:, k, t, :], None, tab3,
                                                        bass.IndirectOffsetOnAxis(ap=rs[:, k, t, 1:2], axis=0)).then_inc(s_g[k], 16)
                        steps(pool, NG, body)

                    @block.vector
                    def _(dve):
                        def group(g, k, r):
                            q = k % 2
                            dve.wait_ge(s_ld[k], (r + 1) * 16)
                            at_least(dve, s_oh, g)
                            dve.tensor_scalar(lo[:], rs[:, k, :, 0], base_node[:, 1, bass.ds(g, 1)], None, ALU.subtract).then_inc(s_lo, 1)
                            dve.wait_ge(s_lo, g + 1)
                            at_least(dve, s_acc, g - 1)
                            dve.tensor_tensor(oh[:, q], bcast(iota_n[:], 1, T), bcast(lo[:], 2, P), ALU.is_equal).then_inc(s_oh, 1)
                            dve.wait_ge(s_g[k], (r + 1) * (16 * T))
                            at_least(dve, s_zr, g - 1)
                            dve.tensor_tensor(z[:, q], G[:, k], ea[:, k], ALU.add).then_inc(s_z, 1)

                        def keep(g, k, r):
                            blk_g = dve.value_load(blk[0:1, 1, bass.ds(g, 1)], min_val=0, max_val=NB)
                            acc = ACC[:, bass.ds(blk_g, 1), 0:D].rearrange("p a c -> p (a c)")
                            dve.wait_ge(s_acc, g + 1)
                            at_least(dve, s_done, g)
                            dve.tensor_tensor(acc, acc, ps_a[:, k % 2, 0:D], ALU.add).then_inc(s_done, 1)

                        def body(g, k, r):
                            group(g, k, r)
                            if not (isinstance(g, int) and g == 0):
                                keep(g - 1, (k - 1) % SLOTS, r if k else r - 1)
                        steps(dve, NG, body)
                        keep(NG - 1, SLOTS - 1, NG // SLOTS - 1)

                    @block.scalar
                    def _(act):
                        def body(g, k, r):
                            act.wait_ge(s_z, g + 1)
                            at_least(act, s_acc, g - 1)
                            act.activation(zr[:, k % 2], z[:, k % 2], ACT.Relu).then_inc(s_zr, 1)
                        steps(act, NG, body)

                    @block.tensor
                    def _(pe):
                        def body(g, k, r):
                            q = k % 2
                            pe.wait_ge(s_oh, g + 1)
                            pe.wait_ge(s_zr, g + 1)
                            at_least(pe, s_done, g - 1)
                            for t in range(T):
                                mm = pe.matmul(ps_a[:, q, 0:D], oh[:, q, t, :], zr[:, q, t, :], start=(t == 0), stop=(t == T - 1))
                            mm.then_inc(s_acc, 1)
                        steps(pe, NG, body)

        def finish_gat():
            with phase() as ctx:
                rd = sb_in(ctx, "b_rd", [P, NB, HEADS])
                small = sb_in(ctx, "b_small", [P, 4, D])
                valid = sb_in(ctx, "b_valid", [P, 2])
                junk = sb_in(ctx, "b_junk", [P, P])
                epsc = sb_in(ctx, "b_eps", [P, 1])
                ps = ps_in(ctx, "b_ps", [P, 2, 512])
                s_v, s_sum, s_tot, s_std0, s_std, s_pre, s_gelu = (sem_in(ctx, "b_" + n) for n in (
                    "steps", "sums_ready", "totals", "var_ready", "std_ready", "pre_gelu", "gelu"))
                O, Q = PT[:, 0:NB, 0:D], PT[:, 0:NB, D:2 * D]
                OL = PT[:, NBLK - 1, 0:D]
                acc = ACC[:, 0:NB, :].rearrange("p b (h c) -> p b h c", h=HEADS)
                C = D // HEADS
                with nc.Block() as block:
                    @block.vector
                    def _(dve):
                        do = chain(dve, s_v)
                        do(dve.memset(epsc[:], 1e-5))
                        do(dve.tensor_tensor_reduce(junk[:], ident[:], iota_n[:], 1.0, 0.0, ALU.mult, ALU.add, valid[:, 0:1]))
                        do(dve.tensor_scalar(valid[:, 1:2], valid[:, 0:1], float(last_rows), None, ALU.is_lt))
                        do(dve.tensor_scalar(rd[:], acc[:, :, :, C], 1e-16, None, ALU.add))
                        do(dve.reciprocal(rd[:], rd[:]))
                        for h in range(HEADS):
                            do(dve.tensor_tensor(PT[:, 0:NB, h * C:(h + 1) * C], acc[:, :, h, 0:C], bcast(rd[:, :, h], 2, C), ALU.mult))
                        do(dve.tensor_tensor(O, O, bcast(rows[:, ROWS["bias"]], 1, NB), ALU.add))
                        for b in range(NBLK, NB):
                            do(dve.memset(PT[:, b, 0:D], 0.0))
                        do(dve.tensor_scalar(OL, OL, valid[:, 1:2], None, ALU.mult))
                        dve.tensor_reduce(small[:, 0], O.rearrange("p b d -> p d b"), AX.X, ALU.add).then_inc(s_sum, 1)
                        dve.wait_ge(s_tot, 1)
                        do(dve.tensor_scalar(small[:, 1], ps[:, 0, 0:D], 1.0 / N, None, ALU.mult))
                        do(dve.tensor_tensor(O, O, bcast(small[:, 1], 1, NB), ALU.subtract))
                        for b in range(NBLK, NB):
                            do(dve.memset(PT[:, b, 0:D], 0.0))
                        do(dve.tensor_scalar(OL, OL, valid[:, 1:2], None, ALU.mult))
                        do(dve.tensor_tensor(Q, O, O, ALU.mult))
                        dve.tensor_reduce(small[:, 2], Q.rearrange("p b d -> p d b"), AX.X, ALU.add).then_inc(s_sum, 1)
                        dve.wait_ge(s_tot, 2)
                        dve.tensor_scalar(small[:, 3], ps[:, 1, 0:D], 1.0 / N, None, ALU.mult).then_inc(s_std0, 1)
                        dve.wait_ge(s_std, 1)
                        do(dve.reciprocal(small[:, 1], small[:, 0]))
                        do(dve.tensor_tensor(small[:, 1], small[:, 1], rows[:, ROWS["gamma"]], ALU.mult))
                        do(dve.tensor_tensor(O, O, bcast(small[:, 1], 1, NB), ALU.mult))
                        do(dve.tensor_tensor(O, O, bcast(rows[:, ROWS["beta"]], 1, NB), ALU.add))
                        dve.tensor_tensor(O, O, H[:], ALU.add).then_inc(s_pre, 1)
                        dve.wait_ge(s_gelu, 1)
                        do(dve.tensor_tensor(X[:], X[:], Q, ALU.add))

                    @block.tensor
                    def _(pe):
                        for i in range(2):
                            pe.wait_ge(s_sum, i + 1)
                            pe.matmul(ps[:, i, 0:D], ones[:], small[:, 2 * i], start=True, stop=True).then_inc(s_tot, 1)

                    @block.scalar
                    def _(act):
                        act.wait_ge(s_std0, 1)
                        act.activation(small[:, 0], small[:, 3], ACT.Sqrt, bias=epsc[:]).then_inc(s_std, 1)
                        act.wait_ge(s_pre, 1)
                        act.activation(Q, O, ACT.Gelu).then_inc(s_gelu, 1)

        def finish_max():
            with phase() as ctx:
                s_v = sem_in(ctx, "x_steps")
                with nc.Block() as block:
                    @block.vector
                    def _(dve):
                        do = chain(dve, s_v)
                        t = PT[:, 0:NB, 0:D]
                        do(dve.tensor_tensor(t, bcast(rows[:, ROWS["b2_l1"]], 1, NB), ACC[:, 0:NB, D:D + 1].broadcast_to([P, NB, D]), ALU.mult))
                        do(dve.tensor_tensor(t, t, ACC[:, 0:NB, 0:D], ALU.add))
                        do(dve.tensor_tensor(X[:], X[:], t, ALU.add))

        def finish_gru():
            with phase() as ctx:
                w = sb_in(ctx, "r_w", [P, 4 * D])
                bias = sb_in(ctx, "r_bias", [2, 4 * D])
                rd = sb_in(ctx, "r_rd", [P, 2, NB])
                hm = sb_in(ctx, "r_hm", [P, 2, 2 * D])
                hmT = sb_in(ctx, "r_hmT", [P, 2, P])
                rz = sb_in(ctx, "r_rz", [P, 2, 2 * D])
                t1 = sb_in(ctx, "r_t1", [P, 2, D])
                n = sb_in(ctx, "r_n", [P, 2, D])
                d = sb_in(ctx, "r_d", [P, D])
                ps_t = ps_in(ctx, "r_ps_t", [P, 2, 512])
                ps_w = ps_in(ctx, "r_ps_w", [P, 2, 512])
                (s_w, s_v, s_cp, s_t, s_hmT, s_mm, s_rz, s_t1, s_pre, s_n, s_d1, s_d2, s_d3, s_d4, s_d5, s_x) = (sem_in(ctx, "r_" + q) for q in (
                    "weights", "steps", "inputs_copied", "turned", "turned_copied", "gates_in", "gates", "reset_applied", "candidate_in",
                    "candidate", "msg_less_n", "scaled", "new_h", "less_h", "selected", "block_done"))
                msg = ACC[:, 0:NB, 0:D]
                with nc.Block() as block:
                    @block.sync
                    def _(sp):
                        sp.dma_start(w[:], wgru).then_inc(s_w, 16)
                        sp.dma_start(bias[:], bgru).then_inc(s_w, 16)
                        sp.wait_ge(s_w, 32)

                    @block.vector
                    def _(dve):
                        do = chain(dve, s_v)
                        den = ACC[:, 0:NB, D]
                        do(dve.tensor_scalar(rd[:, 1], den, 0.0, None, ALU.is_gt))
                        do(dve.tensor_scalar(rd[:, 0], rd[:, 1], -1.0, 1.0, ALU.mult, ALU.add))
                        do(dve.tensor_tensor(rd[:, 0], rd[:, 0], den, ALU.add))
                        do(dve.reciprocal(rd[:, 0], rd[:, 0]))
                        do(dve.tensor_tensor(msg, msg, bcast(rd[:, 0], 2, D), ALU.mult))

                        def at(big, b):
                            return big[:, bass.ds(b, 1), :].rearrange("p a d -> p (a d)")

                        def body(b, k, r):
                            m_b = ACC[:, bass.ds(b, 1), 0:D].rearrange("p a d -> p (a d)")
                            at_least(dve, s_t, b - 1)
                            at_least(dve, s_x, b - 1)
                            dve.tensor_copy(hm[:, k, 0:D], at(H, b)).then_inc(s_cp, 1)
                            dve.tensor_copy(hm[:, k, D:2 * D], m_b).then_inc(s_cp, 1)
                            dve.wait_ge(s_rz, b + 1)
                            dve.tensor_tensor(t1[:, k], rz[:, k, 0:D], ps_w[:, k, 3 * D:4 * D], ALU.mult).then_inc(s_t1, 1)
                            dve.wait_ge(s_t1, b + 1)
                            dve.tensor_tensor(t1[:, k], t1[:, k], ps_w[:, k, 2 * D:3 * D], ALU.add).then_inc(s_pre, 1)
                            dve.wait_ge(s_n, b + 1)
                            at_least(dve, s_x, b)
                            dve.tensor_tensor(d[:], hm[:, k, D:2 * D], n[:, k], ALU.subtract).then_inc(s_d1, 1)
                            dve.wait_ge(s_d1, b + 1)
                            dve.tensor_tensor(d[:], d[:], rz[:, k, D:2 * D], ALU.mult).then_inc(s_d2, 1)
                            dve.wait_ge(s_d2, b + 1)
                            dve.tensor_tensor(d[:], d[:], n[:, k], ALU.add).then_inc(s_d3, 1)
                            dve.wait_ge(s_d3, b + 1)
                            dve.tensor_tensor(d[:], d[:], hm[:, k, 0:D], ALU.subtract).then_inc(s_d4, 1)
                            dve.wait_ge(s_d4, b + 1)
                            dve.scalar_tensor_tensor(d[:], d[:], rd[:, 1, bass.ds(b, 1)], hm[:, k, 0:D], ALU.mult, ALU.add).then_inc(s_d5, 1)
                            dve.wait_ge(s_d5, b + 1)
                            dve.tensor_tensor(at(X, b), at(X, b), d[:], ALU.add).then_inc(s_x, 1)
                        steps(dve, NB, body, 2)

                    @block.tensor
                    def _(pe):
                        pe.wait_ge(s_w, 32)

                        def body(b, k, r):
                            pe.wait_ge(s_cp, b * 2 + 2)
                            at_least(pe, s_hmT, b - 1)
                            pe.transpose(ps_t[:, k, 0:P], hm[:, k, :], ident[:]).then_inc(s_t, 1)
                            pe.wait_ge(s_hmT, b + 1)
                            at_least(pe, s_pre, b - 1)
                            pe.matmul(ps_w[:, k, 0:4 * D], hmT[:, k], w[:], start=True, stop=False)
                            pe.matmul(ps_w[:, k, 0:4 * D], ones[0:2, :], bias[:], start=False, stop=True).then_inc(s_mm, 1)
                        steps(pe, NB, body, 2)

                    @block.scalar
                    def _(act):
                        def body(b, k, r):
                            act.wait_ge(s_t, b + 1)
                            at_least(act, s_mm, b - 1)
                            act.copy(hmT[:, k], ps_t[:, k, 0:P]).then_inc(s_hmT, 1)
                            act.wait_ge(s_mm, b + 1)
                            at_least(act, s_x, b - 1)
                            act.activation(rz[:, k], ps_w[:, k, 0:2 * D], ACT.Sigmoid).then_inc(s_rz, 1)
                            act.wait_ge(s_pre, b + 1)
                            act.activation(n[:, k], t1[:, k], ACT.Tanh).then_inc(s_n, 1)
                        steps(act, NB, body, 2)

        def finish_gine():
            DD = 2 * D
            with phase() as ctx:
                wa = sb_in(ctx, "f_w1", [D + 1, DD])
                wb = sb_in(ctx, "f_w3", [DD, D])
                e1 = sb_in(ctx, "f_e1", [P, 1])
                epsc = sb_in(ctx, "f_eps", [P, 1])
                hb = sb_in(ctx, "f_hb", [P, 2, DD])
                hT = sb_in(ctx, "f_hT", [D + 1, 2, P])
                yT = sb_in(ctx, "f_yT", [DD, 2, P])
                st = sb_in(ctx, "f_st", [P, 2, NB])
                ps_t = ps_in(ctx, "f_ps_t", [P, 2, 512])
                ps_w = ps_in(ctx, "f_ps_w", [P, 2, 512])
                Y = PT[:, 0:NB, 0:DD]
                (s_w, s_v, s_hb, s_t, s_hT, s_mm, s_y, s_var, s_std, s_yb, s_yt, s_yT, s_m2, s_x, s_out) = (sem_in(ctx, "f_" + q) for q in (
                    "weights", "steps", "block_copied", "block_turned", "turned_copied", "hidden", "hidden_kept", "var_ready", "std_ready",
                    "hidden_copied", "hidden_turned", "hidden_turned_copied", "outputs", "block_done", "stored"))
                with nc.Block() as block:
                    @block.sync
                    def _(sp):
                        sp.dma_start(wa[:], w1).then_inc(s_w, 16)
                        sp.dma_start(wb[:], w3).then_inc(s_w, 16)
                        sp.wait_ge(s_x, NB + 1)
                        sp.dma_start(out[0:P * (NBLK - 1), :].rearrange("(b p) d -> p b d", p=P), X[:, 0:NBLK - 1, :]).then_inc(s_out, 16)
                        sp.dma_start(out[P * (NBLK - 1):N, :], X[0:last_rows, NBLK - 1, :]).then_inc(s_out, 16)
                        sp.wait_ge(s_out, 32)

                    @block.vector
                    def _(dve):
                        do = chain(dve, s_v)
                        do(dve.memset(epsc[:], 1e-5))
                        do(dve.memset(hT[D:D + 1, :, :], 1.0))
                        do(dve.tensor_scalar(e1[:], rows[:, ROWS["eps"]], 1.0, None, ALU.add))
                        do(dve.scalar_tensor_tensor(H[:], H[:], e1[:], ACC[:, 0:NB, 0:D], ALU.mult, ALU.add))

                        def hidden(b, k, r):
                            at_least(dve, s_t, b - 1)
                            dve.tensor_copy(hb[:, k, 0:D], H[:, bass.ds(b, 1), :].rearrange("p a d -> p (a d)")).then_inc(s_hb, 1)
                            dve.wait_ge(s_mm, b + 1)
                            settle(dve)
                            dve.tensor_copy(PT[:, bass.ds(b, 1), 0:DD].rearrange("p a d -> p (a d)"), ps_w[:, k, 0:DD]).then_inc(s_y, 1)
                        steps(dve, NB, hidden, 2)
                        dve.wait_ge(s_y, NB)
                        sq = PT[:, 0:NB, 0:DD]
                        do(dve.tensor_reduce(st[:, 0], Y, AX.X, ALU.add))
                        do(dve.tensor_scalar(st[:, 0], st[:, 0], 1.0 / DD, None, ALU.mult))
                        do(dve.tensor_tensor(Y, Y, bcast(st[:, 0], 2, DD), ALU.subtract))
                        do(dve.tensor_tensor(H[:], PT[:, 0:NB, 0:D], PT[:, 0:NB, 0:D], ALU.mult))
                        do(dve.tensor_tensor(ACC[:, 0:NB, 0:D], PT[:, 0:NB, D:DD], PT[:, 0:NB, D:DD], ALU.mult))
                        do(dve.tensor_tensor(H[:], H[:], ACC[:, 0:NB, 0:D], ALU.add))
                        dve.tensor_reduce(st[:, 0], H[:], AX.X, ALU.add).then_inc(s_var, 1)
                        dve.wait_ge(s_std, 1)
                        do(dve.reciprocal(st[:, 1], st[:, 1]))
                        do(dve.tensor_tensor(Y, Y, bcast(st[:, 1], 2, DD), ALU.mult))
                        do(dve.tensor_tensor(Y, Y, bcast(rows[:, ROWS["ln_g"]], 1, NB), ALU.mult))
                        do(dve.tensor_tensor(Y, Y, bcast(rows[:, ROWS["ln_b"]], 1, NB), ALU.add))
                        do(dve.tensor_scalar(Y, Y, 0.0, None, ALU.max))

                        def outputs(b, k, r):
                            at_least(dve, s_yt, b - 1)
                            dve.tensor_copy(hb[:, k, :], PT[:, bass.ds(b, 1), 0:DD].rearrange("p a d -> p (a d)")).then_inc(s_yb, 1)
                            dve.wait_ge(s_m2, b + 1)
                            xb = X[:, bass.ds(b, 1), :].rearrange("p a d -> p (a d)")
                            dve.tensor_tensor(xb, xb, ps_w[:, k, 0:D], ALU.add).then_inc(s_x, 1)
                        steps(dve, NB, outputs, 2)
                        dve.wait_ge(s_x, NB)
                        dve.tensor_tensor(X[:], X[:], bcast(rows[:, ROWS["b2_l3"]], 1, NB), ALU.add).then_inc(s_x, 1)

                    @block.tensor
                    def _(pe):
                        pe.wait_ge(s_w, 32)

                        def hidden(b, k, r):
                            pe.wait_ge(s_hb, b + 1)
                            at_least(pe, s_hT, b - 1)
                            settle(pe)
                            pe.transpose(ps_t[0:D, k, 0:P], hb[:, k, 0:D], ident[:]).then_inc(s_t, 1)
                            pe.wait_ge(s_hT, b + 1)
                            at_least(pe, s_y, b - 1)
                            pe.matmul(ps_w[:, k, 0:DD], hT[:, k], wa[:], start=True, stop=True).then_inc(s_mm, 1)
                        steps(pe, NB, hidden, 2)
                        pe.wait_ge(s_y, NB)

                        def outputs(b, k, r):
                            pe.wait_ge(s_yb, b + 1)
                            at_least(pe, s_yT, b - 1)
                            pe.transpose(ps_t[:, k, 0:P], hb[:, k, :], ident[:]).then_inc(s_yt, 1)
                            pe.wait_ge(s_yT, b + 1)
                            at_least(pe, s_x, b - 1)
                            pe.matmul(ps_w[:, k, 0:D], yT[:, k], wb[:], start=True, stop=True).then_inc(s_m2, 1)
                        steps(pe, NB, outputs, 2)

                    @block.scalar
                    def _(act):
                        act.wait_ge(s_v, 2)

                        def hidden(b, k, r):
                            act.wait_ge(s_t, b + 1)
                            at_least(act, s_mm, b - 1)
                            act.copy(hT[0:D, k], ps_t[0:D, k, 0:P]).then_inc(s_hT, 1)
                        steps(act, NB, hidden, 2)
                        act.wait_ge(s_var, 1)
                        act.activation(st[:, 1], st[:, 0], ACT.Sqrt, bias=epsc[:], scale=1.0 / DD).then_inc(s_std, 1)

                        def outputs(b, k, r):
                            act.wait_ge(s_yt, b + 1)
                            at_least(act, s_m2, b - 1)
                            act.copy(yT[:, k], ps_t[:, k, 0:P]).then_inc(s_yT, 1)
                        steps(act, NB, outputs, 2)

        def store_rows(table):
            with phase() as ctx:
                s_o = sem_in(ctx, "h_stored")
                with nc.Block() as block:
                    @block.sync
                    def _(sp):
                        sp.dma_start(table.rearrange("(b p) d -> p b d", p=P), H[:]).then_inc(s_o, 16)
                        sp.wait_ge(s_o, 16)

        def store_early():
            with phase() as ctx:
                s_o = sem_in(ctx, "x_stored")
                with nc.Block() as block:
                    @block.sync
                    def _(sp):
                        sp.dma_start(out[0:P * (NBLK - 1), :].rearrange("(b p) d -> p b d", p=P), X[:, 0:NBLK - 1, :]).then_inc(s_o, 16)
                        sp.dma_start(out[P * (NBLK - 1):N, :], X[0:last_rows, NBLK - 1, :]).then_inc(s_o, 16)
                        sp.wait_ge(s_o, 32)

        layer_input(0)
        node_tables(0, wtab0, 2 * D, D, tab0)
        attention(0, 0, tab0, HEADS, D, w_e, D)
        if STOP == 2:
            return dict(ACC=ACC)
        finish_gat()
        if STOP == 3:
            return store_early()
        layer_input(1)
        node_tables(1, wtab1, 2 * D, D, tab1, fold=True)
        segment_max()
        finish_max()
        if STOP == 4:
            return store_early()
        layer_input(2)
        node_tables(2, wtab2, 2 * ATT + D, ATT + D, tab2)
        attention(2, 1, tab2, 1, ATT, watt_e, D)
        finish_gru()
        if STOP == 5:
            return store_early()
        layer_input(3)
        store_rows(tab3)
        segment_sum()
        finish_gine()


def laid_out(i):
    def f(name):
        return np.asarray(i[name])

    def zeros(*shape):
        return np.zeros(shape, np.float32)

    w1, att, hh = f("L1_gnn_W1"), f("L2_gnn_W_att1").T, f("L2_gnn_W_hh").T
    b_hh = f("L2_gnn_b_hh")
    return {
        "x": f("x"), "src": f("src"), "dst": f("dst"), "ea16": f("edge_attr_16"), "ea64": f("edge_attr_64"),
        "rowvec": np.concatenate([
            f("L0_gnn_att").reshape(-1), f("L0_gnn_bias"), f("L0_gnn_gamma"), f("L0_gnn_beta"), f("L1_gnn_b2"),
            f("L2_gnn_W_att2").reshape(-1), f("L2_gnn_b_att2"), f("L3_gnn_ln_g"), f("L3_gnn_ln_b"), f("L3_gnn_b2"),
            f("L3_gnn_eps")]),
        "wtab0": np.block([[f("L0_gnn_W_l"), f("L0_gnn_W_r")], [f("L0_gnn_b_l")[None], f("L0_gnn_b_r")[None]]]),
        "w_e": f("L0_gnn_W_e"),
        "wtab1": np.block([[w1[D:], w1[:D]], [zeros(1, D), f("L1_gnn_b1")[None]]]),
        "w2": f("L1_gnn_W2"),
        "wtab2": np.block([[att[D + DE:], f("L2_gnn_W_lin").T, att[:D]],
                           [zeros(1, ATT), f("L2_gnn_b_lin")[None], f("L2_gnn_b_att1")[None]]]),
        "watt_e": att[D:D + DE],
        "wgru": np.block([[f("L2_gnn_W_ih").T, zeros(D, D)], [hh[:, :2 * D], zeros(D, D), hh[:, 2 * D:]]]),
        "bgru": np.stack([np.concatenate([f("L2_gnn_b_ih"), zeros(D)]),
                          np.concatenate([b_hh[:2 * D], zeros(D), b_hh[2 * D:]])]),
        "w1": np.concatenate([f("L3_gnn_W1"), f("L3_gnn_b1")[None]]),
        "w3": f("L3_gnn_W2"),
    }


def kernel(**inputs):
    import concourse.bacc as bacc
    from concourse.bass_utils import run_bass_kernel_spmd as run

    nc = bacc.Bacc("TRN2", target_bir_lowering=False, num_devices=1)
    arrays, args = {}, {}
    for name, a in laid_out(inputs).items():
        a = np.ascontiguousarray(a)
        arrays[f"in_{name}"] = a
        args[name] = nc.dram_tensor(f"in_{name}", a.shape, mybir.dt.from_np(a.dtype), kind="ExternalInput").ap()
    shape = inputs["x"].shape
    out = nc.dram_tensor("out_x", shape, F32, kind="ExternalOutput").ap()
    program(nc, **args, out=out)
    r = run(nc, [arrays], core_ids=[0])
    return r.results[0]["out_x"]
```

```python
from contextlib import ExitStack, contextmanager

import numpy as np
import concourse.bass as bass
from concourse import mybir

F32 = mybir.dt.float32
BF16 = mybir.dt.bfloat16
I32 = mybir.dt.int32
ALU = mybir.AluOpType
ACT = mybir.ActivationFunctionType
AX = mybir.AxisListType

STOP = 0
P = 128
D = 64
DE = 16
T = 4
GE = T * P
SLOTS = 4
ATT = 2 * D + DE
REC = 82
EA16, EA64 = 2, 2 + DE
BIG = 1.0e30
PAD = 2 * GE
FAR = 1 << 20
SORT_T = 5
HEADS = 4


def at_least(eng, sem, value):
    if not isinstance(value, int) or value > 0:
        eng.wait_ge(sem, value)


def steps(eng, n, body, unroll=SLOTS, end=0):
    rounds = n // unroll
    assert n % unroll == 0 and rounds > 1 + end
    for k in range(unroll):
        body(k, k, 0)
    with eng.Fori(1, rounds - end) as r:
        for k in range(unroll):
            body(r * unroll + k, k, r)
    for r in range(rounds - end, rounds):
        for k in range(unroll):
            body(r * unroll + k, k, r)


def before(g, k, r, by=1):
    return (g - by, (k - by) % SLOTS, r if k >= by else r - 1)


def after(g, k, r):
    return (g + 1, (k + 1) % SLOTS, r if k < SLOTS - 1 else r + 1)


def is_group(g, n):
    return isinstance(g, int) and g == n


def settle(eng):
    eng.nop(nofuse=True)


def bcast(ap, axis, n):
    a = ap.unsqueeze(axis)
    shape = list(a.shape)
    shape[axis] = n
    return a.broadcast_to(shape)


ROWS = {}
for _name, _n in (("att", D), ("bias", D), ("gamma", D), ("beta", D), ("b2_l1", D), ("w_att2", ATT), ("b_att2", 1),
                  ("ln_g", 2 * D), ("ln_b", 2 * D), ("b2_l3", D), ("eps", 1)):
    ROWS[_name] = slice(ROWS["_end"] if ROWS else 0, (ROWS["_end"] if ROWS else 0) + _n)
    ROWS["_end"] = ROWS[_name].stop


def program(nc, x, src, dst, ea16, ea64, rowvec, wtab0, w_e, wtab1, w2, wtab2, watt_e, wgru, bgru, w1, w3, out):
    N, E = x.shape[0], src.shape[0]
    NBLK = -(-N // P)
    NB = NBLK + NBLK % 2
    assert E % (P * SORT_T) == 0 and NB < P and D == x.shape[1]
    NG = (E + NBLK * (GE - 1)) // GE
    NG = -(-NG // SLOTS) * SLOTS
    EPP = E // P
    last_rows = N - P * (NBLK - 1)

    with ExitStack() as top:
        def dram(name, shape, dt=F32):
            return nc.dram_tensor(name, shape, dt).ap()

        def sb_in(ctx, name, shape, dt=F32):
            return ctx.enter_context(nc.sbuf_tensor(name, shape, dt))

        def ps_in(ctx, name, shape, dt=F32):
            return ctx.enter_context(nc.psum_tensor(name, shape, dt))

        held = []

        def sem_in(ctx, name):
            held.append(nc.alloc_semaphore(name))
            return held[-1]

        @contextmanager
        def phase():
            with ExitStack() as ctx:
                yield ctx
            nc.clear_and_free_semaphores(held)
            held.clear()
            nc.all_engine_barrier()

        def sb(name, shape, dt=F32):
            return sb_in(top, name, shape, dt)

        keyp = dram("keyp", (1 + E + PAD,), I32)
        srcp = dram("srcp", (E + PAD,), I32)
        eap = dram("eap", (E + PAD, DE))
        rec = dram("rec", (NG * GE, REC), I32)
        tab0 = dram("tab0", (NB * P, D))
        tab1 = dram("tab1", (NB * P, D))
        tab2 = dram("tab2", (NB * P, ATT + D))
        tab3 = dram("tab3", (NB * P, D))

        ident = sb("ident", [P, P])
        iota_n = sb("iota_n", [P, P])
        ones = sb("ones", [P, P])
        identb = sb("identb", [P, P], BF16)
        iota_b = sb("iota_b", [P, P], BF16)
        X = sb("X", [P, NB, D])
        H = sb("H", [P, NB, D])
        blk = sb("blk", [P, 2, NG], I32)
        base_node = sb("base_node", [P, 2, NG])
        goff = sb("goff", [P, NG], I32)
        rows = sb("rows", [P, ROWS["_end"]])

        with phase() as ctx:
            ii = sb_in(ctx, "ii", [P, P], I32)
            z16 = sb_in(ctx, "z16", [P, PAD * DE // P])
            fk = sb_in(ctx, "fk", [P, 16], I32)
            rinit = sb_in(ctx, "rinit", [P, 80, REC], I32)
            s_id, s_x, s_fill, s_dma, s_ones, s_cast = (sem_in(ctx, n) for n in (
                "ident_zero", "x_zero", "pads_filled", "setup_dma", "ones_set", "iota_done"))
            block = ctx.enter_context(nc.Block())

            @block.gpsimd
            def _(pool):
                pool.memset(ident[:], 0.0).then_inc(s_id, 1)
                pool.wait_ge(s_id, 1)
                pool.affine_select(out=ident[:], in_=ident[:], compare_op=ALU.not_equal, fill=1.0, base=0,
                                   pattern=[[-1, P]], channel_multiplier=1).then_inc(s_id, 1)
                pool.iota(ii[:], [[1, P]], base=0, channel_multiplier=0).then_inc(s_id, 1)

            @block.vector
            def _(dve):
                dve.memset(X[:], 0.0).then_inc(s_x, 1)
                dve.memset(z16[:], 0.0).then_inc(s_fill, 1)
                dve.memset(fk[:, 0:8], FAR).then_inc(s_fill, 1)
                dve.memset(fk[:, 8:16], 0).then_inc(s_fill, 1)
                dve.memset(rinit[:], 0).then_inc(s_fill, 1)
                dve.wait_ge(s_fill, 4)
                dve.memset(rinit[:, :, 0:1], -1).then_inc(s_fill, 1)
                dve.memset(ones[:], 1.0).then_inc(s_ones, 1)
                dve.wait_ge(s_id, 3)
                dve.tensor_copy(iota_n[:], ii[:]).then_inc(s_cast, 1)
                dve.tensor_copy(iota_b[:], ii[:]).then_inc(s_cast, 1)
                dve.tensor_copy(identb[:], ident[:]).then_inc(s_cast, 1)

            @block.sync
            def _(sp):
                sp.dma_start(rows[:], rowvec.partition_broadcast(P)).then_inc(s_dma, 16)
                sp.wait_ge(s_x, 1)
                sp.dma_start(X[:, 0:NBLK - 1, :], x[0:P * (NBLK - 1), :].rearrange("(b p) d -> p b d", p=P)).then_inc(s_dma, 16)
                sp.dma_start(X[0:last_rows, NBLK - 1, :], x[P * (NBLK - 1):N, :]).then_inc(s_dma, 16)
                sp.dma_start(keyp[1:1 + E].rearrange("(a b) -> a b", a=16), dst.rearrange("(a b) -> a b", a=16)).then_inc(s_dma, 16)
                sp.dma_start(srcp[0:E].rearrange("(a b) -> a b", a=16), src.rearrange("(a b) -> a b", a=16)).then_inc(s_dma, 16)
                sp.dma_start(eap[0:E, :].rearrange("(a b) d -> a (b d)", a=64), ea16.rearrange("(a b) d -> a (b d)", a=64)).then_inc(s_dma, 16)
                sp.wait_ge(s_fill, 5)
                sp.dma_start(keyp[1 + E:1 + E + PAD].rearrange("(p c) -> p c", p=P), fk[:, 0:8]).then_inc(s_dma, 16)
                sp.dma_start(keyp[0:1].rearrange("(p c) -> p c", p=1), rinit[0:1, 0, 0:1]).then_inc(s_dma, 16)
                sp.dma_start(srcp[E:E + PAD].rearrange("(p c) -> p c", p=P), fk[:, 8:16]).then_inc(s_dma, 16)
                sp.dma_start(eap[E:E + PAD, :].rearrange("(p c) d -> p (c d)", p=P), z16[:]).then_inc(s_dma, 16)
                places = NG * T
                rv = rec.rearrange("(p r) c -> p r c", p=P)
                n = 10
                for r in range(0, places, 80):
                    m = min(80, places - r)
                    sp.dma_start(rv[:, r:r + m, :], rinit[:, 0:m, :]).then_inc(s_dma, 16)
                    n += 1
                sp.wait_ge(s_dma, 16 * n)

        with phase() as ctx:
            keys = [sb_in(ctx, f"keys{o}", [P, EPP], I32) for o in range(2)]
            ki = sb_in(ctx, "ki", [P, EPP], I32)
            hi = [sb_in(ctx, f"hi{o}", [P, EPP]) for o in range(2)]
            junk = sb_in(ctx, "junk", [P, EPP], BF16)
            cnt = sb_in(ctx, "cnt", [P, 2, P])
            small = [sb_in(ctx, f"small{o}", [P, 6, P]) for o in range(2)]
            gi = sb_in(ctx, "gi", [P, 2, P], I32)
            cols = sb_in(ctx, "cols", [P, 2, 2])
            jd = sb_in(ctx, "jd", [P, P])
            giota_i = sb_in(ctx, "giota_i", [P, NG], I32)
            giota = sb_in(ctx, "giota", [P, NG])
            past = sb_in(ctx, "past", [P, 2, NG])
            fo = sb_in(ctx, "fo", [P, NG])
            base = sb_in(ctx, "base", [P, P])
            ps_c = ps_in(ctx, "ps_c", [P, 2, P])
            ps_g = ps_in(ctx, "ps_g", [P, 2, 512])
            s_k, s_gi, s_hi, s_cnt, s_ct, s_sm, s_past, s_psg, s_tab = (sem_in(ctx, n) for n in (
                "keys_landed", "group_iota", "hi_steps", "counted", "counts_summed", "table_steps", "past_ready",
                "group_sums", "group_sums_read"))
            NSL = -(-NG // 512)
            with nc.Block() as block:
                @block.sync
                def _(sp):
                    sp.dma_start(keys[0][:], dst.rearrange("(p c) -> p c", p=P)).then_inc(s_k, 16)
                    sp.dma_start(keys[1][:], src.rearrange("(p c) -> p c", p=P)).then_inc(s_k, 16)

                @block.gpsimd
                def _(pool):
                    pool.iota(giota_i[:], [[1, NG]], base=0, channel_multiplier=0).then_inc(s_gi, 1)

                @block.vector
                def _(dve):
                    nh = 0
                    dve.wait_ge(s_gi, 1)
                    dve.tensor_copy(giota[:], giota_i[:]).then_inc(s_hi, 1)
                    dve.memset(cnt[:], 0.0).then_inc(s_hi, 1)
                    dve.wait_ge(s_k, 32)
                    nh = 2
                    for o in range(2):
                        dve.wait_ge(s_hi, nh)
                        dve.tensor_scalar(ki[:], keys[o][:], 7, None, ALU.arith_shift_right).then_inc(s_hi, 1)
                        dve.wait_ge(s_hi, nh + 1)
                        dve.tensor_copy(hi[o][:], ki[:]).then_inc(s_hi, 1)
                        nh += 2
                    dve.wait_ge(s_hi, nh)
                    for o in range(2):
                        def count(b):
                            dve.tensor_scalar(junk[:], hi[o][:], iota_n[:, bass.ds(b, 1)], None, ALU.is_equal, ALU.add,
                                              accum_out=cnt[:, o, bass.ds(b, 1)]).then_inc(s_cnt, 1)

                        at_least(dve, s_cnt, o * NBLK)
                        count(0)
                        with dve.Fori(1, NBLK) as b:
                            dve.wait_ge(s_cnt, b + o * NBLK)
                            count(b)
                    ns = 0
                    dve.wait_ge(s_ct, 1)

                    def do(ins):
                        nonlocal ns
                        ns += 1
                        ins.then_inc(s_sm, 1)
                        dve.wait_ge(s_sm, ns)

                    for o in range(2):
                        c, gf, gend, pad, padsum, at = (small[o][:, k, :] for k in range(6))
                        do(dve.tensor_copy(c, ps_c[:, o, :]))
                        do(dve.tensor_scalar(gf, c, float(GE - 1), None, ALU.add))
                        do(dve.tensor_copy(gi[:, o, :], gf))
                        do(dve.tensor_scalar(gi[:, o, :], gi[:, o, :], 9, None, ALU.arith_shift_right))
                        do(dve.tensor_copy(gf, gi[:, o, :]))
                        do(dve.tensor_tensor_scan(gend, gf, gf, 0.0, ALU.add, ALU.bypass))
                        do(dve.scalar_tensor_tensor(pad, gf, float(GE), c, ALU.mult, ALU.subtract))
                        do(dve.tensor_tensor(at, gend, gf, ALU.subtract))
                        do(dve.tensor_scalar(at, at, float(GE), None, ALU.mult))
                        do(dve.tensor_tensor_reduce(jd[:], gend, ident[:], 1.0, 0.0, ALU.mult, ALU.add, cols[:, o, 0:1]))
                        do(dve.tensor_tensor_reduce(jd[:], pad, ident[:], 1.0, 0.0, ALU.mult, ALU.add, cols[:, o, 1:2]))
                        do(dve.tensor_scalar(past[:, o, :], giota[:], cols[:, o, 0:1], None, ALU.is_ge))
                    do(dve.tensor_copy(base[:], small[1][:, 5, :]))
                    dve.memset(jd[:], 1.0).then_inc(s_past, 1)
                    nt = 0
                    for o in range(2):
                        for c in range(NSL):
                            a, b = 512 * c, min(NG, 512 * c + 512)
                            nt += 1
                            dve.wait_ge(s_psg, nt)
                            do(dve.tensor_scalar(base_node[:, o, a:b], ps_g[:, nt % 2, 0:b - a], float(NB), None, ALU.min))
                            do(dve.tensor_copy(blk[:, o, a:b], base_node[:, o, a:b]))
                            dve.tensor_scalar(base_node[:, o, a:b], base_node[:, o, a:b], float(P), None, ALU.mult).then_inc(s_tab, 1)
                    for c in range(NSL):
                        a, b = 512 * c, min(NG, 512 * c + 512)
                        nt += 1
                        dve.wait_ge(s_psg, nt)
                        do(dve.scalar_tensor_tensor(fo[:, a:b], giota[:, a:b], float(GE), ps_g[:, nt % 2, 0:b - a], ALU.mult, ALU.subtract))
                        do(dve.tensor_scalar(fo[:, a:b], fo[:, a:b], float(E), None, ALU.min))
                        dve.tensor_copy(goff[:, a:b], fo[:, a:b]).then_inc(s_tab, 1)

                @block.tensor
                def _(pe):
                    pe.wait_ge(s_cnt, 2 * NBLK)
                    pe.matmul(ps_c[:].rearrange("p o b -> p (o b)"), ones[:], cnt[:].rearrange("p o b -> p (o b)"), start=True, stop=True).then_inc(s_ct, 1)
                    pe.wait_ge(s_past, 1)
                    nt = 0
                    for o, w in ((0, None), (1, None), (0, 1)):
                        for c in range(NSL):
                            a, b = 512 * c, min(NG, 512 * c + 512)
                            nt += 1
                            at_least(pe, s_tab, nt - 2)
                            lhs = ones[:] if w is None else cols[:, 0, 1:2].broadcast_to([P, P])
                            pe.matmul(ps_g[:, nt % 2, 0:b - a], lhs, past[:, o, a:b], start=True, stop=True).then_inc(s_psg, 1)

            tri = sb_in(ctx, "tri", [P, P], BF16)
            oneb = sb_in(ctx, "oneb", [P, P], BF16)
            oh = sb_in(ctx, "s_oh", [P, 2, SORT_T, NB], BF16)
            tmp = sb_in(ctx, "s_tmp", [P, SORT_T, NB])
            posf = sb_in(ctx, "posf", [P, SORT_T])
            SS = 5
            posi = sb_in(ctx, "posi", [P, SS, SORT_T], I32)
            rb = sb_in(ctx, "rb", [P, SS, SORT_T, REC])
            ps_r = ps_in(ctx, "ps_r", [P, 2, 512])
            ps_s = ps_in(ctx, "ps_s", [P, 2, 512])
            NSTEP = EPP // SORT_T
            s_tri = sem_in(ctx, "tri_ready")
            s_ld = [sem_in(ctx, f"features_landed{k}") for k in range(SS)]
            s_sc = [sem_in(ctx, f"scattered{k}") for k in range(SS)]
            s_oh, s_r, s_add, s_mul, s_red, s_pos, s_base, s_key = (sem_in(ctx, n) for n in (
                "sort_onehot", "sort_ranks", "sort_added", "sort_masked", "sort_reduced", "places_ready", "base_moved", "keys_in_record"))
            ea16v = ea16.rearrange("(p c) d -> p c d", p=P)
            ea64v = ea64.rearrange("(p c) d -> p c d", p=P)
            rbi = rb[:].bitcast(I32)
            with nc.Block() as block:
                @block.sync
                def _(sp):
                    def body(g, k, r):
                        at_least(sp, s_sc[k], r * (16 * SORT_T))
                        settle(sp)
                        sp.dma_start(rb[:, k, :, EA16:EA16 + DE], ea16v[:, bass.ds(g * SORT_T, SORT_T), :]).then_inc(s_ld[k], 16)
                        sp.dma_start(rb[:, k, :, EA64:EA64 + D], ea64v[:, bass.ds(g * SORT_T, SORT_T), :]).then_inc(s_ld[k], 16)
                    steps(sp, NSTEP, body, SS)

                @block.gpsimd
                def _(pool):
                    pool.memset(oneb[:], 1.0).then_inc(s_tri, 1)
                    pool.wait_ge(s_tri, 1)
                    pool.affine_select(out=tri[:], in_=oneb[:], compare_op=ALU.is_gt, fill=0.0, base=0,
                                       pattern=[[1, P]], channel_multiplier=-1).then_inc(s_tri, 1)

                    def body(g, k, r):
                        pool.wait_ge(s_ld[k], r * 32 + 32)
                        pool.wait_ge(s_pos, g + 1)
                        settle(pool)
                        for t in range(SORT_T):
                            pool.indirect_dma_start(rec, bass.IndirectOffsetOnAxis(ap=posi[:, k, t:t + 1], axis=0),
                                                    rbi[:, k, t, :], None).then_inc(s_sc[k], 16)
                    steps(pool, NSTEP, body, SS)
                    for k in range(SS):
                        pool.wait_ge(s_sc[k], 16 * SORT_T * (NSTEP // SS))

                @block.vector
                def _(dve):
                    def body(g, k, r):
                        q = k % 2 if isinstance(g, int) else k % 2
                        cols_g = bass.ds(g * SORT_T, SORT_T)
                        at_least(dve, s_sc[k], r * (16 * SORT_T))
                        dve.tensor_copy(rbi[:, k, :, 0:1], bcast(keys[1][:, cols_g], 2, 1)).then_inc(s_key, 1)
                        dve.tensor_copy(rbi[:, k, :, 1:2], bcast(keys[0][:, cols_g], 2, 1)).then_inc(s_key, 1)
                        at_least(dve, s_r, g)
                        dve.tensor_tensor(oh[:, 0], bcast(iota_n[:, 0:NB], 1, SORT_T), bcast(hi[1][:, cols_g], 2, NB),
                                          ALU.is_equal).then_inc(s_oh, 1)
                        dve.wait_ge(s_r, g + 1)
                        at_least(dve, s_base, g)
                        dve.tensor_tensor(tmp[:], ps_r[:, 0, 0:SORT_T * NB].rearrange("p (t b) -> p t b", t=SORT_T),
                                          bcast(base[:, 0:NB], 1, SORT_T), ALU.add).then_inc(s_add, 1)
                        dve.wait_ge(s_add, g + 1)
                        dve.tensor_tensor(base[:, 0:NB], base[:, 0:NB], ps_s[:, 0, 0:NB], ALU.add).then_inc(s_base, 1)
                        dve.tensor_tensor(tmp[:], tmp[:], oh[:, 0], ALU.mult).then_inc(s_mul, 1)
                        dve.wait_ge(s_mul, g + 1)
                        dve.tensor_reduce(posf[:], tmp[:], AX.X, ALU.add).then_inc(s_red, 1)
                        dve.wait_ge(s_red, g + 1)
                        dve.wait_ge(s_key, g * 2 + 2)
                        dve.tensor_copy(posi[:, k, :], posf[:]).then_inc(s_pos, 1)
                    steps(dve, NSTEP, body, SS)

                @block.tensor
                def _(pe):
                    pe.wait_ge(s_tri, 2)

                    def body(g, k, r):
                        pe.wait_ge(s_oh, g + 1)
                        at_least(pe, s_base, g)
                        for t in range(SORT_T):
                            pe.matmul(ps_r[:, 0, t * NB:t * NB + NB], tri[:], oh[:, 0, t], start=True, stop=(t == 0))
                            for u in range(t):
                                pe.matmul(ps_r[:, 0, t * NB:t * NB + NB], oneb[:], oh[:, 0, u], start=False, stop=(u == t - 1))
                        for t in range(SORT_T):
                            mm = pe.matmul(ps_s[:, 0, 0:NB], oneb[:], oh[:, 0, t], start=(t == 0), stop=(t == SORT_T - 1))
                        mm.then_inc(s_r, 1)
                    steps(pe, NSTEP, body, SS)


        ACC = sb("ACC", [P, NB + 1, HEADS * (D // HEADS + 1)])
        PT = sb("PT", [P, NB + 1, ATT])

        def chain(eng, sem):
            n = 0

            def do(ins):
                nonlocal n
                n += 1
                ins.then_inc(sem, 1)
                eng.wait_ge(sem, n)
            return do

        def layer_input(layer):
            with phase() as ctx:
                st = sb_in(ctx, f"ln_stat{layer}", [P, 4, NB])
                epsc = sb_in(ctx, f"ln_eps{layer}", [P, 1])
                s_v, s_var, s_std = (sem_in(ctx, f"{n}{layer}") for n in ("ln_steps", "ln_var_ready", "ln_std_ready"))
                sq = PT[:, 0:NB, 0:D]
                with nc.Block() as block:
                    @block.vector
                    def _(dve):
                        do = chain(dve, s_v)
                        do(dve.memset(epsc[:], 1e-5))
                        do(dve.tensor_reduce(st[:, 0, :], X[:], AX.X, ALU.add))
                        do(dve.tensor_scalar(st[:, 0, :], st[:, 0, :], 1.0 / D, None, ALU.mult))
                        do(dve.tensor_tensor(H[:], X[:], bcast(st[:, 0, :], 2, D), ALU.subtract))
                        do(dve.tensor_tensor(sq, H[:], H[:], ALU.mult))
                        dve.tensor_reduce(st[:, 1, :], sq, AX.X, ALU.add).then_inc(s_var, 1)
                        do(dve.memset(ACC[:], 0.0))
                        dve.wait_ge(s_std, 1)
                        do(dve.reciprocal(st[:, 3, :], st[:, 2, :]))
                        do(dve.tensor_tensor(H[:], H[:], bcast(st[:, 3, :], 2, D), ALU.mult))
                        do(dve.tensor_scalar(H[:], H[:], 0.0, None, ALU.max))
                        do(dve.memset(PT[:], 0.0))

                    @block.scalar
                    def _(act):
                        act.wait_ge(s_var, 1)
                        act.activation(st[:, 2, :], st[:, 1, :], ACT.Sqrt, bias=epsc[:], scale=1.0 / D).then_inc(s_std, 1)

        def node_tables(layer, weights, width, n_gather, table, fold=False):
            n_pt = width - n_gather
            with phase() as ctx:
                w = sb_in(ctx, f"w_tab{layer}", [D + 1, width])
                hb = sb_in(ctx, f"hb{layer}", [P, 2, D])
                hT = sb_in(ctx, f"hT{layer}", [D + 1, 2, P])
                stage = sb_in(ctx, f"stage{layer}", [P, 2, n_gather])
                ps_t = ps_in(ctx, f"ps_t{layer}", [P, 2, 512])
                ps_w = ps_in(ctx, f"ps_w{layer}", [P, 2, 512])
                s_w, s_one, s_fold, s_hb, s_t, s_hT, s_mm, s_st, s_pt = (sem_in(ctx, f"{n}{layer}") for n in (
                    "weights_landed", "ones_row", "weights_folded", "block_copied", "block_turned", "turned_copied", "rows_ready", "rows_staged", "rows_kept"))
                s_out = [sem_in(ctx, f"rows_stored{layer}_{k}") for k in range(2)]
                with nc.Block() as block:
                    @block.sync
                    def _(sp):
                        sp.dma_start(w[:], weights).then_inc(s_w, 16)

                        def body(b, k, r):
                            sp.wait_ge(s_st, b + 1)
                            settle(sp)
                            sp.dma_start(table[bass.ds(b * P, P), :], stage[:, k, :]).then_inc(s_out[k], 16)
                        steps(sp, NB, body, 2)
                        for k in range(2):
                            sp.wait_ge(s_out[k], 16 * (NB // 2))

                    @block.vector
                    def _(dve):
                        dve.memset(hT[D:D + 1, :, :], 1.0).then_inc(s_one, 1)
                        if fold:
                            dve.wait_ge(s_w, 16)
                            dve.tensor_tensor(w[0:D, D:2 * D], w[0:D, D:2 * D], w[0:D, 0:D], ALU.subtract).then_inc(s_fold, 1)

                        def body(b, k, r):
                            at_least(dve, s_t, b - 1)
                            dve.tensor_copy(hb[:, k, :], H[:, bass.ds(b, 1), :].rearrange("p a d -> p (a d)")).then_inc(s_hb, 1)
                            dve.wait_ge(s_st, b + 1)
                            settle(dve)
                            dve.tensor_copy(PT[:, bass.ds(b, 1), 0:n_pt].rearrange("p a d -> p (a d)"),
                                            ps_w[:, k, n_gather:width]).then_inc(s_pt, 1)
                        steps(dve, NB, body, 2)

                    @block.tensor
                    def _(pe):
                        pe.wait_ge(s_one, 1)
                        pe.wait_ge(s_w, 16)
                        at_least(pe, s_fold, int(fold))

                        def body(b, k, r):
                            pe.wait_ge(s_hb, b + 1)
                            at_least(pe, s_hT, b - 1)
                            settle(pe)
                            pe.transpose(ps_t[0:D, k, 0:P], hb[:, k, :], ident[:]).then_inc(s_t, 1)
                            pe.wait_ge(s_hT, b + 1)
                            at_least(pe, s_st, b - 1)
                            at_least(pe, s_pt, b - 1)
                            pe.matmul(ps_w[:, k, 0:width], hT[:, k, :], w[:], start=True, stop=True).then_inc(s_mm, 1)
                        steps(pe, NB, body, 2)

                    @block.scalar
                    def _(act):
                        def body(b, k, r):
                            act.wait_ge(s_t, b + 1)
                            at_least(act, s_mm, b - 1)
                            act.copy(hT[0:D, k, :], ps_t[0:D, k, 0:P]).then_inc(s_hT, 1)
                            act.wait_ge(s_mm, b + 1)
                            at_least(act, s_out[k], r * 16)
                            act.copy(stage[:, k, :], ps_w[:, k, 0:n_gather]).then_inc(s_st, 1)
                        steps(act, NB, body, 2)

        def attention(layer, order, table, heads, width, we, n_val):
            R = table.shape[1]
            VC = n_val // heads + 1
            v0 = R - n_val
            banks = 1 if T * width <= 512 else 2
            tpb = T // banks
            att = rows[:, ROWS["att"]] if layer == 0 else rows[:, ROWS["w_att2"]]
            with phase() as ctx:
                def sbl(name, shape, dt=F32):
                    return sb_in(ctx, f"{name}{layer}", shape, dt)

                def seml(name):
                    return sem_in(ctx, f"{name}{layer}")

                w = sbl("w_ea", [T * DE, T, width])
                if layer == 0:
                    key = sbl("key", [P, SLOTS, T, 1], I32)
                    idx = sbl("idx", [P, SLOTS, T, 1], I32)
                    ea = sbl("ea", [P, SLOTS, T, DE])
                    n_loads = 3
                else:
                    rs = sbl("rs", [P, SLOTS, T, REC], I32)
                    key, idx = rs[:, :, :, 0:1], rs[:, :, :, 1:2]
                    ea_in = rs[:].bitcast(F32)[:, :, :, EA16:EA16 + DE]
                    ea = sbl("ea", [P, SLOTS, T, DE])
                    n_loads = 1
                G = sbl("G", [P, SLOTS, T, R])
                lo = sbl("lo", [P, T])
                ohb = sbl("ohb", [P, 2, T, P], BF16)
                oh = sbl("oh", [P, SLOTS, T, P])
                ohN = sbl("ohN", [P, 2, T, P])
                pen = sbl("pen", [P, 2, T, P])
                eaT = sbl("eaT", [T * DE, P])
                z = sbl("z", [P, T, width])
                zs = sbl("zs", [P, T, width]) if layer == 0 else None
                lg = sbl("lg", [P, 2, T, heads])
                lgp = sbl("lgp", [P, T, 2, heads], BF16)
                lgT = sbl("lgT", [2 * heads, T * P], BF16)
                sel = sbl("sel", [2 * heads, heads, P], BF16)
                junk = sbl("junk", [P, 2, T, P], BF16)
                gm = sbl("gm", [P, heads])
                mn = sbl("mn", [P, heads])
                df = sbl("df", [P, heads])
                corr = sbl("corr", [P, heads])
                dd = sbl("dd", [P, T, heads])
                ss = sbl("ss", [P, T, heads])
                V = sbl("V", [P, T, heads, VC])
                M = sbl("M", [P, NB + 1, heads])
                ps_oh = ps_in(ctx, f"ps_oh{layer}", [P, 2 * T, P], BF16)
                ps_ea = ps_in(ctx, f"ps_ea{layer}", [P, 512])
                ps_lT = ps_in(ctx, f"ps_lT{layer}", [P, 2 * T * P], BF16)
                ps_z = ps_in(ctx, f"ps_z{layer}", [P, banks, 512])
                n_lb = min(heads, 2)
                ps_lb = ps_in(ctx, f"ps_lb{layer}", [P, n_lb, T, P])
                ps_m = ps_in(ctx, f"ps_m{layer}", [P, 512])
                ps_a = ps_in(ctx, f"ps_a{layer}", [P, 512])
                zv = [ps_z[:, b, 0:tpb * width].rearrange("p (t c) -> p t c", t=tpb) for b in range(banks)]

                s_w, s_mi, s_eac = seml("ea_weights"), seml("maxima_set"), seml("ea_together")
                s_ld = [seml(f"edges_landed{k}_") for k in range(SLOTS)]
                s_g = [seml(f"gathered{k}_") for k in range(SLOTS)]
                (s_wz, s_lo, s_oh, s_oh32, s_ohT, s_ohN, s_pen, s_eaP, s_eaT, s_z, s_zs, s_act, s_mul, s_lg0, s_lg, s_lp0, s_lp, s_lT, s_lTc, s_sel, s_mn, s_df, s_mb, s_corr,
                 s_me, s_d0, s_d, s_p, s_V, s_acc, s_sc, s_done) = (seml(n) for n in (
                    "ea_weights_zero", "local_key", "onehot", "onehot_32", "onehot_turned", "onehot_nodes", "penalty", "ea_turned", "ea_ready", "edge_rows",
                    "slope_applied", "activated", "weighted", "score_sum", "score", "score_high", "score_low", "score_turned", "score_rows", "selector", "new_max", "max_step", "max_stored", "rescale",
                    "edge_max", "score_less_max", "exponent", "weight", "values", "group_sums", "acc_rescaled", "group_done"))
                s_lb = [seml(f"scores_spread{h}_") for h in range(heads)]
                s_gm = [seml(f"group_max{h}_") for h in range(heads)]

                with nc.Block() as block:
                    @block.sync
                    def _(sp):
                        sp.wait_ge(s_wz, 1)
                        for t in range(T):
                            sp.dma_start(w[t * DE:(t + 1) * DE, t, :], we).then_inc(s_w, 16)

                        def body(g, k, r):
                            at_least(sp, s_lo, g - SLOTS + 1)
                            settle(sp)
                            at_least(sp, s_g[k], r * (16 * T))
                            at_least(sp, s_eac if layer else s_eaP, g - SLOTS + 1)
                            settle(sp)
                            if layer == 0:
                                e = sp.value_load(goff[0:1, bass.ds(g, 1)], min_val=0, max_val=E)
                                sp.dma_start(key[:, k, :, 0], keyp[bass.ds(e + 1, GE)].rearrange("(p t) -> p t", p=P)).then_inc(s_ld[k], 16)
                                sp.dma_start(idx[:, k, :, 0], srcp[bass.ds(e, GE)].rearrange("(p t) -> p t", p=P)).then_inc(s_ld[k], 16)
                                sp.dma_start(ea[:, k], eap[bass.ds(e, GE), :].rearrange("(p t) c -> p t c", p=P)).then_inc(s_ld[k], 16)
                            else:
                                sp.dma_start(rs[:, k], rec[bass.ds(g * GE, GE), :].rearrange("(p t) c -> p t c", p=P)).then_inc(s_ld[k], 16)
                        steps(sp, NG, body)

                    @block.gpsimd
                    def _(pool):
                        def body(g, k, r):
                            pool.wait_ge(s_ld[k], (r + 1) * (16 * n_loads))
                            if layer:
                                at_least(pool, s_eaP, g - SLOTS + 1)
                                settle(pool)
                                pool.tensor_copy(ea[:, k], ea_in[:, k]).then_inc(s_eac, 1)
                            at_least(pool, s_V, g - SLOTS + 1)
                            settle(pool)
                            for t in range(T):
                                pool.indirect_dma_start(G[:, k, t, :], None, table,
                                                        bass.IndirectOffsetOnAxis(ap=idx[:, k, t, :], axis=0)).then_inc(s_g[k], 16)
                        steps(pool, NG, body)

                    @block.vector
                    def _(dve):
                        dve.memset(w[:], 0.0).then_inc(s_wz, 1)
                        dve.tensor_tensor(sel[:], bcast(ident[0:2 * heads, 0:heads], 2, P), bcast(ident[0:2 * heads, heads:2 * heads], 2, P),
                                          ALU.add).then_inc(s_sel, 1)
                        dve.memset(M[:], -BIG).then_inc(s_mi, 1)
                        dve.wait_ge(s_mi, 1)

                        def onehot(g, k, r):
                            q = k % 2
                            dve.wait_ge(s_ld[k], (r + 1) * (16 * n_loads))
                            at_least(dve, s_oh, g)
                            dve.tensor_scalar(lo[:], key[:, k, :, 0], base_node[:, order, bass.ds(g, 1)], None, ALU.subtract).then_inc(s_lo, 1)
                            dve.wait_ge(s_lo, g + 1)
                            at_least(dve, s_ohT, g - 1)
                            at_least(dve, s_oh32, g - 1)
                            for t in range(T):
                                ins = dve.tensor_scalar(ohb[:, q, t, :], iota_b[:], lo[:, t:t + 1], None, ALU.is_equal)
                            ins.then_inc(s_oh, 1)

                        def scores(g, k, r):
                            q = k % 2
                            if layer == 0:
                                dve.wait_ge(s_zs, g + 1)
                                at_least(dve, s_lg, g)
                                dve.tensor_tensor(z[:], zs[:], zv[0], ALU.max).then_inc(s_act, 1)
                                dve.wait_ge(s_act, g + 1)
                                dve.tensor_tensor(z[:], z[:], bcast(att, 1, T), ALU.mult).then_inc(s_mul, 1)
                                dve.wait_ge(s_mul, g + 1)
                                at_least(dve, s_d0, g - 1)
                                dve.tensor_reduce(lg[:, q], z[:].rearrange("p t (h c) -> p t h c", h=heads), AX.X, ALU.add).then_inc(s_lg, 1)
                            else:
                                dve.wait_ge(s_z, g + 1)
                                at_least(dve, s_lg0, g)
                                for b in range(banks):
                                    ts = slice(b * tpb, (b + 1) * tpb)
                                    ins = dve.scalar_tensor_tensor(z[:, ts, :], zv[b], 0.0, bcast(att, 1, tpb), ALU.max, ALU.mult)
                                ins.then_inc(s_mul, 1)
                                dve.wait_ge(s_mul, g + 1)
                                at_least(dve, s_lg, g)
                                dve.tensor_reduce(ss[:], z[:].rearrange("p t (h c) -> p t h c", h=heads), AX.X, ALU.add).then_inc(s_lg0, 1)

                        def split(g, k, r):
                            dve.wait_ge(s_lp0, g + 1)
                            dve.tensor_tensor(lgp[:, :, 1, :], lg[:, k % 2], lgp[:, :, 0, :], ALU.subtract).then_inc(s_lp, 1)

                        def block_of(g):
                            return dve.value_load(blk[0:1, order, bass.ds(g, 1)], min_val=0, max_val=NB)

                        def maxima(blk_g, g, k, r):
                            q = k % 2
                            m_old = M[:, bass.ds(blk_g, 1), :].rearrange("p a h -> p (a h)")
                            for h in range(heads):
                                dve.wait_ge(s_lb[h], g + 1)
                                if h == 0:
                                    dve.wait_ge(s_pen, g + 1)
                                    at_least(dve, s_mn, g)
                                if h >= 2:
                                    dve.wait_ge(s_gm[h - 2], g + 1)
                                settle(dve)
                                dve.tensor_tensor_reduce(junk[:, h % 2].rearrange("p t e -> p (t e)"), ps_lb[:, h % n_lb].rearrange("p t e -> p (t e)"),
                                                         pen[:, q].rearrange("p t e -> p (t e)"), 1.0, -BIG, ALU.add, ALU.max,
                                                         gm[:, h:h + 1]).then_inc(s_gm[h], 1)
                            for h in range(max(0, heads - 2), heads):
                                dve.wait_ge(s_gm[h], g + 1)
                            at_least(dve, s_mb, g)
                            at_least(dve, s_me, g)
                            dve.tensor_tensor(mn[:], m_old, gm[:], ALU.max).then_inc(s_mn, 1)
                            dve.wait_ge(s_mn, g + 1)
                            at_least(dve, s_corr, g)
                            dve.tensor_tensor(df[:], m_old, mn[:], ALU.subtract).then_inc(s_df, 1)
                            dve.wait_ge(s_df, g + 1)
                            settle(dve)
                            dve.tensor_copy(m_old, mn[:]).then_inc(s_mb, 1)

                        def exponents(g, k, r):
                            q = k % 2
                            dve.wait_ge(s_me, g + 1)
                            at_least(dve, s_p, g)
                            dve.tensor_tensor(dd[:].rearrange("p t h -> p (t h)"), lg[:, q].rearrange("p t h -> p (t h)"),
                                              ps_m[:, 0:T * heads], ALU.subtract).then_inc(s_d0, 1)
                            dve.wait_ge(s_d0, g + 1)
                            dve.tensor_scalar(dd[:], dd[:], 1.0, None, ALU.min).then_inc(s_d, 1)

                        def values(g, k, r):
                            dve.wait_ge(s_p, g + 1)
                            dve.tensor_tensor(V[:, :, :, 0:VC - 1], G[:, k, :, v0:R].rearrange("p t (h c) -> p t h c", h=heads),
                                              V[:, :, :, VC - 1:VC].broadcast_to([P, T, heads, VC - 1]), ALU.mult).then_inc(s_V, 1)

                        def keep(blk_g, g, k, r):
                            acc = ACC[:, bass.ds(blk_g, 1), 0:heads * VC].rearrange("p a (h c) -> p (a h) c", h=heads)
                            dve.wait_ge(s_corr, g + 1)
                            at_least(dve, s_done, g)
                            dve.tensor_tensor(acc, acc, bcast(corr[:], 2, VC), ALU.mult).then_inc(s_sc, 1)
                            dve.wait_ge(s_sc, g + 1)
                            dve.wait_ge(s_acc, g + 1)
                            dve.tensor_tensor(acc, acc, ps_a[:, 0:heads * VC].rearrange("p (h c) -> p h c", h=heads), ALU.add).then_inc(s_done, 1)

                        def body(g, k, r):
                            if not any(is_group(g, n) for n in range(2)):
                                keep(block_of(g - 2), *before(g, k, r, 2))
                            if not is_group(g, 0):
                                maxima(block_of(g - 1), *before(g, k, r))
                            scores(g, k, r)
                            split(g, k, r)
                            if not is_group(g, 0):
                                exponents(*before(g, k, r))
                            if not is_group(g, NG - 1):
                                onehot(*after(g, k, r))
                            if not is_group(g, 0):
                                values(*before(g, k, r))
                        onehot(0, 0, 0)
                        steps(dve, NG, body, end=1)
                        last = (NG - 1, SLOTS - 1, NG // SLOTS - 1)
                        keep(block_of(NG - 2), *before(*last))
                        maxima(block_of(NG - 1), *last)
                        exponents(*last)
                        values(*last)
                        keep(block_of(NG - 1), *last)

                    @block.tensor
                    def _(pe):
                        pe.wait_ge(s_w, 16 * T)
                        pe.wait_ge(s_sel, 1)

                        def turn(g, k, r):
                            q = k % 2
                            pe.wait_ge(s_oh, g + 1)
                            at_least(pe, s_pen, g)
                            for t in range(T):
                                mm = pe.transpose(ps_oh[:, t, :], ohb[:, q, t, :], identb[:])
                            mm.then_inc(s_ohT, 1)
                            if layer == 0:
                                pe.wait_ge(s_ld[k], (r + 1) * (16 * n_loads))
                            else:
                                pe.wait_ge(s_eac, g + 1)
                            at_least(pe, s_eaT, g)
                            settle(pe)
                            mm = pe.transpose(ps_ea[0:T * DE, 0:P], ea[:, k], ident[:])
                            mm.then_inc(s_eaP, 1)

                        def turn_scores(g, k, r):
                            pe.wait_ge(s_lp, g + 1)
                            at_least(pe, s_lTc, g)
                            for t in range(T):
                                mm = pe.transpose(ps_lT[0:2 * heads, t * P:(t + 1) * P], lgp[:, t].rearrange("p a h -> p (a h)"), identb[:])
                            mm.then_inc(s_lT, 1)

                        def spread(g, k, r):
                            pe.wait_ge(s_lTc, g + 1)
                            for h in range(heads):
                                if h >= n_lb:
                                    pe.wait_ge(s_gm[h - n_lb], g + 1)
                                else:
                                    at_least(pe, s_gm[max(j for j in range(heads) if j % n_lb == h)], g)
                                pe.matmul(ps_lb[:, h % n_lb].rearrange("p t e -> p (t e)"), sel[:, h, :], lgT[:], start=True, stop=True).then_inc(s_lb[h], 1)

                        def edge_rows(g, k, r):
                            q = k % 2
                            blk_g = pe.value_load(blk[0:1, order, bass.ds(g, 1)], min_val=0, max_val=NB)
                            pe.wait_ge(s_eaT, g + 1)
                            at_least(pe, s_mul if layer else s_act, g)
                            for b in range(banks):
                                pe.matmul(ps_z[:, b, 0:tpb * width], eaT[:], w[:, b * tpb:(b + 1) * tpb, :].rearrange("p t c -> p (t c)"),
                                          start=True, stop=False)
                            pe.wait_ge(s_ohN, g + 1)
                            for t in range(T):
                                pe.matmul(zv[t // tpb][:, t % tpb, :], ohN[:, q, t, :], PT[:, bass.ds(blk_g, 1), 0:width].rearrange("p a c -> p (a c)"),
                                          start=False, stop=False)
                            pe.wait_ge(s_g[k], (r + 1) * (16 * T))
                            for b in range(banks):
                                mm = pe.matmul(zv[b], ident[:], G[:, k, b * tpb:(b + 1) * tpb, 0:width], start=False, stop=True)
                            mm.then_inc(s_z, 1)

                        def edge_maxima(g, k, r):
                            pe.wait_ge(s_mn, g + 1)
                            at_least(pe, s_d0, g)
                            for t in range(T):
                                mm = pe.matmul(ps_m[:, t * heads:(t + 1) * heads], ohN[:, k % 2, t, :], mn[:], start=True, stop=True)
                            mm.then_inc(s_me, 1)

                        def node_sums(g, k, r):
                            pe.wait_ge(s_oh32, g + 1)
                            pe.wait_ge(s_V, g + 1)
                            at_least(pe, s_done, g)
                            for t in range(T):
                                mm = pe.matmul(ps_a[:, 0:heads * VC], oh[:, k, t, :], V[:, t].rearrange("p h c -> p (h c)"),
                                               start=(t == 0), stop=(t == T - 1))
                            mm.then_inc(s_acc, 1)

                        def body(g, k, r):
                            if not is_group(g, 0):
                                spread(*before(g, k, r))
                            edge_rows(g, k, r)
                            if not is_group(g, 0):
                                edge_maxima(*before(g, k, r))
                            turn_scores(g, k, r)
                            if not is_group(g, NG - 1):
                                turn(*after(g, k, r))
                            if not is_group(g, 0):
                                node_sums(*before(g, k, r))
                        turn(0, 0, 0)
                        steps(pe, NG, body, end=1)
                        last = (NG - 1, SLOTS - 1, NG // SLOTS - 1)
                        spread(*last)
                        edge_maxima(*last)
                        node_sums(*last)

                    @block.scalar
                    def _(act):
                        def copies(g, k, r):
                            q = k % 2
                            act.wait_ge(s_ohT, g + 1)
                            at_least(act, s_me, g - 1)
                            act.copy(ohN[:, q], ps_oh[:, 0:T]).then_inc(s_ohN, 1)
                            at_least(act, s_gm[heads - 1], g - 1)
                            act.activation(pen[:, q], ps_oh[:, 0:T], ACT.Copy, bias=-BIG, scale=BIG).then_inc(s_pen, 1)
                            act.wait_ge(s_eaP, g + 1)
                            at_least(act, s_z, g)
                            act.copy(eaT[:], ps_ea[0:T * DE, 0:P]).then_inc(s_eaT, 1)
                            at_least(act, s_acc, g - SLOTS + 1)
                            act.wait_ge(s_oh, g + 1)
                            act.copy(oh[:, k], ohb[:, q]).then_inc(s_oh32, 1)

                        def slope(g, k, r):
                            act.wait_ge(s_z, g + 1)
                            at_least(act, s_act, g)
                            act.activation(zs[:], zv[0], ACT.Copy, scale=0.2).then_inc(s_zs, 1)

                        def high_part(g, k, r):
                            q = k % 2
                            if layer:
                                act.wait_ge(s_lg0, g + 1)
                                at_least(act, s_d0, g - 1)
                                act.activation(lg[:, q], ss[:], ACT.Identity, bias=rows[:, ROWS["b_att2"]]).then_inc(s_lg, 1)
                            act.wait_ge(s_lg, g + 1)
                            at_least(act, s_lT, g)
                            act.copy(lgp[:, :, 0, :], lg[:, q]).then_inc(s_lp0, 1)

                        def rescale(g, k, r):
                            act.wait_ge(s_df, g + 1)
                            at_least(act, s_sc, g)
                            act.activation(corr[:], df[:], ACT.Exp).then_inc(s_corr, 1)

                        def weights(g, k, r):
                            act.wait_ge(s_d, g + 1)
                            at_least(act, s_acc, g)
                            act.activation(V[:, :, :, VC - 1], dd[:], ACT.Exp).then_inc(s_p, 1)

                        def score_rows(g, k, r):
                            act.wait_ge(s_lT, g + 1)
                            at_least(act, s_lb[heads - 1], g)
                            act.copy(lgT[:], ps_lT[0:2 * heads, 0:T * P]).then_inc(s_lTc, 1)

                        def body(g, k, r):
                            if layer == 0:
                                slope(g, k, r)
                            if not is_group(g, 0):
                                rescale(*before(g, k, r))
                            high_part(g, k, r)
                            if not is_group(g, 0):
                                weights(*before(g, k, r))
                            score_rows(g, k, r)
                            if not is_group(g, NG - 1):
                                copies(*after(g, k, r))
                        copies(0, 0, 0)
                        steps(act, NG, body, end=1)
                        last = (NG - 1, SLOTS - 1, NG // SLOTS - 1)
                        rescale(*last)
                        weights(*last)

        def segment_max():
            with phase() as ctx:
                w = sb_in(ctx, "w2_sb", [D, D])
                key = sb_in(ctx, "m_key", [P, SLOTS, T], I32)
                nxt = sb_in(ctx, "m_next", [P, SLOTS, T], I32)
                idx = sb_in(ctx, "m_idx", [P, SLOTS, T, 1], I32)
                row = sb_in(ctx, "m_row", [D, SLOTS, 1 + GE], I32)
                G = sb_in(ctx, "m_G", [P, SLOTS, T, D])
                lo = sb_in(ctx, "m_lo", [P, 3, T])
                oh = sb_in(ctx, "m_oh", [P, T, P], BF16)
                ohL = sb_in(ctx, "m_ohL", [P, 2, T, P])
                ohN = sb_in(ctx, "m_ohN", [P, T, P])
                fl = sb_in(ctx, "m_fl", [D, GE])
                flp = sb_in(ctx, "m_flp", [D, 2, GE])
                z = sb_in(ctx, "m_z", [P, T, D])
                zr = sb_in(ctx, "m_zr", [P, T, D])
                zT = sb_in(ctx, "m_zT", [D, GE])
                S = sb_in(ctx, "m_S", [D, 2, GE])
                Sx = sb_in(ctx, "m_Sx", [P, T, D + 1])
                ps_oh = ps_in(ctx, "m_ps_oh", [P, 2 * T, P], BF16)
                ps_z = ps_in(ctx, "m_ps_z", [P, T, P])
                ps_t = ps_in(ctx, "m_ps_t", [P, GE])
                ps_m = ps_in(ctx, "m_ps_m", [P, GE])
                ps_s = ps_in(ctx, "m_ps_s", [P, T, P])
                ps_a = ps_in(ctx, "m_ps_a", [P, 512])
                (s_w, s_one, s_lo, s_eq, s_lol, s_oh, s_ohL, s_fl, s_flp, s_ohT, s_ohN, s_kr, s_z, s_zr, s_tp, s_zT, s_msg, s_scan, s_st, s_Sx,
                 s_acc, s_done) = (sem_in(ctx, "m_" + n) for n in (
                    "weights", "ones_column", "local_key", "same_as_next", "last_key", "onehot", "onehot_last", "changes", "resets",
                    "onehot_turned", "onehot_nodes", "key_rows", "rows_added", "hidden", "hidden_turned", "hidden_copied", "messages",
                    "scanned", "scan_turned", "scan_copied", "group_values", "group_done"))
                s_ld = [sem_in(ctx, f"m_edges_landed{k}") for k in range(SLOTS)]
                s_g = [sem_in(ctx, f"m_gathered{k}") for k in range(SLOTS)]
                N_LOADS = 4
                with nc.Block() as block:
                    @block.sync
                    def _(sp):
                        sp.dma_start(w[:], w2).then_inc(s_w, 16)

                        def body(g, k, r):
                            at_least(sp, s_lol, g - SLOTS + 1)
                            at_least(sp, s_fl, g - SLOTS + 1)
                            settle(sp)
                            at_least(sp, s_g[k], r * (16 * T))
                            settle(sp)
                            e = sp.value_load(goff[0:1, bass.ds(g, 1)], min_val=0, max_val=E)
                            sp.dma_start(key[:, k, :], keyp[bass.ds(e + 1, GE)].rearrange("(p t) -> p t", p=P)).then_inc(s_ld[k], 16)
                            sp.dma_start(nxt[:, k, :], keyp[bass.ds(e + 2, GE)].rearrange("(p t) -> p t", p=P)).then_inc(s_ld[k], 16)
                            sp.dma_start(idx[:, k, :, 0], srcp[bass.ds(e, GE)].rearrange("(p t) -> p t", p=P)).then_inc(s_ld[k], 16)
                            sp.dma_start(row[:, k, :], keyp[bass.ds(e, GE + 1)].partition_broadcast(D)).then_inc(s_ld[k], 16)
                        steps(sp, NG, body)

                    @block.gpsimd
                    def _(pool):
                        def body(g, k, r):
                            at_least(pool, s_z, g - SLOTS + 1)
                            pool.wait_ge(s_ld[k], (r + 1) * (16 * N_LOADS))
                            settle(pool)
                            for t in range(T):
                                pool.indirect_dma_start(G[:, k, t, :], None, tab1,
                                                        bass.IndirectOffsetOnAxis(ap=idx[:, k, t, :], axis=0)).then_inc(s_g[k], 16)
                        steps(pool, NG, body)

                    @block.vector
                    def _(dve):
                        dve.memset(Sx[:], 1.0).then_inc(s_one, 1)

                        def onehots(g, k, r):
                            q = k % 2
                            dve.wait_ge(s_ld[k], (r + 1) * (16 * N_LOADS))
                            dve.tensor_scalar(lo[:, 0], key[:, k], base_node[:, 0, bass.ds(g, 1)], None, ALU.subtract).then_inc(s_lo, 1)
                            dve.tensor_tensor(lo[:, 1], key[:, k], nxt[:, k], ALU.is_equal).then_inc(s_eq, 1)
                            dve.wait_ge(s_lo, g + 1)
                            dve.wait_ge(s_eq, g + 1)
                            dve.scalar_tensor_tensor(lo[:, 2], lo[:, 1], float(FAR), lo[:, 0], ALU.mult, ALU.add).then_inc(s_lol, 1)
                            at_least(dve, s_ohT, g)
                            for t in range(T):
                                ins = dve.tensor_scalar(oh[:, t, :], iota_b[:], lo[:, 0, t:t + 1], None, ALU.is_equal)
                            ins.then_inc(s_oh, 1)
                            dve.wait_ge(s_lol, g + 1)
                            at_least(dve, s_acc, g - 1)
                            dve.tensor_tensor(ohL[:, q], bcast(iota_n[:], 1, T), bcast(lo[:, 2], 2, P), ALU.is_equal).then_inc(s_ohL, 1)
                            at_least(dve, s_flp, g)
                            dve.tensor_tensor(fl[:], row[:, k, 1:1 + GE], row[:, k, 0:GE], ALU.not_equal).then_inc(s_fl, 1)

                        def scan(g, k, r):
                            q = k % 2
                            first = isinstance(g, int) and g == 0
                            dve.wait_ge(s_msg, g + 1)
                            dve.wait_ge(s_flp, g + 1)
                            at_least(dve, s_st, g - 1)
                            at_least(dve, s_scan, g)
                            dve.tensor_tensor_scan(S[:, q], flp[:, q], ps_m[0:D, :], 0.0 if first else S[:, 1 - q, GE - 1:GE],
                                                   ALU.add, ALU.max).then_inc(s_scan, 1)

                        def add(g, k, r):
                            dve.wait_ge(s_g[k], (r + 1) * (16 * T))
                            dve.wait_ge(s_kr, g + 1)
                            at_least(dve, s_zr, g)
                            dve.tensor_tensor(z[:], ps_z[:, :, 0:D], G[:, k], ALU.add).then_inc(s_z, 1)

                        def keep(g, k, r):
                            blk_g = dve.value_load(blk[0:1, 0, bass.ds(g, 1)], min_val=0, max_val=NB)
                            acc = ACC[:, bass.ds(blk_g, 1), 0:D + 1].rearrange("p a c -> p (a c)")
                            dve.wait_ge(s_acc, g + 1)
                            at_least(dve, s_done, g)
                            dve.tensor_tensor(acc, acc, ps_a[:, 0:D + 1], ALU.add).then_inc(s_done, 1)

                        def body(g, k, r):
                            prev = (g - 1, (k - 1) % SLOTS, r if k else r - 1)
                            first = isinstance(g, int) and g == 0
                            onehots(g, k, r)
                            if not first:
                                scan(*prev)
                            add(g, k, r)
                            if not first:
                                keep(*prev)
                        steps(dve, NG, body)
                        last = (NG - 1, SLOTS - 1, NG // SLOTS - 1)
                        scan(*last)
                        keep(*last)

                    @block.tensor
                    def _(pe):
                        pe.wait_ge(s_w, 16)

                        def turn(g, k, r):
                            pe.wait_ge(s_oh, g + 1)
                            at_least(pe, s_ohN, g)
                            for t in range(T):
                                mm = pe.transpose(ps_oh[:, t, :], oh[:, t, :], identb[:])
                            mm.then_inc(s_ohT, 1)

                        def messages(g, k, r):
                            pe.wait_ge(s_zr, g + 1)
                            at_least(pe, s_zT, g)
                            settle(pe)
                            for t in range(T):
                                mm = pe.transpose(ps_t[0:D, :].rearrange("d (p t) -> d t p", t=T)[:, t, :], zr[:, t, :], ident[:])
                            mm.then_inc(s_tp, 1)
                            pe.wait_ge(s_zT, g + 1)
                            at_least(pe, s_scan, g)
                            settle(pe)
                            pe.matmul(ps_m[0:D, :], w[:], zT[:], start=True, stop=True).then_inc(s_msg, 1)

                        def key_rows(g, k, r):
                            blk_g = pe.value_load(blk[0:1, 0, bass.ds(g, 1)], min_val=0, max_val=NB)
                            pe.wait_ge(s_ohN, g + 1)
                            at_least(pe, s_z, g)
                            for t in range(T):
                                mm = pe.matmul(ps_z[:, t, 0:D], ohN[:, t, :], PT[:, bass.ds(blk_g, 1), 0:D].rearrange("p a c -> p (a c)"),
                                               start=True, stop=True)
                            mm.then_inc(s_kr, 1)

                        def values(g, k, r):
                            q = k % 2
                            pe.wait_ge(s_scan, g + 1)
                            at_least(pe, s_Sx, g)
                            settle(pe)
                            for t in range(T):
                                mm = pe.transpose(ps_s[:, t, 0:D], S[:, q, :].rearrange("d (p t) -> d t p", t=T)[:, t, :], ident[0:D, 0:D])
                            mm.then_inc(s_st, 1)
                            pe.wait_ge(s_Sx, g + 1)
                            pe.wait_ge(s_ohL, g + 1)
                            at_least(pe, s_done, g)
                            for t in range(T):
                                mm = pe.matmul(ps_a[:, 0:D + 1], ohL[:, q, t, :], Sx[:, t, :], start=(t == 0), stop=(t == T - 1))
                            mm.then_inc(s_acc, 1)

                        def body(g, k, r):
                            prev = (g - 1, (k - 1) % SLOTS, r if k else r - 1)
                            first = isinstance(g, int) and g == 0
                            turn(g, k, r)
                            if not first:
                                messages(*prev)
                            key_rows(g, k, r)
                            if not first:
                                values(*prev)
                        steps(pe, NG, body)
                        last = (NG - 1, SLOTS - 1, NG // SLOTS - 1)
                        messages(*last)
                        values(*last)

                    @block.scalar
                    def _(act):
                        act.wait_ge(s_one, 1)

                        def copies(g, k, r):
                            act.wait_ge(s_ohT, g + 1)
                            at_least(act, s_kr, g)
                            act.copy(ohN[:], ps_oh[:, 0:T]).then_inc(s_ohN, 1)
                            act.wait_ge(s_fl, g + 1)
                            at_least(act, s_scan, g - 1)
                            act.activation(flp[:, k % 2], fl[:], ACT.Copy, scale=-3.0e38).then_inc(s_flp, 1)

                        def hidden_turned(g, k, r):
                            act.wait_ge(s_tp, g + 1)
                            at_least(act, s_msg, g)
                            act.copy(zT[:], ps_t[0:D, :]).then_inc(s_zT, 1)

                        def scanned(g, k, r):
                            act.wait_ge(s_st, g + 1)
                            at_least(act, s_acc, g)
                            act.copy(Sx[:, :, 0:D], ps_s[:, :, 0:D]).then_inc(s_Sx, 1)

                        def relu(g, k, r):
                            act.wait_ge(s_z, g + 1)
                            at_least(act, s_tp, g)
                            act.activation(zr[:], z[:], ACT.Relu).then_inc(s_zr, 1)

                        def body(g, k, r):
                            prev = (g - 1, (k - 1) % SLOTS, r if k else r - 1)
                            first = isinstance(g, int) and g == 0
                            copies(g, k, r)
                            if not first:
                                hidden_turned(*prev)
                            relu(g, k, r)
                            if not first:
                                scanned(*prev)
                        steps(act, NG, body)
                        last = (NG - 1, SLOTS - 1, NG // SLOTS - 1)
                        hidden_turned(*last)
                        scanned(*last)

        def segment_sum():
            with phase() as ctx:
                rs = sb_in(ctx, "g_rs", [P, SLOTS, T, REC], I32)
                ea = rs[:].bitcast(F32)[:, :, :, EA64:EA64 + D]
                G = sb_in(ctx, "g_G", [P, SLOTS, T, D])
                lo = sb_in(ctx, "g_lo", [P, T])
                oh = sb_in(ctx, "g_oh", [P, 2, T, P])
                z = sb_in(ctx, "g_z", [P, 2, T, D])
                zr = sb_in(ctx, "g_zr", [P, 2, T, D])
                ps_a = ps_in(ctx, "g_ps_a", [P, 2, 512])
                s_lo, s_oh, s_z, s_zr, s_acc, s_done = (sem_in(ctx, "g_" + n) for n in (
                    "local_key", "onehot", "rows_added", "messages", "group_sums", "group_done"))
                s_ld = [sem_in(ctx, f"g_edges_landed{k}") for k in range(SLOTS)]
                s_g = [sem_in(ctx, f"g_gathered{k}") for k in range(SLOTS)]
                with nc.Block() as block:
                    @block.sync
                    def _(sp):
                        def body(g, k, r):
                            at_least(sp, s_z, g - SLOTS + 1)
                            settle(sp)
                            at_least(sp, s_g[k], r * (16 * T))
                            settle(sp)
                            sp.dma_start(rs[:, k], rec[bass.ds(g * GE, GE), :].rearrange("(p t) c -> p t c", p=P)).then_inc(s_ld[k], 16)
                        steps(sp, NG, body)

                    @block.gpsimd
                    def _(pool):
                        def body(g, k, r):
                            at_least(pool, s_z, g - SLOTS + 1)
                            pool.wait_ge(s_ld[k], (r + 1) * 16)
                            settle(pool)
                            for t in range(T):
                                pool.indirect_dma_start(G[:, k, t, :], None, tab3,
                                                        bass.IndirectOffsetOnAxis(ap=rs[:, k, t, 1:2], axis=0)).then_inc(s_g[k], 16)
                        steps(pool, NG, body)

                    @block.vector
                    def _(dve):
                        def group(g, k, r):
                            q = k % 2
                            dve.wait_ge(s_ld[k], (r + 1) * 16)
                            at_least(dve, s_oh, g)
                            dve.tensor_scalar(lo[:], rs[:, k, :, 0], base_node[:, 1, bass.ds(g, 1)], None, ALU.subtract).then_inc(s_lo, 1)
                            dve.wait_ge(s_lo, g + 1)
                            at_least(dve, s_acc, g - 1)
                            dve.tensor_tensor(oh[:, q], bcast(iota_n[:], 1, T), bcast(lo[:], 2, P), ALU.is_equal).then_inc(s_oh, 1)
                            dve.wait_ge(s_g[k], (r + 1) * (16 * T))
                            at_least(dve, s_zr, g - 1)
                            dve.tensor_tensor(z[:, q], G[:, k], ea[:, k], ALU.add).then_inc(s_z, 1)

                        def keep(g, k, r):
                            blk_g = dve.value_load(blk[0:1, 1, bass.ds(g, 1)], min_val=0, max_val=NB)
                            acc = ACC[:, bass.ds(blk_g, 1), 0:D].rearrange("p a c -> p (a c)")
                            dve.wait_ge(s_acc, g + 1)
                            at_least(dve, s_done, g)
                            dve.tensor_tensor(acc, acc, ps_a[:, k % 2, 0:D], ALU.add).then_inc(s_done, 1)

                        def body(g, k, r):
                            group(g, k, r)
                            if not (isinstance(g, int) and g == 0):
                                keep(g - 1, (k - 1) % SLOTS, r if k else r - 1)
                        steps(dve, NG, body)
                        keep(NG - 1, SLOTS - 1, NG // SLOTS - 1)

                    @block.scalar
                    def _(act):
                        def body(g, k, r):
                            act.wait_ge(s_z, g + 1)
                            at_least(act, s_acc, g - 1)
                            act.activation(zr[:, k % 2], z[:, k % 2], ACT.Relu).then_inc(s_zr, 1)
                        steps(act, NG, body)

                    @block.tensor
                    def _(pe):
                        def body(g, k, r):
                            q = k % 2
                            pe.wait_ge(s_oh, g + 1)
                            pe.wait_ge(s_zr, g + 1)
                            at_least(pe, s_done, g - 1)
                            for t in range(T):
                                mm = pe.matmul(ps_a[:, q, 0:D], oh[:, q, t, :], zr[:, q, t, :], start=(t == 0), stop=(t == T - 1))
                            mm.then_inc(s_acc, 1)
                        steps(pe, NG, body)

        def finish_gat():
            with phase() as ctx:
                rd = sb_in(ctx, "b_rd", [P, NB, HEADS])
                small = sb_in(ctx, "b_small", [P, 4, D])
                valid = sb_in(ctx, "b_valid", [P, 2])
                junk = sb_in(ctx, "b_junk", [P, P])
                epsc = sb_in(ctx, "b_eps", [P, 1])
                ps = ps_in(ctx, "b_ps", [P, 2, 512])
                s_v, s_sum, s_tot, s_std0, s_std, s_pre, s_gelu = (sem_in(ctx, "b_" + n) for n in (
                    "steps", "sums_ready", "totals", "var_ready", "std_ready", "pre_gelu", "gelu"))
                O, Q = PT[:, 0:NB, 0:D], PT[:, 0:NB, D:2 * D]
                OL = PT[:, NBLK - 1, 0:D]
                acc = ACC[:, 0:NB, :].rearrange("p b (h c) -> p b h c", h=HEADS)
                C = D // HEADS
                with nc.Block() as block:
                    @block.vector
                    def _(dve):
                        do = chain(dve, s_v)
                        do(dve.memset(epsc[:], 1e-5))
                        do(dve.tensor_tensor_reduce(junk[:], ident[:], iota_n[:], 1.0, 0.0, ALU.mult, ALU.add, valid[:, 0:1]))
                        do(dve.tensor_scalar(valid[:, 1:2], valid[:, 0:1], float(last_rows), None, ALU.is_lt))
                        do(dve.tensor_scalar(rd[:], acc[:, :, :, C], 1e-16, None, ALU.add))
                        do(dve.reciprocal(rd[:], rd[:]))
                        for h in range(HEADS):
                            do(dve.tensor_tensor(PT[:, 0:NB, h * C:(h + 1) * C], acc[:, :, h, 0:C], bcast(rd[:, :, h], 2, C), ALU.mult))
                        do(dve.tensor_tensor(O, O, bcast(rows[:, ROWS["bias"]], 1, NB), ALU.add))
                        for b in range(NBLK, NB):
                            do(dve.memset(PT[:, b, 0:D], 0.0))
                        do(dve.tensor_scalar(OL, OL, valid[:, 1:2], None, ALU.mult))
                        dve.tensor_reduce(small[:, 0], O.rearrange("p b d -> p d b"), AX.X, ALU.add).then_inc(s_sum, 1)
                        dve.wait_ge(s_tot, 1)
                        do(dve.tensor_scalar(small[:, 1], ps[:, 0, 0:D], 1.0 / N, None, ALU.mult))
                        do(dve.tensor_tensor(O, O, bcast(small[:, 1], 1, NB), ALU.subtract))
                        for b in range(NBLK, NB):
                            do(dve.memset(PT[:, b, 0:D], 0.0))
                        do(dve.tensor_scalar(OL, OL, valid[:, 1:2], None, ALU.mult))
                        do(dve.tensor_tensor(Q, O, O, ALU.mult))
                        dve.tensor_reduce(small[:, 2], Q.rearrange("p b d -> p d b"), AX.X, ALU.add).then_inc(s_sum, 1)
                        dve.wait_ge(s_tot, 2)
                        dve.tensor_scalar(small[:, 3], ps[:, 1, 0:D], 1.0 / N, None, ALU.mult).then_inc(s_std0, 1)
                        dve.wait_ge(s_std, 1)
                        do(dve.reciprocal(small[:, 1], small[:, 0]))
                        do(dve.tensor_tensor(small[:, 1], small[:, 1], rows[:, ROWS["gamma"]], ALU.mult))
                        do(dve.tensor_tensor(O, O, bcast(small[:, 1], 1, NB), ALU.mult))
                        do(dve.tensor_tensor(O, O, bcast(rows[:, ROWS["beta"]], 1, NB), ALU.add))
                        dve.tensor_tensor(O, O, H[:], ALU.add).then_inc(s_pre, 1)
                        dve.wait_ge(s_gelu, 1)
                        do(dve.tensor_tensor(X[:], X[:], Q, ALU.add))

                    @block.tensor
                    def _(pe):
                        for i in range(2):
                            pe.wait_ge(s_sum, i + 1)
                            pe.matmul(ps[:, i, 0:D], ones[:], small[:, 2 * i], start=True, stop=True).then_inc(s_tot, 1)

                    @block.scalar
                    def _(act):
                        act.wait_ge(s_std0, 1)
                        act.activation(small[:, 0], small[:, 3], ACT.Sqrt, bias=epsc[:]).then_inc(s_std, 1)
                        act.wait_ge(s_pre, 1)
                        act.activation(Q, O, ACT.Gelu).then_inc(s_gelu, 1)

        def finish_max():
            with phase() as ctx:
                s_v = sem_in(ctx, "x_steps")
                with nc.Block() as block:
                    @block.vector
                    def _(dve):
                        do = chain(dve, s_v)
                        t = PT[:, 0:NB, 0:D]
                        do(dve.tensor_tensor(t, bcast(rows[:, ROWS["b2_l1"]], 1, NB), ACC[:, 0:NB, D:D + 1].broadcast_to([P, NB, D]), ALU.mult))
                        do(dve.tensor_tensor(t, t, ACC[:, 0:NB, 0:D], ALU.add))
                        do(dve.tensor_tensor(X[:], X[:], t, ALU.add))

        def finish_gru():
            with phase() as ctx:
                w = sb_in(ctx, "r_w", [P, 4 * D])
                bias = sb_in(ctx, "r_bias", [2, 4 * D])
                rd = sb_in(ctx, "r_rd", [P, 2, NB])
                hm = sb_in(ctx, "r_hm", [P, 2, 2 * D])
                hmT = sb_in(ctx, "r_hmT", [P, 2, P])
                rz = sb_in(ctx, "r_rz", [P, 2, 2 * D])
                t1 = sb_in(ctx, "r_t1", [P, 2, D])
                n = sb_in(ctx, "r_n", [P, 2, D])
                d = sb_in(ctx, "r_d", [P, D])
                ps_t = ps_in(ctx, "r_ps_t", [P, 2, 512])
                ps_w = ps_in(ctx, "r_ps_w", [P, 2, 512])
                (s_w, s_v, s_cp, s_t, s_hmT, s_mm, s_rz, s_t1, s_pre, s_n, s_d1, s_d2, s_d3, s_d4, s_d5, s_x) = (sem_in(ctx, "r_" + q) for q in (
                    "weights", "steps", "inputs_copied", "turned", "turned_copied", "gates_in", "gates", "reset_applied", "candidate_in",
                    "candidate", "msg_less_n", "scaled", "new_h", "less_h", "selected", "block_done"))
                msg = ACC[:, 0:NB, 0:D]
                with nc.Block() as block:
                    @block.sync
                    def _(sp):
                        sp.dma_start(w[:], wgru).then_inc(s_w, 16)
                        sp.dma_start(bias[:], bgru).then_inc(s_w, 16)
                        sp.wait_ge(s_w, 32)

                    @block.vector
                    def _(dve):
                        do = chain(dve, s_v)
                        den = ACC[:, 0:NB, D]
                        do(dve.tensor_scalar(rd[:, 1], den, 0.0, None, ALU.is_gt))
                        do(dve.tensor_scalar(rd[:, 0], rd[:, 1], -1.0, 1.0, ALU.mult, ALU.add))
                        do(dve.tensor_tensor(rd[:, 0], rd[:, 0], den, ALU.add))
                        do(dve.reciprocal(rd[:, 0], rd[:, 0]))
                        do(dve.tensor_tensor(msg, msg, bcast(rd[:, 0], 2, D), ALU.mult))

                        def at(big, b):
                            return big[:, bass.ds(b, 1), :].rearrange("p a d -> p (a d)")

                        def body(b, k, r):
                            m_b = ACC[:, bass.ds(b, 1), 0:D].rearrange("p a d -> p (a d)")
                            at_least(dve, s_t, b - 1)
                            at_least(dve, s_x, b - 1)
                            dve.tensor_copy(hm[:, k, 0:D], at(H, b)).then_inc(s_cp, 1)
                            dve.tensor_copy(hm[:, k, D:2 * D], m_b).then_inc(s_cp, 1)
                            dve.wait_ge(s_rz, b + 1)
                            dve.tensor_tensor(t1[:, k], rz[:, k, 0:D], ps_w[:, k, 3 * D:4 * D], ALU.mult).then_inc(s_t1, 1)
                            dve.wait_ge(s_t1, b + 1)
                            dve.tensor_tensor(t1[:, k], t1[:, k], ps_w[:, k, 2 * D:3 * D], ALU.add).then_inc(s_pre, 1)
                            dve.wait_ge(s_n, b + 1)
                            at_least(dve, s_x, b)
                            dve.tensor_tensor(d[:], hm[:, k, D:2 * D], n[:, k], ALU.subtract).then_inc(s_d1, 1)
                            dve.wait_ge(s_d1, b + 1)
                            dve.tensor_tensor(d[:], d[:], rz[:, k, D:2 * D], ALU.mult).then_inc(s_d2, 1)
                            dve.wait_ge(s_d2, b + 1)
                            dve.tensor_tensor(d[:], d[:], n[:, k], ALU.add).then_inc(s_d3, 1)
                            dve.wait_ge(s_d3, b + 1)
                            dve.tensor_tensor(d[:], d[:], hm[:, k, 0:D], ALU.subtract).then_inc(s_d4, 1)
                            dve.wait_ge(s_d4, b + 1)
                            dve.scalar_tensor_tensor(d[:], d[:], rd[:, 1, bass.ds(b, 1)], hm[:, k, 0:D], ALU.mult, ALU.add).then_inc(s_d5, 1)
                            dve.wait_ge(s_d5, b + 1)
                            dve.tensor_tensor(at(X, b), at(X, b), d[:], ALU.add).then_inc(s_x, 1)
                        steps(dve, NB, body, 2)

                    @block.tensor
                    def _(pe):
                        pe.wait_ge(s_w, 32)

                        def body(b, k, r):
                            pe.wait_ge(s_cp, b * 2 + 2)
                            at_least(pe, s_hmT, b - 1)
                            pe.transpose(ps_t[:, k, 0:P], hm[:, k, :], ident[:]).then_inc(s_t, 1)
                            pe.wait_ge(s_hmT, b + 1)
                            at_least(pe, s_pre, b - 1)
                            pe.matmul(ps_w[:, k, 0:4 * D], hmT[:, k], w[:], start=True, stop=False)
                            pe.matmul(ps_w[:, k, 0:4 * D], ones[0:2, :], bias[:], start=False, stop=True).then_inc(s_mm, 1)
                        steps(pe, NB, body, 2)

                    @block.scalar
                    def _(act):
                        def body(b, k, r):
                            act.wait_ge(s_t, b + 1)
                            at_least(act, s_mm, b - 1)
                            act.copy(hmT[:, k], ps_t[:, k, 0:P]).then_inc(s_hmT, 1)
                            act.wait_ge(s_mm, b + 1)
                            at_least(act, s_x, b - 1)
                            act.activation(rz[:, k], ps_w[:, k, 0:2 * D], ACT.Sigmoid).then_inc(s_rz, 1)
                            act.wait_ge(s_pre, b + 1)
                            act.activation(n[:, k], t1[:, k], ACT.Tanh).then_inc(s_n, 1)
                        steps(act, NB, body, 2)

        def finish_gine():
            DD = 2 * D
            with phase() as ctx:
                wa = sb_in(ctx, "f_w1", [D + 1, DD])
                wb = sb_in(ctx, "f_w3", [DD, D])
                e1 = sb_in(ctx, "f_e1", [P, 1])
                epsc = sb_in(ctx, "f_eps", [P, 1])
                hb = sb_in(ctx, "f_hb", [P, 2, DD])
                hT = sb_in(ctx, "f_hT", [D + 1, 2, P])
                yT = sb_in(ctx, "f_yT", [DD, 2, P])
                st = sb_in(ctx, "f_st", [P, 2, NB])
                ps_t = ps_in(ctx, "f_ps_t", [P, 2, 512])
                ps_w = ps_in(ctx, "f_ps_w", [P, 2, 512])
                Y = PT[:, 0:NB, 0:DD]
                (s_w, s_v, s_hb, s_t, s_hT, s_mm, s_y, s_var, s_std, s_yb, s_yt, s_yT, s_m2, s_x, s_out) = (sem_in(ctx, "f_" + q) for q in (
                    "weights", "steps", "block_copied", "block_turned", "turned_copied", "hidden", "hidden_kept", "var_ready", "std_ready",
                    "hidden_copied", "hidden_turned", "hidden_turned_copied", "outputs", "block_done", "stored"))
                with nc.Block() as block:
                    @block.sync
                    def _(sp):
                        sp.dma_start(wa[:], w1).then_inc(s_w, 16)
                        sp.dma_start(wb[:], w3).then_inc(s_w, 16)
                        sp.wait_ge(s_x, NB + 1)
                        sp.dma_start(out[0:P * (NBLK - 1), :].rearrange("(b p) d -> p b d", p=P), X[:, 0:NBLK - 1, :]).then_inc(s_out, 16)
                        sp.dma_start(out[P * (NBLK - 1):N, :], X[0:last_rows, NBLK - 1, :]).then_inc(s_out, 16)
                        sp.wait_ge(s_out, 32)

                    @block.vector
                    def _(dve):
                        do = chain(dve, s_v)
                        do(dve.memset(epsc[:], 1e-5))
                        do(dve.memset(hT[D:D + 1, :, :], 1.0))
                        do(dve.tensor_scalar(e1[:], rows[:, ROWS["eps"]], 1.0, None, ALU.add))
                        do(dve.scalar_tensor_tensor(H[:], H[:], e1[:], ACC[:, 0:NB, 0:D], ALU.mult, ALU.add))

                        def hidden(b, k, r):
                            at_least(dve, s_t, b - 1)
                            dve.tensor_copy(hb[:, k, 0:D], H[:, bass.ds(b, 1), :].rearrange("p a d -> p (a d)")).then_inc(s_hb, 1)
                            dve.wait_ge(s_mm, b + 1)
                            settle(dve)
                            dve.tensor_copy(PT[:, bass.ds(b, 1), 0:DD].rearrange("p a d -> p (a d)"), ps_w[:, k, 0:DD]).then_inc(s_y, 1)
                        steps(dve, NB, hidden, 2)
                        dve.wait_ge(s_y, NB)
                        sq = PT[:, 0:NB, 0:DD]
                        do(dve.tensor_reduce(st[:, 0], Y, AX.X, ALU.add))
                        do(dve.tensor_scalar(st[:, 0], st[:, 0], 1.0 / DD, None, ALU.mult))
                        do(dve.tensor_tensor(Y, Y, bcast(st[:, 0], 2, DD), ALU.subtract))
                        do(dve.tensor_tensor(H[:], PT[:, 0:NB, 0:D], PT[:, 0:NB, 0:D], ALU.mult))
                        do(dve.tensor_tensor(ACC[:, 0:NB, 0:D], PT[:, 0:NB, D:DD], PT[:, 0:NB, D:DD], ALU.mult))
                        do(dve.tensor_tensor(H[:], H[:], ACC[:, 0:NB, 0:D], ALU.add))
                        dve.tensor_reduce(st[:, 0], H[:], AX.X, ALU.add).then_inc(s_var, 1)
                        dve.wait_ge(s_std, 1)
                        do(dve.reciprocal(st[:, 1], st[:, 1]))
                        do(dve.tensor_tensor(Y, Y, bcast(st[:, 1], 2, DD), ALU.mult))
                        do(dve.tensor_tensor(Y, Y, bcast(rows[:, ROWS["ln_g"]], 1, NB), ALU.mult))
                        do(dve.tensor_tensor(Y, Y, bcast(rows[:, ROWS["ln_b"]], 1, NB), ALU.add))
                        do(dve.tensor_scalar(Y, Y, 0.0, None, ALU.max))

                        def outputs(b, k, r):
                            at_least(dve, s_yt, b - 1)
                            dve.tensor_copy(hb[:, k, :], PT[:, bass.ds(b, 1), 0:DD].rearrange("p a d -> p (a d)")).then_inc(s_yb, 1)
                            dve.wait_ge(s_m2, b + 1)
                            xb = X[:, bass.ds(b, 1), :].rearrange("p a d -> p (a d)")
                            dve.tensor_tensor(xb, xb, ps_w[:, k, 0:D], ALU.add).then_inc(s_x, 1)
                        steps(dve, NB, outputs, 2)
                        dve.wait_ge(s_x, NB)
                        dve.tensor_tensor(X[:], X[:], bcast(rows[:, ROWS["b2_l3"]], 1, NB), ALU.add).then_inc(s_x, 1)

                    @block.tensor
                    def _(pe):
                        pe.wait_ge(s_w, 32)

                        def hidden(b, k, r):
                            pe.wait_ge(s_hb, b + 1)
                            at_least(pe, s_hT, b - 1)
                            settle(pe)
                            pe.transpose(ps_t[0:D, k, 0:P], hb[:, k, 0:D], ident[:]).then_inc(s_t, 1)
                            pe.wait_ge(s_hT, b + 1)
                            at_least(pe, s_y, b - 1)
                            pe.matmul(ps_w[:, k, 0:DD], hT[:, k], wa[:], start=True, stop=True).then_inc(s_mm, 1)
                        steps(pe, NB, hidden, 2)
                        pe.wait_ge(s_y, NB)

                        def outputs(b, k, r):
                            pe.wait_ge(s_yb, b + 1)
                            at_least(pe, s_yT, b - 1)
                            pe.transpose(ps_t[:, k, 0:P], hb[:, k, :], ident[:]).then_inc(s_yt, 1)
                            pe.wait_ge(s_yT, b + 1)
                            at_least(pe, s_x, b - 1)
                            pe.matmul(ps_w[:, k, 0:D], yT[:, k], wb[:], start=True, stop=True).then_inc(s_m2, 1)
                        steps(pe, NB, outputs, 2)

                    @block.scalar
                    def _(act):
                        act.wait_ge(s_v, 2)

                        def hidden(b, k, r):
                            act.wait_ge(s_t, b + 1)
                            at_least(act, s_mm, b - 1)
                            act.copy(hT[0:D, k], ps_t[0:D, k, 0:P]).then_inc(s_hT, 1)
                        steps(act, NB, hidden, 2)
                        act.wait_ge(s_var, 1)
                        act.activation(st[:, 1], st[:, 0], ACT.Sqrt, bias=epsc[:], scale=1.0 / DD).then_inc(s_std, 1)

                        def outputs(b, k, r):
                            act.wait_ge(s_yt, b + 1)
                            at_least(act, s_m2, b - 1)
                            act.copy(yT[:, k], ps_t[:, k, 0:P]).then_inc(s_yT, 1)
                        steps(act, NB, outputs, 2)

        def store_rows(table):
            with phase() as ctx:
                s_o = sem_in(ctx, "h_stored")
                with nc.Block() as block:
                    @block.sync
                    def _(sp):
                        sp.dma_start(table.rearrange("(b p) d -> p b d", p=P), H[:]).then_inc(s_o, 16)
                        sp.wait_ge(s_o, 16)

        def store_early():
            with phase() as ctx:
                s_o = sem_in(ctx, "x_stored")
                with nc.Block() as block:
                    @block.sync
                    def _(sp):
                        sp.dma_start(out[0:P * (NBLK - 1), :].rearrange("(b p) d -> p b d", p=P), X[:, 0:NBLK - 1, :]).then_inc(s_o, 16)
                        sp.dma_start(out[P * (NBLK - 1):N, :], X[0:last_rows, NBLK - 1, :]).then_inc(s_o, 16)
                        sp.wait_ge(s_o, 32)

        layer_input(0)
        node_tables(0, wtab0, 2 * D, D, tab0)
        attention(0, 0, tab0, HEADS, D, w_e, D)
        if STOP == 2:
            return dict(ACC=ACC)
        finish_gat()
        if STOP == 3:
            return store_early()
        layer_input(1)
        node_tables(1, wtab1, 2 * D, D, tab1, fold=True)
        segment_max()
        finish_max()
        if STOP == 4:
            return store_early()
        layer_input(2)
        node_tables(2, wtab2, 2 * ATT + D, ATT + D, tab2)
        attention(2, 1, tab2, 1, ATT, watt_e, D)
        finish_gru()
        if STOP == 5:
            return store_early()
        layer_input(3)
        store_rows(tab3)
        segment_sum()
        finish_gine()


def laid_out(i):
    def f(name):
        return np.asarray(i[name])

    def zeros(*shape):
        return np.zeros(shape, np.float32)

    w1, att, hh = f("L1_gnn_W1"), f("L2_gnn_W_att1").T, f("L2_gnn_W_hh").T
    b_hh = f("L2_gnn_b_hh")
    return {
        "x": f("x"), "src": f("src"), "dst": f("dst"), "ea16": f("edge_attr_16"), "ea64": f("edge_attr_64"),
        "rowvec": np.concatenate([
            f("L0_gnn_att").reshape(-1), f("L0_gnn_bias"), f("L0_gnn_gamma"), f("L0_gnn_beta"), f("L1_gnn_b2"),
            f("L2_gnn_W_att2").reshape(-1), f("L2_gnn_b_att2"), f("L3_gnn_ln_g"), f("L3_gnn_ln_b"), f("L3_gnn_b2"),
            f("L3_gnn_eps")]),
        "wtab0": np.block([[f("L0_gnn_W_l"), f("L0_gnn_W_r")], [f("L0_gnn_b_l")[None], f("L0_gnn_b_r")[None]]]),
        "w_e": f("L0_gnn_W_e"),
        "wtab1": np.block([[w1[D:], w1[:D]], [zeros(1, D), f("L1_gnn_b1")[None]]]),
        "w2": f("L1_gnn_W2"),
        "wtab2": np.block([[att[D + DE:], f("L2_gnn_W_lin").T, att[:D]],
                           [zeros(1, ATT), f("L2_gnn_b_lin")[None], f("L2_gnn_b_att1")[None]]]),
        "watt_e": att[D:D + DE],
        "wgru": np.block([[f("L2_gnn_W_ih").T, zeros(D, D)], [hh[:, :2 * D], zeros(D, D), hh[:, 2 * D:]]]),
        "bgru": np.stack([np.concatenate([f("L2_gnn_b_ih"), zeros(D)]),
                          np.concatenate([b_hh[:2 * D], zeros(D), b_hh[2 * D:]])]),
        "w1": np.concatenate([f("L3_gnn_W1"), f("L3_gnn_b1")[None]]),
        "w3": f("L3_gnn_W2"),
    }


def kernel(**inputs):
    import concourse.bacc as bacc
    from concourse.bass_utils import run_bass_kernel_spmd as run

    nc = bacc.Bacc("TRN2", target_bir_lowering=False, num_devices=1)
    arrays, args = {}, {}
    for name, a in laid_out(inputs).items():
        a = np.ascontiguousarray(a)
        arrays[f"in_{name}"] = a
        args[name] = nc.dram_tensor(f"in_{name}", a.shape, mybir.dt.from_np(a.dtype), kind="ExternalInput").ap()
    shape = inputs["x"].shape
    out = nc.dram_tensor("out_x", shape, F32, kind="ExternalOutput").ap()
    program(nc, **args, out=out)
    r = run(nc, [arrays], core_ids=[0])
    return r.results[0]["out_x"]
```

```python
from contextlib import ExitStack, contextmanager

import numpy as np
import concourse.bass as bass
from concourse import mybir

F32 = mybir.dt.float32
BF16 = mybir.dt.bfloat16
I32 = mybir.dt.int32
ALU = mybir.AluOpType
ACT = mybir.ActivationFunctionType
AX = mybir.AxisListType

P = 128
D = 64
DE = 16
T = 4
GE = T * P
SLOTS = 4
ATT = 2 * D + DE
REC = 82
EA16, EA64 = 2, 2 + DE
BIG = 1.0e30
PAD = 2 * GE
FAR = 1 << 20
SORT_T = 5
HEADS = 4


def at_least(eng, sem, value):
    if not isinstance(value, int) or value > 0:
        eng.wait_ge(sem, value)


def steps(eng, n, body, unroll=SLOTS, end=0):
    rounds = n // unroll
    assert n % unroll == 0 and rounds > 1 + end
    for k in range(unroll):
        body(k, k, 0)
    with eng.Fori(1, rounds - end) as r:
        for k in range(unroll):
            body(r * unroll + k, k, r)
    for r in range(rounds - end, rounds):
        for k in range(unroll):
            body(r * unroll + k, k, r)


def before(g, k, r, by=1):
    return (g - by, (k - by) % SLOTS, r if k >= by else r - 1)


def after(g, k, r):
    return (g + 1, (k + 1) % SLOTS, r if k < SLOTS - 1 else r + 1)


def stage(f, lag, n, g, k, r, unroll=SLOTS):
    if not isinstance(g, int) or 0 <= g - lag < n:
        f(g - lag, (k - lag) % unroll, r + (k - lag) // unroll)


def pipeline(eng, n, body, late, unroll=SLOTS):
    steps(eng, n, body, unroll, end=1)
    for g in range(n, n + late):
        body(g, g % unroll, g // unroll)


def one_ahead(eng, n, *stages):
    def body(*at):
        for f, lag in stages:
            stage(f, lag, n, *at, unroll=2)
    for f, lag in stages:
        if lag < 0:
            f(0, 0, 0)
    pipeline(eng, n, body, max(0, *(lag for _, lag in stages)), unroll=2)


def is_group(g, n):
    return isinstance(g, int) and g == n


def settle(eng):
    eng.nop(nofuse=True)


def bcast(ap, axis, n):
    a = ap.unsqueeze(axis)
    shape = list(a.shape)
    shape[axis] = n
    return a.broadcast_to(shape)


ROWS = {}
for _name, _n in (("att", D), ("bias", D), ("gamma", D), ("beta", D), ("b2_l1", D), ("w_att2", ATT), ("b_att2", 1),
                  ("ln_g", 2 * D), ("ln_b", 2 * D), ("b2_l3", D), ("eps", 1)):
    ROWS[_name] = slice(ROWS["_end"] if ROWS else 0, (ROWS["_end"] if ROWS else 0) + _n)
    ROWS["_end"] = ROWS[_name].stop


def program(nc, x, src, dst, ea16, ea64, rowvec, wtab0, w_e, wtab1, w2, wtab2, watt_e, wgru, bgru, w1, w3, out):
    N, E = x.shape[0], src.shape[0]
    NBLK = -(-N // P)
    NB = NBLK + NBLK % 2
    assert E % (P * SORT_T) == 0 and NB < P and D == x.shape[1]
    NG = (E + NBLK * (GE - 1)) // GE
    NG = -(-NG // SLOTS) * SLOTS
    EPP = E // P
    last_rows = N - P * (NBLK - 1)

    with ExitStack() as top:
        def dram(name, shape, dt=F32):
            return nc.dram_tensor(name, shape, dt).ap()

        def sb_in(ctx, name, shape, dt=F32):
            return ctx.enter_context(nc.sbuf_tensor(name, shape, dt))

        def ps_in(ctx, name, shape, dt=F32):
            return ctx.enter_context(nc.psum_tensor(name, shape, dt))

        held = []

        def sem_in(ctx, name):
            held.append(nc.alloc_semaphore(name))
            return held[-1]

        @contextmanager
        def phase():
            with ExitStack() as ctx:
                yield ctx
            nc.clear_and_free_semaphores(held)
            held.clear()
            nc.all_engine_barrier()

        def sb(name, shape, dt=F32):
            return sb_in(top, name, shape, dt)

        keyp = dram("keyp", (1 + E + PAD,), I32)
        srcp = dram("srcp", (E + PAD,), I32)
        eap = dram("eap", (E + PAD, DE))
        rec = dram("rec", (NG * GE, REC), I32)
        tab0 = dram("tab0", (NB * P, D))
        tab1 = dram("tab1", (NB * P, D))
        tab2 = dram("tab2", (NB * P, ATT + D))
        tab3 = dram("tab3", (NB * P, D))

        ident = sb("ident", [P, P])
        iota_n = sb("iota_n", [P, P])
        ones = sb("ones", [P, P])
        identb = sb("identb", [P, P], BF16)
        iota_b = sb("iota_b", [P, P], BF16)
        X = sb("X", [P, NB, D])
        H = sb("H", [P, NB, D])
        blk = sb("blk", [P, 2, NG], I32)
        base_node = sb("base_node", [P, 2, NG])
        goff = sb("goff", [P, NG], I32)
        rows = sb("rows", [P, ROWS["_end"]])

        with phase() as ctx:
            ii = sb_in(ctx, "ii", [P, P], I32)
            z16 = sb_in(ctx, "z16", [P, PAD * DE // P])
            fk = sb_in(ctx, "fk", [P, 16], I32)
            s_id, s_x, s_fill, s_dma, s_ones, s_cast = (sem_in(ctx, n) for n in (
                "ident_zero", "x_zero", "pads_filled", "setup_dma", "ones_set", "iota_done"))
            block = ctx.enter_context(nc.Block())

            @block.gpsimd
            def _(pool):
                pool.memset(ident[:], 0.0).then_inc(s_id, 1)
                pool.wait_ge(s_id, 1)
                pool.affine_select(out=ident[:], in_=ident[:], compare_op=ALU.not_equal, fill=1.0, base=0,
                                   pattern=[[-1, P]], channel_multiplier=1).then_inc(s_id, 1)
                pool.iota(ii[:], [[1, P]], base=0, channel_multiplier=0).then_inc(s_id, 1)

            @block.vector
            def _(dve):
                dve.memset(X[:], 0.0).then_inc(s_x, 1)
                dve.memset(z16[:], 0.0).then_inc(s_fill, 1)
                dve.memset(fk[:, 0:8], FAR).then_inc(s_fill, 1)
                dve.memset(fk[:, 8:16], 0).then_inc(s_fill, 1)
                dve.memset(ones[:], 1.0).then_inc(s_ones, 1)
                dve.wait_ge(s_id, 3)
                dve.tensor_copy(iota_n[:], ii[:]).then_inc(s_cast, 1)
                dve.tensor_copy(iota_b[:], ii[:]).then_inc(s_cast, 1)
                dve.tensor_copy(identb[:], ident[:]).then_inc(s_cast, 1)

            @block.sync
            def _(sp):
                sp.dma_start(rows[:], rowvec.partition_broadcast(P)).then_inc(s_dma, 16)
                sp.wait_ge(s_x, 1)
                sp.dma_start(X[:, 0:NBLK - 1, :], x[0:P * (NBLK - 1), :].rearrange("(b p) d -> p b d", p=P)).then_inc(s_dma, 16)
                sp.dma_start(X[0:last_rows, NBLK - 1, :], x[P * (NBLK - 1):N, :]).then_inc(s_dma, 16)
                sp.dma_start(keyp[1:1 + E].rearrange("(a b) -> a b", a=16), dst.rearrange("(a b) -> a b", a=16)).then_inc(s_dma, 16)
                sp.dma_start(srcp[0:E].rearrange("(a b) -> a b", a=16), src.rearrange("(a b) -> a b", a=16)).then_inc(s_dma, 16)
                sp.dma_start(eap[0:E, :].rearrange("(a b) d -> a (b d)", a=64), ea16.rearrange("(a b) d -> a (b d)", a=64)).then_inc(s_dma, 16)
                sp.wait_ge(s_fill, 3)
                sp.dma_start(keyp[1 + E:1 + E + PAD].rearrange("(p c) -> p c", p=P), fk[:, 0:8]).then_inc(s_dma, 16)
                sp.dma_start(keyp[0:1].rearrange("(p c) -> p c", p=1), fk[0:1, 0:1]).then_inc(s_dma, 16)
                sp.dma_start(srcp[E:E + PAD].rearrange("(p c) -> p c", p=P), fk[:, 8:16]).then_inc(s_dma, 16)
                sp.dma_start(eap[E:E + PAD, :].rearrange("(p c) d -> p (c d)", p=P), z16[:]).then_inc(s_dma, 16)
                sp.wait_ge(s_dma, 16 * 10)

        with phase() as ctx:
            keys = [sb_in(ctx, f"keys{o}", [P, EPP], I32) for o in range(2)]
            ki = sb_in(ctx, "ki", [P, EPP], I32)
            hi = [sb_in(ctx, f"hi{o}", [P, EPP]) for o in range(2)]
            junk = sb_in(ctx, "junk", [P, EPP], BF16)
            cnt = sb_in(ctx, "cnt", [P, 2, P])
            small = [sb_in(ctx, f"small{o}", [P, 6, P]) for o in range(2)]
            gi = sb_in(ctx, "gi", [P, 2, P], I32)
            cols = sb_in(ctx, "cols", [P, 2, 2])
            jd = sb_in(ctx, "jd", [P, P])
            giota_i = sb_in(ctx, "giota_i", [P, NG], I32)
            giota = sb_in(ctx, "giota", [P, NG])
            past = sb_in(ctx, "past", [P, 2, NG])
            fo = sb_in(ctx, "fo", [P, NG])
            base = sb_in(ctx, "base", [P, P])
            ps_c = ps_in(ctx, "ps_c", [P, 2, P])
            ps_g = ps_in(ctx, "ps_g", [P, 2, 512])
            s_k, s_gi, s_hi, s_cnt, s_ct, s_sm, s_past, s_psg, s_tab = (sem_in(ctx, n) for n in (
                "keys_landed", "group_iota", "hi_steps", "counted", "counts_summed", "table_steps", "past_ready",
                "group_sums", "group_sums_read"))
            NSL = -(-NG // 512)
            RUN = 80
            rinit = sb_in(ctx, "rinit", [P, RUN, REC], I32)
            s_rz, s_rm, s_rec = (sem_in(ctx, n) for n in ("record_zeroed", "record_marked", "records_set"))
            n_rec = -(-NG * T // RUN)
            with nc.Block() as block:
                @block.sync
                def _(sp):
                    sp.dma_start(keys[0][:], dst.rearrange("(p c) -> p c", p=P)).then_inc(s_k, 16)
                    sp.dma_start(keys[1][:], src.rearrange("(p c) -> p c", p=P)).then_inc(s_k, 16)
                    sp.wait_ge(s_rm, 1)
                    places = rec.rearrange("(p r) c -> p r c", p=P)
                    for r in range(0, NG * T, RUN):
                        m = min(RUN, NG * T - r)
                        sp.dma_start(places[:, r:r + m, :], rinit[:, 0:m, :]).then_inc(s_rec, 16)

                @block.gpsimd
                def _(pool):
                    pool.iota(giota_i[:], [[1, NG]], base=0, channel_multiplier=0).then_inc(s_gi, 1)
                    pool.memset(rinit[:], 0).then_inc(s_rz, 1)
                    pool.wait_ge(s_rz, 1)
                    pool.memset(rinit[:, :, 0:1], -1).then_inc(s_rm, 1)

                @block.vector
                def _(dve):
                    nh = 0
                    dve.wait_ge(s_gi, 1)
                    dve.tensor_copy(giota[:], giota_i[:]).then_inc(s_hi, 1)
                    dve.memset(cnt[:], 0.0).then_inc(s_hi, 1)
                    dve.wait_ge(s_k, 32)
                    nh = 2
                    for o in range(2):
                        dve.wait_ge(s_hi, nh)
                        dve.tensor_scalar(ki[:], keys[o][:], 7, None, ALU.arith_shift_right).then_inc(s_hi, 1)
                        dve.wait_ge(s_hi, nh + 1)
                        dve.tensor_copy(hi[o][:], ki[:]).then_inc(s_hi, 1)
                        nh += 2
                    dve.wait_ge(s_hi, nh)
                    for o in range(2):
                        def count(b):
                            dve.tensor_scalar(junk[:], hi[o][:], iota_n[:, bass.ds(b, 1)], None, ALU.is_equal, ALU.add,
                                              accum_out=cnt[:, o, bass.ds(b, 1)]).then_inc(s_cnt, 1)

                        at_least(dve, s_cnt, o * NBLK)
                        count(0)
                        with dve.Fori(1, NBLK) as b:
                            dve.wait_ge(s_cnt, b + o * NBLK)
                            count(b)
                    ns = 0
                    dve.wait_ge(s_ct, 1)

                    def do(ins):
                        nonlocal ns
                        ns += 1
                        ins.then_inc(s_sm, 1)
                        dve.wait_ge(s_sm, ns)

                    for o in range(2):
                        c, gf, gend, pad, padsum, at = (small[o][:, k, :] for k in range(6))
                        do(dve.tensor_copy(c, ps_c[:, o, :]))
                        do(dve.tensor_scalar(gf, c, float(GE - 1), None, ALU.add))
                        do(dve.tensor_copy(gi[:, o, :], gf))
                        do(dve.tensor_scalar(gi[:, o, :], gi[:, o, :], 9, None, ALU.arith_shift_right))
                        do(dve.tensor_copy(gf, gi[:, o, :]))
                        do(dve.tensor_tensor_scan(gend, gf, gf, 0.0, ALU.add, ALU.bypass))
                        do(dve.scalar_tensor_tensor(pad, gf, float(GE), c, ALU.mult, ALU.subtract))
                        do(dve.tensor_tensor(at, gend, gf, ALU.subtract))
                        do(dve.tensor_scalar(at, at, float(GE), None, ALU.mult))
                        do(dve.tensor_tensor_reduce(jd[:], gend, ident[:], 1.0, 0.0, ALU.mult, ALU.add, cols[:, o, 0:1]))
                        do(dve.tensor_tensor_reduce(jd[:], pad, ident[:], 1.0, 0.0, ALU.mult, ALU.add, cols[:, o, 1:2]))
                        do(dve.tensor_scalar(past[:, o, :], giota[:], cols[:, o, 0:1], None, ALU.is_ge))
                    do(dve.tensor_copy(base[:], small[1][:, 5, :]))
                    dve.memset(jd[:], 1.0).then_inc(s_past, 1)
                    nt = 0
                    for o in range(2):
                        for c in range(NSL):
                            a, b = 512 * c, min(NG, 512 * c + 512)
                            nt += 1
                            dve.wait_ge(s_psg, nt)
                            do(dve.tensor_scalar(base_node[:, o, a:b], ps_g[:, nt % 2, 0:b - a], float(NB), None, ALU.min))
                            do(dve.tensor_copy(blk[:, o, a:b], base_node[:, o, a:b]))
                            dve.tensor_scalar(base_node[:, o, a:b], base_node[:, o, a:b], float(P), None, ALU.mult).then_inc(s_tab, 1)
                    for c in range(NSL):
                        a, b = 512 * c, min(NG, 512 * c + 512)
                        nt += 1
                        dve.wait_ge(s_psg, nt)
                        do(dve.scalar_tensor_tensor(fo[:, a:b], giota[:, a:b], float(GE), ps_g[:, nt % 2, 0:b - a], ALU.mult, ALU.subtract))
                        do(dve.tensor_scalar(fo[:, a:b], fo[:, a:b], float(E), None, ALU.min))
                        dve.tensor_copy(goff[:, a:b], fo[:, a:b]).then_inc(s_tab, 1)

                @block.tensor
                def _(pe):
                    pe.wait_ge(s_cnt, 2 * NBLK)
                    pe.matmul(ps_c[:].rearrange("p o b -> p (o b)"), ones[:], cnt[:].rearrange("p o b -> p (o b)"), start=True, stop=True).then_inc(s_ct, 1)
                    pe.wait_ge(s_past, 1)
                    nt = 0
                    for o, w in ((0, None), (1, None), (0, 1)):
                        for c in range(NSL):
                            a, b = 512 * c, min(NG, 512 * c + 512)
                            nt += 1
                            at_least(pe, s_tab, nt - 2)
                            lhs = ones[:] if w is None else cols[:, 0, 1:2].broadcast_to([P, P])
                            pe.matmul(ps_g[:, nt % 2, 0:b - a], lhs, past[:, o, a:b], start=True, stop=True).then_inc(s_psg, 1)

            tri = sb_in(ctx, "tri", [P, P], BF16)
            oneb = sb_in(ctx, "oneb", [P, P], BF16)
            oh = sb_in(ctx, "s_oh", [P, 2, SORT_T, NB], BF16)
            tmp = sb_in(ctx, "s_tmp", [P, SORT_T, NB])
            posf = sb_in(ctx, "posf", [P, SORT_T])
            SS = 5
            posi = sb_in(ctx, "posi", [P, SS, SORT_T], I32)
            rb = sb_in(ctx, "rb", [P, SS, SORT_T, REC])
            ps_r = ps_in(ctx, "ps_r", [P, 2, 512])
            ps_s = ps_in(ctx, "ps_s", [P, 2, 512])
            NSTEP = EPP // SORT_T
            s_tri = sem_in(ctx, "tri_ready")
            s_ld = [sem_in(ctx, f"features_landed{k}") for k in range(SS)]
            s_sc = [sem_in(ctx, f"scattered{k}") for k in range(SS)]
            s_oh, s_r, s_add, s_mul, s_red, s_pos, s_base, s_key = (sem_in(ctx, n) for n in (
                "sort_onehot", "sort_ranks", "sort_added", "sort_masked", "sort_reduced", "places_ready", "base_moved", "keys_in_record"))
            ea16v = ea16.rearrange("(p c) d -> p c d", p=P)
            ea64v = ea64.rearrange("(p c) d -> p c d", p=P)
            rbi = rb[:].bitcast(I32)
            with nc.Block() as block:
                @block.sync
                def _(sp):
                    def body(g, k, r):
                        at_least(sp, s_sc[k], r * (16 * SORT_T))
                        settle(sp)
                        sp.dma_start(rb[:, k, :, EA16:EA16 + DE], ea16v[:, bass.ds(g * SORT_T, SORT_T), :]).then_inc(s_ld[k], 16)
                        sp.dma_start(rb[:, k, :, EA64:EA64 + D], ea64v[:, bass.ds(g * SORT_T, SORT_T), :]).then_inc(s_ld[k], 16)
                    steps(sp, NSTEP, body, SS)

                @block.gpsimd
                def _(pool):
                    pool.memset(oneb[:], 1.0).then_inc(s_tri, 1)
                    pool.wait_ge(s_tri, 1)
                    pool.affine_select(out=tri[:], in_=oneb[:], compare_op=ALU.is_gt, fill=0.0, base=0,
                                       pattern=[[1, P]], channel_multiplier=-1).then_inc(s_tri, 1)
                    pool.wait_ge(s_rec, 16 * n_rec)

                    def body(g, k, r):
                        pool.wait_ge(s_ld[k], r * 32 + 32)
                        pool.wait_ge(s_pos, g + 1)
                        settle(pool)
                        for t in range(SORT_T):
                            pool.indirect_dma_start(rec, bass.IndirectOffsetOnAxis(ap=posi[:, k, t:t + 1], axis=0),
                                                    rbi[:, k, t, :], None).then_inc(s_sc[k], 16)
                    steps(pool, NSTEP, body, SS)
                    for k in range(SS):
                        pool.wait_ge(s_sc[k], 16 * SORT_T * (NSTEP // SS))

                @block.vector
                def _(dve):
                    def body(g, k, r):
                        cols_g = bass.ds(g * SORT_T, SORT_T)
                        at_least(dve, s_sc[k], r * (16 * SORT_T))
                        dve.tensor_copy(rbi[:, k, :, 0:1], bcast(keys[1][:, cols_g], 2, 1)).then_inc(s_key, 1)
                        dve.tensor_copy(rbi[:, k, :, 1:2], bcast(keys[0][:, cols_g], 2, 1)).then_inc(s_key, 1)
                        at_least(dve, s_r, g)
                        dve.tensor_tensor(oh[:, 0], bcast(iota_n[:, 0:NB], 1, SORT_T), bcast(hi[1][:, cols_g], 2, NB),
                                          ALU.is_equal).then_inc(s_oh, 1)
                        dve.wait_ge(s_r, g + 1)
                        at_least(dve, s_base, g)
                        dve.tensor_tensor(tmp[:], ps_r[:, 0, 0:SORT_T * NB].rearrange("p (t b) -> p t b", t=SORT_T),
                                          bcast(base[:, 0:NB], 1, SORT_T), ALU.add).then_inc(s_add, 1)
                        dve.wait_ge(s_add, g + 1)
                        dve.tensor_tensor(base[:, 0:NB], base[:, 0:NB], ps_s[:, 0, 0:NB], ALU.add).then_inc(s_base, 1)
                        dve.tensor_tensor(tmp[:], tmp[:], oh[:, 0], ALU.mult).then_inc(s_mul, 1)
                        dve.wait_ge(s_mul, g + 1)
                        dve.tensor_reduce(posf[:], tmp[:], AX.X, ALU.add).then_inc(s_red, 1)
                        dve.wait_ge(s_red, g + 1)
                        dve.wait_ge(s_key, g * 2 + 2)
                        dve.tensor_copy(posi[:, k, :], posf[:]).then_inc(s_pos, 1)
                    steps(dve, NSTEP, body, SS)

                @block.tensor
                def _(pe):
                    pe.wait_ge(s_tri, 2)

                    def body(g, k, r):
                        pe.wait_ge(s_oh, g + 1)
                        at_least(pe, s_base, g)
                        for t in range(SORT_T):
                            pe.matmul(ps_r[:, 0, t * NB:t * NB + NB], tri[:], oh[:, 0, t], start=True, stop=(t == 0))
                            for u in range(t):
                                pe.matmul(ps_r[:, 0, t * NB:t * NB + NB], oneb[:], oh[:, 0, u], start=False, stop=(u == t - 1))
                        for t in range(SORT_T):
                            mm = pe.matmul(ps_s[:, 0, 0:NB], oneb[:], oh[:, 0, t], start=(t == 0), stop=(t == SORT_T - 1))
                        mm.then_inc(s_r, 1)
                    steps(pe, NSTEP, body, SS)


        ACC = sb("ACC", [P, NB + 1, HEADS * (D // HEADS + 1)])
        PT = sb("PT", [P, NB + 1, 3, ATT], BF16)
        room = PT[:].rearrange("p b s c -> p b (s c)").bitcast(F32)

        def in_place_of_h(ctx, *buffers):
            views, used = [], 0
            lent = SLOTS * T * sum(width for _, width in buffers) <= NB * D
            for name, width in buffers:
                size = SLOTS * T * width
                views.append(H[:].rearrange("p b d -> p (b d)")[:, used:used + size].rearrange("p (k t c) -> p k t c", k=SLOTS, t=T)
                             if lent else sb_in(ctx, name, [P, SLOTS, T, width]))
                used += size
            return views

        def chain(eng, sem):
            n = 0

            def do(ins):
                nonlocal n
                n += 1
                ins.then_inc(sem, 1)
                eng.wait_ge(sem, n)
            return do

        def layer_input(layer):
            with phase() as ctx:
                st = sb_in(ctx, f"ln_stat{layer}", [P, 4, NB])
                epsc = sb_in(ctx, f"ln_eps{layer}", [P, 1])
                s_v, s_var, s_std = (sem_in(ctx, f"{n}{layer}") for n in ("ln_steps", "ln_var_ready", "ln_std_ready"))
                sq = room[:, 0:NB, 0:D]
                with nc.Block() as block:
                    @block.vector
                    def _(dve):
                        do = chain(dve, s_v)
                        do(dve.memset(epsc[:], 1e-5))
                        do(dve.tensor_reduce(st[:, 0, :], X[:], AX.X, ALU.add))
                        do(dve.tensor_scalar(st[:, 0, :], st[:, 0, :], 1.0 / D, None, ALU.mult))
                        do(dve.tensor_tensor(H[:], X[:], bcast(st[:, 0, :], 2, D), ALU.subtract))
                        do(dve.tensor_tensor(sq, H[:], H[:], ALU.mult))
                        dve.tensor_reduce(st[:, 1, :], sq, AX.X, ALU.add).then_inc(s_var, 1)
                        do(dve.memset(ACC[:], 0.0))
                        dve.wait_ge(s_std, 1)
                        do(dve.reciprocal(st[:, 3, :], st[:, 2, :]))
                        do(dve.tensor_tensor(H[:], H[:], bcast(st[:, 3, :], 2, D), ALU.mult))
                        do(dve.tensor_scalar(H[:], H[:], 0.0, None, ALU.max))
                        do(dve.memset(PT[:], 0.0))

                    @block.scalar
                    def _(act):
                        act.wait_ge(s_var, 1)
                        act.activation(st[:, 2, :], st[:, 1, :], ACT.Sqrt, bias=epsc[:], scale=1.0 / D).then_inc(s_std, 1)

        def node_tables(layer, weights, width, n_gather, table, fold=False):
            n_pt = width - n_gather
            with phase() as ctx:
                w = sb_in(ctx, f"w_tab{layer}", [D + 1, width])
                hb = sb_in(ctx, f"hb{layer}", [P, 2, D])
                hT = sb_in(ctx, f"hT{layer}", [D + 1, 2, P])
                staged = sb_in(ctx, f"staged{layer}", [P, 2, n_gather])
                rest = sb_in(ctx, f"rest{layer}", [P, n_pt])
                ps_t = ps_in(ctx, f"ps_t{layer}", [P, 2, 512])
                ps_w = ps_in(ctx, f"ps_w{layer}", [P, 2, 512])
                s_w, s_one, s_fold, s_hb, s_t, s_hT, s_mm, s_st, s_p0, s_r, s_p1, s_pt = (sem_in(ctx, f"{n}{layer}") for n in (
                    "weights_landed", "ones_row", "weights_folded", "block_copied", "block_turned", "turned_copied", "rows_ready", "rows_staged",
                    "first_part", "first_rest", "second_part", "rows_kept"))
                s_out = [sem_in(ctx, f"rows_stored{layer}_{k}") for k in range(2)]
                with nc.Block() as block:
                    @block.sync
                    def _(sp):
                        sp.dma_start(w[:], weights).then_inc(s_w, 16)

                        def body(b, k, r):
                            sp.wait_ge(s_st, b + 1)
                            settle(sp)
                            sp.dma_start(table[bass.ds(b * P, P), :], staged[:, k, :]).then_inc(s_out[k], 16)
                        steps(sp, NB, body, 2)
                        for k in range(2):
                            sp.wait_ge(s_out[k], 16 * (NB // 2))

                    @block.vector
                    def _(dve):
                        dve.memset(hT[D:D + 1, :, :], 1.0).then_inc(s_one, 1)
                        if fold:
                            dve.wait_ge(s_w, 16)
                            dve.tensor_tensor(w[0:D, D:2 * D], w[0:D, D:2 * D], w[0:D, 0:D], ALU.subtract).then_inc(s_fold, 1)

                        def copy(b, k, r):
                            at_least(dve, s_t, b - 1)
                            dve.tensor_copy(hb[:, k, :], H[:, bass.ds(b, 1), :].rearrange("p a d -> p (a d)")).then_inc(s_hb, 1)

                        def keep(b, k, r):
                            dve.wait_ge(s_st, b + 1)
                            part = [PT[:, bass.ds(b, 1), i, 0:n_pt].rearrange("p a d -> p (a d)") for i in range(3)]
                            settle(dve)
                            dve.tensor_copy(part[0], ps_w[:, k, n_gather:width]).then_inc(s_p0, 1)
                            dve.wait_ge(s_p0, b + 1)
                            at_least(dve, s_pt, b)
                            dve.tensor_tensor(rest[:], ps_w[:, k, n_gather:width], part[0], ALU.subtract).then_inc(s_r, 1)
                            dve.wait_ge(s_r, b + 1)
                            settle(dve)
                            dve.tensor_copy(part[1], rest[:]).then_inc(s_p1, 1)
                            dve.wait_ge(s_p1, b + 1)
                            dve.tensor_tensor(part[2], rest[:], part[1], ALU.subtract).then_inc(s_pt, 1)
                        one_ahead(dve, NB, (copy, -1), (keep, 0))

                    @block.tensor
                    def _(pe):
                        pe.wait_ge(s_one, 1)
                        pe.wait_ge(s_w, 16)
                        at_least(pe, s_fold, int(fold))

                        def body(b, k, r):
                            pe.wait_ge(s_hb, b + 1)
                            at_least(pe, s_hT, b - 1)
                            settle(pe)
                            pe.transpose(ps_t[0:D, k, 0:P], hb[:, k, :], ident[:]).then_inc(s_t, 1)
                            pe.wait_ge(s_hT, b + 1)
                            at_least(pe, s_st, b - 1)
                            at_least(pe, s_pt, b - 1)
                            pe.matmul(ps_w[:, k, 0:width], hT[:, k, :], w[:], start=True, stop=True).then_inc(s_mm, 1)
                        steps(pe, NB, body, 2)

                    @block.scalar
                    def _(act):
                        def body(b, k, r):
                            act.wait_ge(s_t, b + 1)
                            at_least(act, s_mm, b - 1)
                            act.copy(hT[0:D, k, :], ps_t[0:D, k, 0:P]).then_inc(s_hT, 1)
                            act.wait_ge(s_mm, b + 1)
                            at_least(act, s_out[k], r * 16)
                            act.copy(staged[:, k, :], ps_w[:, k, 0:n_gather]).then_inc(s_st, 1)
                        steps(act, NB, body, 2)

        def attention(layer, order, table, heads, width, we, n_val):
            R = table.shape[1]
            VC = n_val // heads + 1
            v0 = R - n_val
            banks = 1 if T * width <= 512 else 2
            tpb = T // banks
            att = rows[:, ROWS["att"]] if layer == 0 else rows[:, ROWS["w_att2"]]
            with phase() as ctx:
                def sbl(name, shape, dt=F32):
                    return sb_in(ctx, f"{name}{layer}", shape, dt)

                def seml(name):
                    return sem_in(ctx, f"{name}{layer}")

                w = sbl("w_ea", [T * DE, T, width])
                if layer == 0:
                    key = sbl("key", [P, SLOTS, T, 1], I32)
                    idx = sbl("idx", [P, SLOTS, T, 1], I32)
                    ea = sbl("ea", [P, SLOTS, T, DE])
                    n_loads = 3
                else:
                    rs = sbl("rs", [P, SLOTS, T, REC], I32)
                    key, idx = rs[:, :, :, 0:1], rs[:, :, :, 1:2]
                    ea_in = rs[:].bitcast(F32)[:, :, :, EA16:EA16 + DE]
                    ea = sbl("ea", [P, SLOTS, T, DE])
                    n_loads = 1
                G, oh = in_place_of_h(ctx, (f"G{layer}", R), (f"oh{layer}", P))
                lo = sbl("lo", [P, T])
                ohb = sbl("ohb", [P, 2, T, P], BF16)
                ohN = sbl("ohN", [P, SLOTS, T, P], BF16)
                pen = sbl("pen", [P, SLOTS, T, P], BF16)
                eaT = sbl("eaT", [T * DE, P])
                z = sbl("z", [P, T, width])
                zs = sbl("zs", [P, T, width]) if layer == 0 else None
                lg = sbl("lg", [P, 2, T, heads])
                lgp = sbl("lgp", [P, T, 2, heads], BF16)
                lgT = sbl("lgT", [2 * heads, T * P], BF16)
                sel = sbl("sel", [2 * heads, heads, P], BF16)
                junk = sbl("junk", [P, 2, T, P], BF16)
                gm = sbl("gm", [P, heads])
                mn = sbl("mn", [P, heads])
                mnp = sbl("mnp", [P, 2, heads], BF16)
                df = sbl("df", [P, heads])
                corr = sbl("corr", [P, 2, heads])
                dd = sbl("dd", [P, T, heads])
                ss = sbl("ss", [P, T, heads])
                V = sbl("V", [P, T, heads, VC])
                M = sbl("M", [P, NB + 1, heads])
                ps_oh = ps_in(ctx, f"ps_oh{layer}", [P, 2 * T, P], BF16)
                ps_ea = ps_in(ctx, f"ps_ea{layer}", [P, 512])
                ps_lT = ps_in(ctx, f"ps_lT{layer}", [P, 2 * T * P], BF16)
                ps_z = ps_in(ctx, f"ps_z{layer}", [P, banks, 512])
                n_lb = min(heads, 2)
                ps_lb = ps_in(ctx, f"ps_lb{layer}", [P, n_lb, T, P])
                ps_m = ps_in(ctx, f"ps_m{layer}", [P, 512])
                ps_a = ps_in(ctx, f"ps_a{layer}", [P, 512])
                zv = [ps_z[:, b, 0:tpb * width].rearrange("p (t c) -> p t c", t=tpb) for b in range(banks)]

                s_w, s_mi, s_eac = seml("ea_weights"), seml("maxima_set"), seml("ea_together")
                s_ld = [seml(f"edges_landed{k}_") for k in range(SLOTS)]
                s_g = [seml(f"gathered{k}_") for k in range(SLOTS)]
                (s_wz, s_lo, s_oh, s_oh32, s_ohT, s_ohN, s_pen, s_eaP, s_eaT, s_z, s_zs, s_act, s_mul, s_lg0, s_lg, s_lp0, s_lp, s_lT, s_lTc, s_sel, s_mn, s_df, s_mb, s_corr,
                 s_me, s_d0, s_d, s_p, s_V, s_acc, s_sc, s_done, s_mh, s_ml) = (seml(n) for n in (
                    "ea_weights_zero", "local_key", "onehot", "onehot_32", "onehot_turned", "onehot_nodes", "penalty", "ea_turned", "ea_ready", "edge_rows",
                    "slope_applied", "activated", "weighted", "score_sum", "score", "score_high", "score_low", "score_turned", "score_rows", "selector", "new_max", "max_step", "max_stored", "rescale",
                    "edge_max", "score_less_max", "exponent", "weight", "values", "group_sums", "acc_rescaled", "group_done", "max_high", "max_low"))
                s_lb = [seml(f"scores_spread{h}_") for h in range(heads)]
                s_gm = [seml(f"group_max{h}_") for h in range(heads)]

                with nc.Block() as block:
                    @block.sync
                    def _(sp):
                        sp.wait_ge(s_wz, 1)
                        for t in range(T):
                            sp.dma_start(w[t * DE:(t + 1) * DE, t, :], we).then_inc(s_w, 16)

                        def body(g, k, r):
                            at_least(sp, s_lo, g - SLOTS + 1)
                            settle(sp)
                            at_least(sp, s_g[k], r * (16 * T))
                            at_least(sp, s_eac if layer else s_eaP, g - SLOTS + 1)
                            settle(sp)
                            if layer == 0:
                                e = sp.value_load(goff[0:1, bass.ds(g, 1)], min_val=0, max_val=E)
                                sp.dma_start(key[:, k, :, 0], keyp[bass.ds(e + 1, GE)].rearrange("(p t) -> p t", p=P)).then_inc(s_ld[k], 16)
                                sp.dma_start(idx[:, k, :, 0], srcp[bass.ds(e, GE)].rearrange("(p t) -> p t", p=P)).then_inc(s_ld[k], 16)
                                sp.dma_start(ea[:, k], eap[bass.ds(e, GE), :].rearrange("(p t) c -> p t c", p=P)).then_inc(s_ld[k], 16)
                            else:
                                sp.dma_start(rs[:, k], rec[bass.ds(g * GE, GE), :].rearrange("(p t) c -> p t c", p=P)).then_inc(s_ld[k], 16)
                        steps(sp, NG, body)

                    @block.gpsimd
                    def _(pool):
                        def body(g, k, r):
                            pool.wait_ge(s_ld[k], (r + 1) * (16 * n_loads))
                            if layer:
                                at_least(pool, s_eaP, g - SLOTS + 1)
                                settle(pool)
                                pool.tensor_copy(ea[:, k], ea_in[:, k]).then_inc(s_eac, 1)
                            at_least(pool, s_V, g - SLOTS + 1)
                            settle(pool)
                            for t in range(T):
                                pool.indirect_dma_start(G[:, k, t, :], None, table,
                                                        bass.IndirectOffsetOnAxis(ap=idx[:, k, t, :], axis=0)).then_inc(s_g[k], 16)
                        steps(pool, NG, body)

                    @block.vector
                    def _(dve):
                        dve.memset(w[:], 0.0).then_inc(s_wz, 1)
                        dve.tensor_tensor(sel[:], bcast(ident[0:2 * heads, 0:heads], 2, P), bcast(ident[0:2 * heads, heads:2 * heads], 2, P),
                                          ALU.add).then_inc(s_sel, 1)
                        dve.memset(M[:], -BIG).then_inc(s_mi, 1)
                        dve.wait_ge(s_mi, 1)

                        def local_keys(g, k, r):
                            dve.wait_ge(s_ld[k], (r + 1) * (16 * n_loads))
                            at_least(dve, s_oh, g)
                            dve.tensor_scalar(lo[:], key[:, k, :, 0], base_node[:, order, bass.ds(g, 1)], None, ALU.subtract).then_inc(s_lo, 1)

                        def onehot(g, k, r):
                            q = k % 2
                            dve.wait_ge(s_lo, g + 1)
                            at_least(dve, s_ohT, g - 1)
                            at_least(dve, s_oh32, g - 1)
                            for t in range(T):
                                ins = dve.tensor_scalar(ohb[:, q, t, :], iota_b[:], lo[:, t:t + 1], None, ALU.is_equal)
                            ins.then_inc(s_oh, 1)

                        def scores(g, k, r):
                            q = k % 2
                            if layer == 0:
                                dve.wait_ge(s_zs, g + 1)
                                at_least(dve, s_lg, g)
                                dve.tensor_tensor(z[:], zs[:], zv[0], ALU.max).then_inc(s_act, 1)
                                dve.wait_ge(s_act, g + 1)
                                dve.tensor_tensor(z[:], z[:], bcast(att, 1, T), ALU.mult).then_inc(s_mul, 1)
                                dve.wait_ge(s_mul, g + 1)
                                at_least(dve, s_d0, g - 1)
                                dve.tensor_reduce(lg[:, q], z[:].rearrange("p t (h c) -> p t h c", h=heads), AX.X, ALU.add).then_inc(s_lg, 1)
                            else:
                                dve.wait_ge(s_z, g + 1)
                                dve.wait_ge(s_g[k], (r + 1) * (16 * T))
                                at_least(dve, s_lg0, g)
                                for b in range(banks):
                                    ts = slice(b * tpb, (b + 1) * tpb)
                                    ins = dve.tensor_tensor(z[:, ts, :], zv[b], G[:, k, ts, 0:width], ALU.add)
                                ins.then_inc(s_act, 1)
                                dve.wait_ge(s_act, g + 1)
                                dve.scalar_tensor_tensor(z[:], z[:], 0.0, bcast(att, 1, T), ALU.max, ALU.mult).then_inc(s_mul, 1)
                                dve.wait_ge(s_mul, g + 1)
                                at_least(dve, s_lg, g)
                                dve.tensor_reduce(ss[:], z[:].rearrange("p t (h c) -> p t h c", h=heads), AX.X, ALU.add).then_inc(s_lg0, 1)

                        def split(g, k, r):
                            dve.wait_ge(s_lp0, g + 1)
                            dve.tensor_tensor(lgp[:, :, 1, :], lg[:, k % 2], lgp[:, :, 0, :], ALU.subtract).then_inc(s_lp, 1)

                        def block_of(g):
                            return dve.value_load(blk[0:1, order, bass.ds(g, 1)], min_val=0, max_val=NB)

                        def maxima(g, k, r):
                            m_old = M[:, bass.ds(blocks[1], 1), :].rearrange("p a h -> p (a h)")
                            for h in range(heads):
                                dve.wait_ge(s_lb[h], g + 1)
                                if h == 0:
                                    dve.wait_ge(s_pen, g + 1)
                                    at_least(dve, s_mn, g)
                                if h >= 2:
                                    dve.wait_ge(s_gm[h - 2], g + 1)
                                settle(dve)
                                dve.tensor_tensor_reduce(junk[:, h % 2].rearrange("p t e -> p (t e)"), ps_lb[:, h % n_lb].rearrange("p t e -> p (t e)"),
                                                         pen[:, k].rearrange("p t e -> p (t e)"), 1.0, -BIG, ALU.add, ALU.max,
                                                         gm[:, h:h + 1]).then_inc(s_gm[h], 1)
                            for h in range(max(0, heads - 2), heads):
                                dve.wait_ge(s_gm[h], g + 1)
                            at_least(dve, s_mb, g)
                            dve.tensor_tensor(mn[:], m_old, gm[:], ALU.max).then_inc(s_mn, 1)
                            dve.wait_ge(s_mn, g + 1)
                            at_least(dve, s_me, g)
                            dve.tensor_copy(mnp[:, 0], mn[:]).then_inc(s_mh, 1)
                            at_least(dve, s_corr, g)
                            dve.tensor_tensor(df[:], m_old, mn[:], ALU.subtract).then_inc(s_df, 1)
                            dve.wait_ge(s_df, g + 1)
                            dve.tensor_tensor(m_old, mn[:], mn[:], ALU.max).then_inc(s_mb, 1)
                            dve.wait_ge(s_mh, g + 1)
                            dve.tensor_tensor(mnp[:, 1], mn[:], mnp[:, 0], ALU.subtract).then_inc(s_ml, 1)

                        def exponents(g, k, r):
                            q = k % 2
                            dve.wait_ge(s_me, g + 1)
                            at_least(dve, s_p, g)
                            dve.tensor_tensor(dd[:].rearrange("p t h -> p (t h)"), lg[:, q].rearrange("p t h -> p (t h)"),
                                              ps_m[:, 0:T * heads], ALU.subtract).then_inc(s_d0, 1)
                            dve.wait_ge(s_d0, g + 1)
                            dve.tensor_scalar(dd[:], dd[:], 1.0, None, ALU.min).then_inc(s_d, 1)

                        def values(g, k, r):
                            dve.wait_ge(s_p, g + 1)
                            dve.tensor_tensor(V[:, :, :, 0:VC - 1], G[:, k, :, v0:R].rearrange("p t (h c) -> p t h c", h=heads),
                                              V[:, :, :, VC - 1:VC].broadcast_to([P, T, heads, VC - 1]), ALU.mult).then_inc(s_V, 1)

                        def keep(g, k, r):
                            acc = ACC[:, bass.ds(blocks[0], 1), 0:heads * VC].rearrange("p a (h c) -> p (a h) c", h=heads)
                            dve.wait_ge(s_corr, g + 1)
                            at_least(dve, s_done, g)
                            dve.tensor_tensor(acc, acc, bcast(corr[:, k % 2], 2, VC), ALU.mult).then_inc(s_sc, 1)
                            dve.wait_ge(s_sc, g + 1)
                            dve.wait_ge(s_acc, g + 1)
                            dve.tensor_tensor(acc, acc, ps_a[:, 0:heads * VC].rearrange("p (h c) -> p h c", h=heads), ALU.add).then_inc(s_done, 1)

                        blocks = [None, None]

                        def body(g, k, r):
                            at = (g, k, r)
                            stage(scores, 0, NG, *at)
                            stage(onehot, -2, NG, *at)
                            if k and not is_group(g, 1):
                                blocks[0] = blocks[1]
                            elif not k and not is_group(g, 0):
                                blocks[0] = block_of(g - 2)
                            if not is_group(g, 0) and not is_group(g, NG + 1):
                                blocks[1] = block_of(g - 1)
                            stage(split, 0, NG, *at)
                            stage(maxima, 1, NG, *at)
                            stage(keep, 2, NG, *at)
                            stage(exponents, 1, NG, *at)
                            stage(local_keys, -3, NG, *at)
                            stage(values, 1, NG, *at)
                        for g in range(2):
                            local_keys(g, g, 0)
                            onehot(g, g, 0)
                        local_keys(2, 2, 0)
                        pipeline(dve, NG, body, 2)

                    @block.tensor
                    def _(pe):
                        pe.wait_ge(s_w, 16 * T)
                        pe.wait_ge(s_sel, 1)

                        def turn(g, k, r):
                            q = k % 2
                            pe.wait_ge(s_oh, g + 1)
                            at_least(pe, s_pen, g)
                            for t in range(T):
                                mm = pe.transpose(ps_oh[:, t, :], ohb[:, q, t, :], identb[:])
                            mm.then_inc(s_ohT, 1)
                            if layer == 0:
                                pe.wait_ge(s_ld[k], (r + 1) * (16 * n_loads))
                            else:
                                pe.wait_ge(s_eac, g + 1)
                            at_least(pe, s_eaT, g)
                            settle(pe)
                            mm = pe.transpose(ps_ea[0:T * DE, 0:P], ea[:, k], ident[:])
                            mm.then_inc(s_eaP, 1)

                        def turn_scores(g, k, r):
                            pe.wait_ge(s_lp, g + 1)
                            at_least(pe, s_lTc, g)
                            for t in range(T):
                                mm = pe.transpose(ps_lT[0:2 * heads, t * P:(t + 1) * P], lgp[:, t].rearrange("p a h -> p (a h)"), identb[:])
                            mm.then_inc(s_lT, 1)

                        def spread(g, k, r, some):
                            pe.wait_ge(s_lTc, g + 1)
                            for h in some:
                                if h >= n_lb:
                                    pe.wait_ge(s_gm[h - n_lb], g + 1)
                                else:
                                    at_least(pe, s_gm[max(j for j in range(heads) if j % n_lb == h)], g)
                                pe.matmul(ps_lb[:, h % n_lb].rearrange("p t e -> p (t e)"), sel[:, h, :], lgT[:], start=True, stop=True).then_inc(s_lb[h], 1)

                        def feature_rows(g, k, r):
                            pe.wait_ge(s_eaT, g + 1)
                            at_least(pe, s_act, g)
                            for b in range(banks):
                                pe.matmul(ps_z[:, b, 0:tpb * width], eaT[:], w[:, b * tpb:(b + 1) * tpb, :].rearrange("p t c -> p (t c)"),
                                          start=True, stop=False)

                        def key_rows(g, k, r):
                            blk_g = pe.value_load(blk[0:1, order, bass.ds(g, 1)], min_val=0, max_val=NB)
                            pe.wait_ge(s_ohN, g + 1)
                            for t in range(T):
                                for i in range(3):
                                    mm = pe.matmul(zv[t // tpb][:, t % tpb, :], ohN[:, k, t, :], PT[:, bass.ds(blk_g, 1), i, 0:width].rearrange("p a c -> p (a c)"),
                                                   start=False, stop=(layer != 0 and i == 2 and t % tpb == tpb - 1))
                            if layer != 0:
                                mm.then_inc(s_z, 1)

                        def gathered_rows(g, k, r):
                            pe.wait_ge(s_g[k], (r + 1) * (16 * T))
                            pe.matmul(zv[0], ident[:], G[:, k, :, 0:width], start=False, stop=True).then_inc(s_z, 1)

                        def edge_maxima(g, k, r):
                            pe.wait_ge(s_mh, g + 1)
                            pe.wait_ge(s_ml, g + 1)
                            at_least(pe, s_d0, g)
                            for t in range(T):
                                for i in range(2):
                                    mm = pe.matmul(ps_m[:, t * heads:(t + 1) * heads], ohN[:, k, t, :], mnp[:, i], start=(i == 0), stop=(i == 1))
                            mm.then_inc(s_me, 1)

                        def node_sums(g, k, r):
                            pe.wait_ge(s_oh32, g + 1)
                            pe.wait_ge(s_V, g + 1)
                            at_least(pe, s_done, g)
                            for t in range(T):
                                mm = pe.matmul(ps_a[:, 0:heads * VC], oh[:, k, t, :], V[:, t].rearrange("p h c -> p (h c)"),
                                               start=(t == 0), stop=(t == T - 1))
                            mm.then_inc(s_acc, 1)

                        def spread_first(g, k, r):
                            spread(g, k, r, range(n_lb))

                        def spread_others(g, k, r):
                            spread(g, k, r, range(n_lb, heads))

                        def body(*at):
                            stage(spread_first, 1, NG, *at)
                            stage(node_sums, 2, NG, *at)
                            stage(feature_rows, -1, NG, *at)
                            stage(turn_scores, 0, NG, *at)
                            stage(spread_others, 1, NG, *at)
                            stage(key_rows, -1, NG, *at)
                            if layer == 0:
                                stage(gathered_rows, -1, NG, *at)
                            stage(edge_maxima, 1, NG, *at)
                            stage(turn, -2, NG, *at)
                        for ready in (turn, feature_rows, key_rows) + (() if layer else (gathered_rows,)):
                            ready(0, 0, 0)
                        turn(1, 1, 0)
                        pipeline(pe, NG, body, 2)

                    @block.scalar
                    def _(act):
                        def features(g, k, r):
                            act.wait_ge(s_eaP, g + 1)
                            at_least(act, s_z, g)
                            act.copy(eaT[:], ps_ea[0:T * DE, 0:P]).then_inc(s_eaT, 1)

                        def copies(g, k, r):
                            q = k % 2
                            act.wait_ge(s_ohT, g + 1)
                            at_least(act, s_me, g - SLOTS + 1)
                            act.copy(ohN[:, k], ps_oh[:, 0:T]).then_inc(s_ohN, 1)
                            at_least(act, s_gm[heads - 1], g - SLOTS + 1)
                            act.activation(pen[:, k], ps_oh[:, 0:T], ACT.Copy, bias=-BIG, scale=BIG).then_inc(s_pen, 1)
                            at_least(act, s_acc, g - SLOTS + 1)
                            act.wait_ge(s_oh, g + 1)
                            act.copy(oh[:, k], ohb[:, q]).then_inc(s_oh32, 1)

                        def slope(g, k, r):
                            act.wait_ge(s_z, g + 1)
                            at_least(act, s_act, g)
                            act.activation(zs[:], zv[0], ACT.Copy, scale=0.2).then_inc(s_zs, 1)

                        def high_part(g, k, r):
                            q = k % 2
                            if layer:
                                act.wait_ge(s_lg0, g + 1)
                                at_least(act, s_d0, g - 1)
                                act.activation(lg[:, q], ss[:], ACT.Identity, bias=rows[:, ROWS["b_att2"]]).then_inc(s_lg, 1)
                            act.wait_ge(s_lg, g + 1)
                            at_least(act, s_lT, g)
                            act.copy(lgp[:, :, 0, :], lg[:, q]).then_inc(s_lp0, 1)

                        def rescale(g, k, r):
                            act.wait_ge(s_df, g + 1)
                            at_least(act, s_sc, g - 1)
                            act.activation(corr[:, k % 2], df[:], ACT.Exp).then_inc(s_corr, 1)

                        def weights(g, k, r):
                            act.wait_ge(s_d, g + 1)
                            at_least(act, s_acc, g)
                            act.activation(V[:, :, :, VC - 1], dd[:], ACT.Exp).then_inc(s_p, 1)

                        def score_rows(g, k, r):
                            act.wait_ge(s_lT, g + 1)
                            at_least(act, s_lb[heads - 1], g)
                            act.copy(lgT[:], ps_lT[0:2 * heads, 0:T * P]).then_inc(s_lTc, 1)

                        def body(*at):
                            stage(high_part, 0, NG, *at)
                            stage(score_rows, 0, NG, *at)
                            if layer == 0:
                                stage(slope, -1, NG, *at)
                            stage(weights, 1, NG, *at)
                            stage(rescale, 1, NG, *at)
                            stage(features, -2, NG, *at)
                            stage(copies, -2, NG, *at)
                        features(0, 0, 0)
                        copies(0, 0, 0)
                        if layer == 0:
                            slope(0, 0, 0)
                        features(1, 1, 0)
                        copies(1, 1, 0)
                        pipeline(act, NG, body, 2)

        def segment_max():
            with phase() as ctx:
                w = sb_in(ctx, "w2_sb", [D, D])
                key = sb_in(ctx, "m_key", [P, SLOTS, T], I32)
                nxt = sb_in(ctx, "m_next", [P, SLOTS, T], I32)
                idx = sb_in(ctx, "m_idx", [P, SLOTS, T, 1], I32)
                row = sb_in(ctx, "m_row", [D, SLOTS, 1 + GE], I32)
                lo = sb_in(ctx, "m_lo", [P, 3, T])
                oh = sb_in(ctx, "m_oh", [P, T, P], BF16)
                ohN = sb_in(ctx, "m_ohN", [P, 2, T, P], BF16)
                fl = sb_in(ctx, "m_fl", [D, GE])
                G, ohL, flps = in_place_of_h(ctx, ("m_G", D), ("m_ohL", P), ("m_flp", P))
                flp = flps[0:D].rearrange("p k t e -> p k (t e)")
                z = sb_in(ctx, "m_z", [P, T, D])
                zr = sb_in(ctx, "m_zr", [P, T, D])
                zT = sb_in(ctx, "m_zT", [D, GE])
                S = sb_in(ctx, "m_S", [D, 2, GE])
                Sx = sb_in(ctx, "m_Sx", [P, T, D + 1])
                ps_oh = ps_in(ctx, "m_ps_oh", [P, 2 * T, P], BF16)
                ps_z = ps_in(ctx, "m_ps_z", [P, T, P])
                ps_t = ps_in(ctx, "m_ps_t", [P, GE])
                ps_m = ps_in(ctx, "m_ps_m", [P, GE])
                ps_s = ps_in(ctx, "m_ps_s", [P, T, P])
                ps_a = ps_in(ctx, "m_ps_a", [P, 512])
                (s_w, s_one, s_lo, s_eq, s_lol, s_oh, s_ohL, s_fl, s_flp, s_ohT, s_ohN, s_kr, s_z, s_zr, s_tp, s_zT, s_msg, s_scan, s_st, s_Sx,
                 s_acc, s_done) = (sem_in(ctx, "m_" + n) for n in (
                    "weights", "ones_column", "local_key", "same_as_next", "last_key", "onehot", "onehot_last", "changes", "resets",
                    "onehot_turned", "onehot_nodes", "key_rows", "rows_added", "hidden", "hidden_turned", "hidden_copied", "messages",
                    "scanned", "scan_turned", "scan_copied", "group_values", "group_done"))
                s_ld = [sem_in(ctx, f"m_edges_landed{k}") for k in range(SLOTS)]
                s_g = [sem_in(ctx, f"m_gathered{k}") for k in range(SLOTS)]
                N_LOADS = 4
                with nc.Block() as block:
                    @block.sync
                    def _(sp):
                        sp.dma_start(w[:], w2).then_inc(s_w, 16)

                        def body(g, k, r):
                            at_least(sp, s_lol, g - SLOTS + 1)
                            at_least(sp, s_fl, g - SLOTS + 1)
                            settle(sp)
                            at_least(sp, s_g[k], r * (16 * T))
                            settle(sp)
                            e = sp.value_load(goff[0:1, bass.ds(g, 1)], min_val=0, max_val=E)
                            sp.dma_start(key[:, k, :], keyp[bass.ds(e + 1, GE)].rearrange("(p t) -> p t", p=P)).then_inc(s_ld[k], 16)
                            sp.dma_start(nxt[:, k, :], keyp[bass.ds(e + 2, GE)].rearrange("(p t) -> p t", p=P)).then_inc(s_ld[k], 16)
                            sp.dma_start(idx[:, k, :, 0], srcp[bass.ds(e, GE)].rearrange("(p t) -> p t", p=P)).then_inc(s_ld[k], 16)
                            sp.dma_start(row[:, k, :], keyp[bass.ds(e, GE + 1)].partition_broadcast(D)).then_inc(s_ld[k], 16)
                        steps(sp, NG, body)

                    @block.gpsimd
                    def _(pool):
                        def body(g, k, r):
                            at_least(pool, s_z, g - SLOTS + 1)
                            pool.wait_ge(s_ld[k], (r + 1) * (16 * N_LOADS))
                            settle(pool)
                            for t in range(T):
                                pool.indirect_dma_start(G[:, k, t, :], None, tab1,
                                                        bass.IndirectOffsetOnAxis(ap=idx[:, k, t, :], axis=0)).then_inc(s_g[k], 16)
                        steps(pool, NG, body)

                    @block.vector
                    def _(dve):
                        dve.memset(Sx[:], 1.0).then_inc(s_one, 1)

                        def onehots(g, k, r):
                            dve.wait_ge(s_ld[k], (r + 1) * (16 * N_LOADS))
                            at_least(dve, s_oh, g)
                            at_least(dve, s_ohL, g)
                            dve.tensor_scalar(lo[:, 0], key[:, k], base_node[:, 0, bass.ds(g, 1)], None, ALU.subtract).then_inc(s_lo, 1)
                            dve.tensor_tensor(lo[:, 1], key[:, k], nxt[:, k], ALU.is_equal).then_inc(s_eq, 1)
                            dve.wait_ge(s_lo, g + 1)
                            dve.wait_ge(s_eq, g + 1)
                            dve.scalar_tensor_tensor(lo[:, 2], lo[:, 1], float(FAR), lo[:, 0], ALU.mult, ALU.add).then_inc(s_lol, 1)
                            at_least(dve, s_ohT, g)
                            for t in range(T):
                                ins = dve.tensor_scalar(oh[:, t, :], iota_b[:], lo[:, 0, t:t + 1], None, ALU.is_equal)
                            ins.then_inc(s_oh, 1)

                        def last_edges(g, k, r):
                            dve.wait_ge(s_lol, g + 1)
                            at_least(dve, s_acc, g - SLOTS + 1)
                            dve.tensor_tensor(ohL[:, k], bcast(iota_n[:], 1, T), bcast(lo[:, 2], 2, P), ALU.is_equal).then_inc(s_ohL, 1)
                            at_least(dve, s_flp, g)
                            dve.tensor_tensor(fl[:], row[:, k, 1:1 + GE], row[:, k, 0:GE], ALU.not_equal).then_inc(s_fl, 1)

                        def scan(g, k, r):
                            q = k % 2
                            first = isinstance(g, int) and g == 0
                            dve.wait_ge(s_msg, g + 1)
                            dve.wait_ge(s_flp, g + 1)
                            at_least(dve, s_st, g - 1)
                            at_least(dve, s_scan, g)
                            dve.tensor_tensor_scan(S[:, q], flp[:, k], ps_m[0:D, :], 0.0 if first else S[:, 1 - q, GE - 1:GE],
                                                   ALU.add, ALU.max).then_inc(s_scan, 1)

                        def add(g, k, r):
                            dve.wait_ge(s_g[k], (r + 1) * (16 * T))
                            dve.wait_ge(s_kr, g + 1)
                            at_least(dve, s_zr, g)
                            dve.tensor_tensor(z[:], ps_z[:, :, 0:D], G[:, k], ALU.add).then_inc(s_z, 1)

                        def keep(g, k, r):
                            blk_g = dve.value_load(blk[0:1, 0, bass.ds(g, 1)], min_val=0, max_val=NB)
                            acc = ACC[:, bass.ds(blk_g, 1), 0:D + 1].rearrange("p a c -> p (a c)")
                            dve.wait_ge(s_acc, g + 1)
                            at_least(dve, s_done, g)
                            dve.tensor_tensor(acc, acc, ps_a[:, 0:D + 1], ALU.add).then_inc(s_done, 1)

                        def body(*at):
                            stage(last_edges, -1, NG, *at)
                            stage(add, 0, NG, *at)
                            stage(onehots, -2, NG, *at)
                            stage(scan, 1, NG, *at)
                            stage(keep, 2, NG, *at)
                        onehots(0, 0, 0)
                        last_edges(0, 0, 0)
                        onehots(1, 1, 0)
                        pipeline(dve, NG, body, 2)

                    @block.tensor
                    def _(pe):
                        pe.wait_ge(s_w, 16)

                        def turn(g, k, r):
                            pe.wait_ge(s_oh, g + 1)
                            at_least(pe, s_ohN, g)
                            for t in range(T):
                                mm = pe.transpose(ps_oh[:, t, :], oh[:, t, :], identb[:])
                            mm.then_inc(s_ohT, 1)

                        def turn_hidden(g, k, r):
                            pe.wait_ge(s_zr, g + 1)
                            at_least(pe, s_zT, g)
                            settle(pe)
                            for t in range(T):
                                mm = pe.transpose(ps_t[0:D, :].rearrange("d (p t) -> d t p", t=T)[:, t, :], zr[:, t, :], ident[:])
                            mm.then_inc(s_tp, 1)

                        def messages(g, k, r):
                            pe.wait_ge(s_zT, g + 1)
                            at_least(pe, s_scan, g)
                            settle(pe)
                            pe.matmul(ps_m[0:D, :], w[:], zT[:], start=True, stop=True).then_inc(s_msg, 1)

                        def key_rows(g, k, r):
                            blk_g = pe.value_load(blk[0:1, 0, bass.ds(g, 1)], min_val=0, max_val=NB)
                            pe.wait_ge(s_ohN, g + 1)
                            at_least(pe, s_z, g)
                            for t in range(T):
                                for i in range(3):
                                    mm = pe.matmul(ps_z[:, t, 0:D], ohN[:, k % 2, t, :], PT[:, bass.ds(blk_g, 1), i, 0:D].rearrange("p a c -> p (a c)"),
                                                   start=(i == 0), stop=(i == 2))
                            mm.then_inc(s_kr, 1)

                        def turn_scanned(g, k, r):
                            q = k % 2
                            pe.wait_ge(s_scan, g + 1)
                            at_least(pe, s_Sx, g)
                            settle(pe)
                            for t in range(T):
                                mm = pe.transpose(ps_s[:, t, 0:D], S[:, q, :].rearrange("d (p t) -> d t p", t=T)[:, t, :], ident[0:D, 0:D])
                            mm.then_inc(s_st, 1)

                        def values(g, k, r):
                            pe.wait_ge(s_Sx, g + 1)
                            pe.wait_ge(s_ohL, g + 1)
                            at_least(pe, s_done, g)
                            for t in range(T):
                                mm = pe.matmul(ps_a[:, 0:D + 1], ohL[:, k, t, :], Sx[:, t, :], start=(t == 0), stop=(t == T - 1))
                            mm.then_inc(s_acc, 1)

                        def body(*at):
                            stage(turn_hidden, 1, NG, *at)
                            stage(turn, -1, NG, *at)
                            stage(turn_scanned, 2, NG, *at)
                            stage(key_rows, 0, NG, *at)
                            stage(messages, 1, NG, *at)
                            stage(values, 2, NG, *at)
                        turn(0, 0, 0)
                        pipeline(pe, NG, body, 2)

                    @block.scalar
                    def _(act):
                        act.wait_ge(s_one, 1)

                        def copies(g, k, r):
                            act.wait_ge(s_ohT, g + 1)
                            at_least(act, s_kr, g - 1)
                            act.copy(ohN[:, k % 2], ps_oh[:, 0:T]).then_inc(s_ohN, 1)
                            act.wait_ge(s_fl, g + 1)
                            at_least(act, s_scan, g - SLOTS + 1)
                            act.activation(flp[:, k], fl[:], ACT.Copy, scale=-3.0e38).then_inc(s_flp, 1)

                        def hidden_turned(g, k, r):
                            act.wait_ge(s_tp, g + 1)
                            at_least(act, s_msg, g)
                            act.copy(zT[:], ps_t[0:D, :]).then_inc(s_zT, 1)

                        def scanned(g, k, r):
                            act.wait_ge(s_st, g + 1)
                            at_least(act, s_acc, g)
                            act.copy(Sx[:, :, 0:D], ps_s[:, :, 0:D]).then_inc(s_Sx, 1)

                        def relu(g, k, r):
                            act.wait_ge(s_z, g + 1)
                            at_least(act, s_tp, g)
                            act.activation(zr[:], z[:], ACT.Relu).then_inc(s_zr, 1)

                        def body(*at):
                            stage(hidden_turned, 1, NG, *at)
                            stage(scanned, 2, NG, *at)
                            stage(copies, -1, NG, *at)
                            stage(relu, 0, NG, *at)
                        copies(0, 0, 0)
                        pipeline(act, NG, body, 2)

        def segment_sum():
            with phase() as ctx:
                rs = sb_in(ctx, "g_rs", [P, SLOTS, T, REC], I32)
                ea = rs[:].bitcast(F32)[:, :, :, EA64:EA64 + D]
                G = sb_in(ctx, "g_G", [P, SLOTS, T, D])
                lo = sb_in(ctx, "g_lo", [P, T])
                oh = sb_in(ctx, "g_oh", [P, 2, T, P])
                z = sb_in(ctx, "g_z", [P, 2, T, D])
                zr = sb_in(ctx, "g_zr", [P, 2, T, D])
                ps_a = ps_in(ctx, "g_ps_a", [P, 2, 512])
                s_lo, s_oh, s_z, s_zr, s_acc, s_done = (sem_in(ctx, "g_" + n) for n in (
                    "local_key", "onehot", "rows_added", "messages", "group_sums", "group_done"))
                s_ld = [sem_in(ctx, f"g_edges_landed{k}") for k in range(SLOTS)]
                s_g = [sem_in(ctx, f"g_gathered{k}") for k in range(SLOTS)]
                with nc.Block() as block:
                    @block.sync
                    def _(sp):
                        def body(g, k, r):
                            at_least(sp, s_z, g - SLOTS + 1)
                            settle(sp)
                            at_least(sp, s_g[k], r * (16 * T))
                            settle(sp)
                            sp.dma_start(rs[:, k], rec[bass.ds(g * GE, GE), :].rearrange("(p t) c -> p t c", p=P)).then_inc(s_ld[k], 16)
                        steps(sp, NG, body)

                    @block.gpsimd
                    def _(pool):
                        def body(g, k, r):
                            at_least(pool, s_z, g - SLOTS + 1)
                            pool.wait_ge(s_ld[k], (r + 1) * 16)
                            settle(pool)
                            for t in range(T):
                                pool.indirect_dma_start(G[:, k, t, :], None, tab3,
                                                        bass.IndirectOffsetOnAxis(ap=rs[:, k, t, 1:2], axis=0)).then_inc(s_g[k], 16)
                        steps(pool, NG, body)

                    @block.vector
                    def _(dve):
                        def group(g, k, r):
                            q = k % 2
                            dve.wait_ge(s_ld[k], (r + 1) * 16)
                            at_least(dve, s_oh, g)
                            dve.tensor_scalar(lo[:], rs[:, k, :, 0], base_node[:, 1, bass.ds(g, 1)], None, ALU.subtract).then_inc(s_lo, 1)
                            dve.wait_ge(s_lo, g + 1)
                            at_least(dve, s_acc, g - 1)
                            dve.tensor_tensor(oh[:, q], bcast(iota_n[:], 1, T), bcast(lo[:], 2, P), ALU.is_equal).then_inc(s_oh, 1)
                            dve.wait_ge(s_g[k], (r + 1) * (16 * T))
                            at_least(dve, s_zr, g - 1)
                            dve.tensor_tensor(z[:, q], G[:, k], ea[:, k], ALU.add).then_inc(s_z, 1)

                        def keep(g, k, r):
                            blk_g = dve.value_load(blk[0:1, 1, bass.ds(g, 1)], min_val=0, max_val=NB)
                            acc = ACC[:, bass.ds(blk_g, 1), 0:D].rearrange("p a c -> p (a c)")
                            dve.wait_ge(s_acc, g + 1)
                            at_least(dve, s_done, g)
                            dve.tensor_tensor(acc, acc, ps_a[:, k % 2, 0:D], ALU.add).then_inc(s_done, 1)

                        def body(g, k, r):
                            group(g, k, r)
                            if not (isinstance(g, int) and g == 0):
                                keep(g - 1, (k - 1) % SLOTS, r if k else r - 1)
                        steps(dve, NG, body)
                        keep(NG - 1, SLOTS - 1, NG // SLOTS - 1)

                    @block.scalar
                    def _(act):
                        def body(g, k, r):
                            act.wait_ge(s_z, g + 1)
                            at_least(act, s_acc, g - 1)
                            act.activation(zr[:, k % 2], z[:, k % 2], ACT.Relu).then_inc(s_zr, 1)
                        steps(act, NG, body)

                    @block.tensor
                    def _(pe):
                        def body(g, k, r):
                            q = k % 2
                            pe.wait_ge(s_oh, g + 1)
                            pe.wait_ge(s_zr, g + 1)
                            at_least(pe, s_done, g - 1)
                            for t in range(T):
                                mm = pe.matmul(ps_a[:, q, 0:D], oh[:, q, t, :], zr[:, q, t, :], start=(t == 0), stop=(t == T - 1))
                            mm.then_inc(s_acc, 1)
                        steps(pe, NG, body)

        def finish_gat():
            with phase() as ctx:
                rd = sb_in(ctx, "b_rd", [P, NB, HEADS])
                small = sb_in(ctx, "b_small", [P, 4, D])
                valid = sb_in(ctx, "b_valid", [P, 2])
                junk = sb_in(ctx, "b_junk", [P, P])
                epsc = sb_in(ctx, "b_eps", [P, 1])
                ps = ps_in(ctx, "b_ps", [P, 2, 512])
                s_v, s_sum, s_tot, s_std0, s_std, s_pre, s_gelu = (sem_in(ctx, "b_" + n) for n in (
                    "steps", "sums_ready", "totals", "var_ready", "std_ready", "pre_gelu", "gelu"))
                O, Q = room[:, 0:NB, 0:D], room[:, 0:NB, D:2 * D]
                OL = room[:, NBLK - 1, 0:D]
                acc = ACC[:, 0:NB, :].rearrange("p b (h c) -> p b h c", h=HEADS)
                C = D // HEADS
                with nc.Block() as block:
                    @block.vector
                    def _(dve):
                        do = chain(dve, s_v)
                        do(dve.memset(epsc[:], 1e-5))
                        do(dve.tensor_tensor_reduce(junk[:], ident[:], iota_n[:], 1.0, 0.0, ALU.mult, ALU.add, valid[:, 0:1]))
                        do(dve.tensor_scalar(valid[:, 1:2], valid[:, 0:1], float(last_rows), None, ALU.is_lt))
                        do(dve.tensor_scalar(rd[:], acc[:, :, :, C], 1e-16, None, ALU.add))
                        do(dve.reciprocal(rd[:], rd[:]))
                        for h in range(HEADS):
                            do(dve.tensor_tensor(room[:, 0:NB, h * C:(h + 1) * C], acc[:, :, h, 0:C], bcast(rd[:, :, h], 2, C), ALU.mult))
                        do(dve.tensor_tensor(O, O, bcast(rows[:, ROWS["bias"]], 1, NB), ALU.add))
                        for b in range(NBLK, NB):
                            do(dve.memset(room[:, b, 0:D], 0.0))
                        do(dve.tensor_scalar(OL, OL, valid[:, 1:2], None, ALU.mult))
                        dve.tensor_reduce(small[:, 0], O.rearrange("p b d -> p d b"), AX.X, ALU.add).then_inc(s_sum, 1)
                        dve.wait_ge(s_tot, 1)
                        do(dve.tensor_scalar(small[:, 1], ps[:, 0, 0:D], 1.0 / N, None, ALU.mult))
                        do(dve.tensor_tensor(O, O, bcast(small[:, 1], 1, NB), ALU.subtract))
                        for b in range(NBLK, NB):
                            do(dve.memset(room[:, b, 0:D], 0.0))
                        do(dve.tensor_scalar(OL, OL, valid[:, 1:2], None, ALU.mult))
                        do(dve.tensor_tensor(Q, O, O, ALU.mult))
                        dve.tensor_reduce(small[:, 2], Q.rearrange("p b d -> p d b"), AX.X, ALU.add).then_inc(s_sum, 1)
                        dve.wait_ge(s_tot, 2)
                        dve.tensor_scalar(small[:, 3], ps[:, 1, 0:D], 1.0 / N, None, ALU.mult).then_inc(s_std0, 1)
                        dve.wait_ge(s_std, 1)
                        do(dve.reciprocal(small[:, 1], small[:, 0]))
                        do(dve.tensor_tensor(small[:, 1], small[:, 1], rows[:, ROWS["gamma"]], ALU.mult))
                        do(dve.tensor_tensor(O, O, bcast(small[:, 1], 1, NB), ALU.mult))
                        do(dve.tensor_tensor(O, O, bcast(rows[:, ROWS["beta"]], 1, NB), ALU.add))
                        dve.tensor_tensor(O, O, H[:], ALU.add).then_inc(s_pre, 1)
                        dve.wait_ge(s_gelu, 1)
                        do(dve.tensor_tensor(X[:], X[:], Q, ALU.add))

                    @block.tensor
                    def _(pe):
                        for i in range(2):
                            pe.wait_ge(s_sum, i + 1)
                            pe.matmul(ps[:, i, 0:D], ones[:], small[:, 2 * i], start=True, stop=True).then_inc(s_tot, 1)

                    @block.scalar
                    def _(act):
                        act.wait_ge(s_std0, 1)
                        act.activation(small[:, 0], small[:, 3], ACT.Sqrt, bias=epsc[:]).then_inc(s_std, 1)
                        act.wait_ge(s_pre, 1)
                        act.activation(Q, O, ACT.Gelu).then_inc(s_gelu, 1)

        def finish_max():
            with phase() as ctx:
                s_v = sem_in(ctx, "x_steps")
                with nc.Block() as block:
                    @block.vector
                    def _(dve):
                        do = chain(dve, s_v)
                        t = room[:, 0:NB, 0:D]
                        do(dve.tensor_tensor(t, bcast(rows[:, ROWS["b2_l1"]], 1, NB), ACC[:, 0:NB, D:D + 1].broadcast_to([P, NB, D]), ALU.mult))
                        do(dve.tensor_tensor(t, t, ACC[:, 0:NB, 0:D], ALU.add))
                        do(dve.tensor_tensor(X[:], X[:], t, ALU.add))

        def finish_gru():
            with phase() as ctx:
                w = sb_in(ctx, "r_w", [P, 4 * D])
                bias = sb_in(ctx, "r_bias", [2, 4 * D])
                rd = sb_in(ctx, "r_rd", [P, 2, NB])
                hm = sb_in(ctx, "r_hm", [P, 2, 2 * D])
                hmT = sb_in(ctx, "r_hmT", [P, 2, P])
                rz = sb_in(ctx, "r_rz", [P, 2, 2 * D])
                t1 = sb_in(ctx, "r_t1", [P, 2, D])
                n = sb_in(ctx, "r_n", [P, 2, D])
                d = sb_in(ctx, "r_d", [P, D])
                ps_t = ps_in(ctx, "r_ps_t", [P, 2, 512])
                ps_w = ps_in(ctx, "r_ps_w", [P, 2, 512])
                (s_w, s_v, s_cp, s_t, s_hmT, s_mm, s_rz, s_t1, s_pre, s_n, s_d1, s_d2, s_d3, s_d4, s_d5, s_x) = (sem_in(ctx, "r_" + q) for q in (
                    "weights", "steps", "inputs_copied", "turned", "turned_copied", "gates_in", "gates", "reset_applied", "candidate_in",
                    "candidate", "msg_less_n", "scaled", "new_h", "less_h", "selected", "block_done"))
                msg = ACC[:, 0:NB, 0:D]
                with nc.Block() as block:
                    @block.sync
                    def _(sp):
                        sp.dma_start(w[:], wgru).then_inc(s_w, 16)
                        sp.dma_start(bias[:], bgru).then_inc(s_w, 16)
                        sp.wait_ge(s_w, 32)

                    @block.vector
                    def _(dve):
                        do = chain(dve, s_v)
                        den = ACC[:, 0:NB, D]
                        do(dve.tensor_scalar(rd[:, 1], den, 0.0, None, ALU.is_gt))
                        do(dve.tensor_scalar(rd[:, 0], rd[:, 1], -1.0, 1.0, ALU.mult, ALU.add))
                        do(dve.tensor_tensor(rd[:, 0], rd[:, 0], den, ALU.add))
                        do(dve.reciprocal(rd[:, 0], rd[:, 0]))
                        do(dve.tensor_tensor(msg, msg, bcast(rd[:, 0], 2, D), ALU.mult))

                        def at(big, b):
                            return big[:, bass.ds(b, 1), :].rearrange("p a d -> p (a d)")

                        def copy(b, k, r):
                            m_b = ACC[:, bass.ds(b, 1), 0:D].rearrange("p a d -> p (a d)")
                            at_least(dve, s_t, b - 1)
                            at_least(dve, s_x, b - 1)
                            dve.tensor_copy(hm[:, k, 0:D], at(H, b)).then_inc(s_cp, 1)
                            dve.tensor_copy(hm[:, k, D:2 * D], m_b).then_inc(s_cp, 1)

                        def before_tanh(b, k, r):
                            dve.wait_ge(s_rz, b + 1)
                            at_least(dve, s_n, b - 1)
                            dve.tensor_tensor(t1[:, k], rz[:, k, 0:D], ps_w[:, k, 3 * D:4 * D], ALU.mult).then_inc(s_t1, 1)
                            dve.wait_ge(s_t1, b + 1)
                            dve.tensor_tensor(t1[:, k], t1[:, k], ps_w[:, k, 2 * D:3 * D], ALU.add).then_inc(s_pre, 1)

                        def blend(b, k, r):
                            dve.wait_ge(s_n, b + 1)
                            at_least(dve, s_x, b)
                            dve.tensor_tensor(d[:], hm[:, k, D:2 * D], n[:, k], ALU.subtract).then_inc(s_d1, 1)
                            dve.wait_ge(s_d1, b + 1)
                            dve.tensor_tensor(d[:], d[:], rz[:, k, D:2 * D], ALU.mult).then_inc(s_d2, 1)
                            dve.wait_ge(s_d2, b + 1)
                            dve.tensor_tensor(d[:], d[:], n[:, k], ALU.add).then_inc(s_d3, 1)
                            dve.wait_ge(s_d3, b + 1)
                            dve.tensor_tensor(d[:], d[:], hm[:, k, 0:D], ALU.subtract).then_inc(s_d4, 1)
                            dve.wait_ge(s_d4, b + 1)
                            dve.scalar_tensor_tensor(d[:], d[:], rd[:, 1, bass.ds(b, 1)], hm[:, k, 0:D], ALU.mult, ALU.add).then_inc(s_d5, 1)
                            dve.wait_ge(s_d5, b + 1)
                            dve.tensor_tensor(at(X, b), at(X, b), d[:], ALU.add).then_inc(s_x, 1)
                        one_ahead(dve, NB, (blend, 1), (copy, -1), (before_tanh, 0))

                    @block.tensor
                    def _(pe):
                        pe.wait_ge(s_w, 32)

                        def body(b, k, r):
                            pe.wait_ge(s_cp, b * 2 + 2)
                            at_least(pe, s_hmT, b - 1)
                            pe.transpose(ps_t[:, k, 0:P], hm[:, k, :], ident[:]).then_inc(s_t, 1)
                            pe.wait_ge(s_hmT, b + 1)
                            at_least(pe, s_pre, b - 1)
                            pe.matmul(ps_w[:, k, 0:4 * D], hmT[:, k], w[:], start=True, stop=False)
                            pe.matmul(ps_w[:, k, 0:4 * D], ones[0:2, :], bias[:], start=False, stop=True).then_inc(s_mm, 1)
                        steps(pe, NB, body, 2)

                    @block.scalar
                    def _(act):
                        def turned(b, k, r):
                            act.wait_ge(s_t, b + 1)
                            at_least(act, s_mm, b - 1)
                            act.copy(hmT[:, k], ps_t[:, k, 0:P]).then_inc(s_hmT, 1)

                        def gates(b, k, r):
                            act.wait_ge(s_mm, b + 1)
                            at_least(act, s_x, b - 1)
                            act.activation(rz[:, k], ps_w[:, k, 0:2 * D], ACT.Sigmoid).then_inc(s_rz, 1)

                        def candidate(b, k, r):
                            act.wait_ge(s_pre, b + 1)
                            at_least(act, s_x, b - 1)
                            act.activation(n[:, k], t1[:, k], ACT.Tanh).then_inc(s_n, 1)
                        one_ahead(act, NB, (turned, -1), (candidate, 0), (gates, -1))

        def finish_gine():
            DD = 2 * D
            with phase() as ctx:
                wa = sb_in(ctx, "f_w1", [D + 1, DD])
                wb = sb_in(ctx, "f_w3", [DD, D])
                e1 = sb_in(ctx, "f_e1", [P, 1])
                epsc = sb_in(ctx, "f_eps", [P, 1])
                hb = sb_in(ctx, "f_hb", [P, 2, DD])
                hT = sb_in(ctx, "f_hT", [D + 1, 2, P])
                yT = sb_in(ctx, "f_yT", [DD, 2, P])
                st = sb_in(ctx, "f_st", [P, 2, NB])
                ps_t = ps_in(ctx, "f_ps_t", [P, 2, 512])
                ps_w = ps_in(ctx, "f_ps_w", [P, 2, 512])
                Y = room[:, 0:NB, 0:DD]
                (s_w, s_v, s_hb, s_t, s_hT, s_mm, s_y, s_var, s_std, s_yb, s_yt, s_yT, s_m2, s_x, s_out) = (sem_in(ctx, "f_" + q) for q in (
                    "weights", "steps", "block_copied", "block_turned", "turned_copied", "hidden", "hidden_kept", "var_ready", "std_ready",
                    "hidden_copied", "hidden_turned", "hidden_turned_copied", "outputs", "block_done", "stored"))
                with nc.Block() as block:
                    @block.sync
                    def _(sp):
                        sp.dma_start(wa[:], w1).then_inc(s_w, 16)
                        sp.dma_start(wb[:], w3).then_inc(s_w, 16)
                        sp.wait_ge(s_x, NB + 1)
                        sp.dma_start(out[0:P * (NBLK - 1), :].rearrange("(b p) d -> p b d", p=P), X[:, 0:NBLK - 1, :]).then_inc(s_out, 16)
                        sp.dma_start(out[P * (NBLK - 1):N, :], X[0:last_rows, NBLK - 1, :]).then_inc(s_out, 16)
                        sp.wait_ge(s_out, 32)

                    @block.vector
                    def _(dve):
                        do = chain(dve, s_v)
                        do(dve.memset(epsc[:], 1e-5))
                        do(dve.memset(hT[D:D + 1, :, :], 1.0))
                        do(dve.tensor_scalar(e1[:], rows[:, ROWS["eps"]], 1.0, None, ALU.add))
                        do(dve.scalar_tensor_tensor(H[:], H[:], e1[:], ACC[:, 0:NB, 0:D], ALU.mult, ALU.add))

                        def hidden(b, k, r):
                            at_least(dve, s_t, b - 1)
                            dve.tensor_copy(hb[:, k, 0:D], H[:, bass.ds(b, 1), :].rearrange("p a d -> p (a d)")).then_inc(s_hb, 1)

                        def keep(b, k, r):
                            dve.wait_ge(s_mm, b + 1)
                            settle(dve)
                            dve.tensor_copy(room[:, bass.ds(b, 1), 0:DD].rearrange("p a d -> p (a d)"), ps_w[:, k, 0:DD]).then_inc(s_y, 1)
                        one_ahead(dve, NB, (hidden, -1), (keep, 0))
                        dve.wait_ge(s_y, NB)
                        sq = room[:, 0:NB, 0:DD]
                        do(dve.tensor_reduce(st[:, 0], Y, AX.X, ALU.add))
                        do(dve.tensor_scalar(st[:, 0], st[:, 0], 1.0 / DD, None, ALU.mult))
                        do(dve.tensor_tensor(Y, Y, bcast(st[:, 0], 2, DD), ALU.subtract))
                        do(dve.tensor_tensor(H[:], room[:, 0:NB, 0:D], room[:, 0:NB, 0:D], ALU.mult))
                        do(dve.tensor_tensor(ACC[:, 0:NB, 0:D], room[:, 0:NB, D:DD], room[:, 0:NB, D:DD], ALU.mult))
                        do(dve.tensor_tensor(H[:], H[:], ACC[:, 0:NB, 0:D], ALU.add))
                        dve.tensor_reduce(st[:, 0], H[:], AX.X, ALU.add).then_inc(s_var, 1)
                        dve.wait_ge(s_std, 1)
                        do(dve.reciprocal(st[:, 1], st[:, 1]))
                        do(dve.tensor_tensor(Y, Y, bcast(st[:, 1], 2, DD), ALU.mult))
                        do(dve.tensor_tensor(Y, Y, bcast(rows[:, ROWS["ln_g"]], 1, NB), ALU.mult))
                        do(dve.tensor_tensor(Y, Y, bcast(rows[:, ROWS["ln_b"]], 1, NB), ALU.add))
                        do(dve.tensor_scalar(Y, Y, 0.0, None, ALU.max))

                        def outputs(b, k, r):
                            at_least(dve, s_yt, b - 1)
                            dve.tensor_copy(hb[:, k, :], room[:, bass.ds(b, 1), 0:DD].rearrange("p a d -> p (a d)")).then_inc(s_yb, 1)

                        def add(b, k, r):
                            dve.wait_ge(s_m2, b + 1)
                            xb = X[:, bass.ds(b, 1), :].rearrange("p a d -> p (a d)")
                            dve.tensor_tensor(xb, xb, ps_w[:, k, 0:D], ALU.add).then_inc(s_x, 1)
                        one_ahead(dve, NB, (outputs, -1), (add, 0))
                        dve.wait_ge(s_x, NB)
                        dve.tensor_tensor(X[:], X[:], bcast(rows[:, ROWS["b2_l3"]], 1, NB), ALU.add).then_inc(s_x, 1)

                    @block.tensor
                    def _(pe):
                        pe.wait_ge(s_w, 32)

                        def hidden(b, k, r):
                            pe.wait_ge(s_hb, b + 1)
                            at_least(pe, s_hT, b - 1)
                            settle(pe)
                            pe.transpose(ps_t[0:D, k, 0:P], hb[:, k, 0:D], ident[:]).then_inc(s_t, 1)
                            pe.wait_ge(s_hT, b + 1)
                            at_least(pe, s_y, b - 1)
                            pe.matmul(ps_w[:, k, 0:DD], hT[:, k], wa[:], start=True, stop=True).then_inc(s_mm, 1)
                        steps(pe, NB, hidden, 2)
                        pe.wait_ge(s_y, NB)

                        def outputs(b, k, r):
                            pe.wait_ge(s_yb, b + 1)
                            at_least(pe, s_yT, b - 1)
                            pe.transpose(ps_t[:, k, 0:P], hb[:, k, :], ident[:]).then_inc(s_yt, 1)
                            pe.wait_ge(s_yT, b + 1)
                            at_least(pe, s_x, b - 1)
                            pe.matmul(ps_w[:, k, 0:D], yT[:, k], wb[:], start=True, stop=True).then_inc(s_m2, 1)
                        steps(pe, NB, outputs, 2)

                    @block.scalar
                    def _(act):
                        act.wait_ge(s_v, 2)

                        def hidden(b, k, r):
                            act.wait_ge(s_t, b + 1)
                            at_least(act, s_mm, b - 1)
                            act.copy(hT[0:D, k], ps_t[0:D, k, 0:P]).then_inc(s_hT, 1)
                        steps(act, NB, hidden, 2)
                        act.wait_ge(s_var, 1)
                        act.activation(st[:, 1], st[:, 0], ACT.Sqrt, bias=epsc[:], scale=1.0 / DD).then_inc(s_std, 1)

                        def outputs(b, k, r):
                            act.wait_ge(s_yt, b + 1)
                            at_least(act, s_m2, b - 1)
                            act.copy(yT[:, k], ps_t[:, k, 0:P]).then_inc(s_yT, 1)
                        steps(act, NB, outputs, 2)

        def load_rows(table, what):
            with phase() as ctx:
                s_i = sem_in(ctx, f"{what}_loaded")
                with nc.Block() as block:
                    @block.sync
                    def _(sp):
                        sp.dma_start(H[:], table.rearrange("(b p) d -> p b d", p=P)).then_inc(s_i, 16)
                        sp.wait_ge(s_i, 16)

        def store_rows(table, what):
            with phase() as ctx:
                s_o = sem_in(ctx, f"{what}_stored")
                with nc.Block() as block:
                    @block.sync
                    def _(sp):
                        sp.dma_start(table.rearrange("(b p) d -> p b d", p=P), H[:]).then_inc(s_o, 16)
                        sp.wait_ge(s_o, 16)

        layer_input(0)
        node_tables(0, wtab0, 2 * D, D, tab0)
        store_rows(tab3, "h0")
        attention(0, 0, tab0, HEADS, D, w_e, D)
        load_rows(tab3, "h0")
        finish_gat()
        layer_input(1)
        node_tables(1, wtab1, 2 * D, D, tab1, fold=True)
        segment_max()
        finish_max()
        layer_input(2)
        node_tables(2, wtab2, 2 * ATT + D, ATT + D, tab2)
        store_rows(tab3, "h2")
        attention(2, 1, tab2, 1, ATT, watt_e, D)
        load_rows(tab3, "h2")
        finish_gru()
        layer_input(3)
        store_rows(tab3, "h3")
        segment_sum()
        finish_gine()


def laid_out(i):
    def f(name):
        return np.asarray(i[name])

    def zeros(*shape):
        return np.zeros(shape, np.float32)

    w1, att, hh = f("L1_gnn_W1"), f("L2_gnn_W_att1").T, f("L2_gnn_W_hh").T
    b_hh = f("L2_gnn_b_hh")
    return {
        "x": f("x"), "src": f("src"), "dst": f("dst"), "ea16": f("edge_attr_16"), "ea64": f("edge_attr_64"),
        "rowvec": np.concatenate([
            f("L0_gnn_att").reshape(-1), f("L0_gnn_bias"), f("L0_gnn_gamma"), f("L0_gnn_beta"), f("L1_gnn_b2"),
            f("L2_gnn_W_att2").reshape(-1), f("L2_gnn_b_att2"), f("L3_gnn_ln_g"), f("L3_gnn_ln_b"), f("L3_gnn_b2"),
            f("L3_gnn_eps")]),
        "wtab0": np.block([[f("L0_gnn_W_l"), f("L0_gnn_W_r")], [f("L0_gnn_b_l")[None], f("L0_gnn_b_r")[None]]]),
        "w_e": f("L0_gnn_W_e"),
        "wtab1": np.block([[w1[D:], w1[:D]], [zeros(1, D), f("L1_gnn_b1")[None]]]),
        "w2": f("L1_gnn_W2"),
        "wtab2": np.block([[att[D + DE:], f("L2_gnn_W_lin").T, att[:D]],
                           [zeros(1, ATT), f("L2_gnn_b_lin")[None], f("L2_gnn_b_att1")[None]]]),
        "watt_e": att[D:D + DE],
        "wgru": np.block([[f("L2_gnn_W_ih").T, zeros(D, D)], [hh[:, :2 * D], zeros(D, D), hh[:, 2 * D:]]]),
        "bgru": np.stack([np.concatenate([f("L2_gnn_b_ih"), zeros(D)]),
                          np.concatenate([b_hh[:2 * D], zeros(D), b_hh[2 * D:]])]),
        "w1": np.concatenate([f("L3_gnn_W1"), f("L3_gnn_b1")[None]]),
        "w3": f("L3_gnn_W2"),
    }


def kernel(**inputs):
    import concourse.bacc as bacc
    from concourse.bass_utils import run_bass_kernel_spmd as run

    nc = bacc.Bacc("TRN2", target_bir_lowering=False, num_devices=1)
    arrays, args = {}, {}
    for name, a in laid_out(inputs).items():
        a = np.ascontiguousarray(a)
        arrays[f"in_{name}"] = a
        args[name] = nc.dram_tensor(f"in_{name}", a.shape, mybir.dt.from_np(a.dtype), kind="ExternalInput").ap()
    shape = inputs["x"].shape
    out = nc.dram_tensor("out_x", shape, F32, kind="ExternalOutput").ap()
    program(nc, **args, out=out)
    r = run(nc, [arrays], core_ids=[0])
    return r.results[0]["out_x"]
```
